# Optimizing a Trainium2 kernel written in Bass

```python
import numpy as np
import jax
import jax.numpy as jnp

def _softmax(x, axis=-1):
    return jax.nn.softmax(x, axis=axis)

def _gelu(x):
    return jax.nn.gelu(x, approximate=True)

def _silu(x):
    return jax.nn.silu(x)

def _sigmoid(x):
    return jax.nn.sigmoid(x)

def _layernorm(x, axis=-1, eps=1e-05):
    m = jnp.mean(x, axis=axis, keepdims=True)
    v = jnp.var(x, axis=axis, keepdims=True)
    return (x - m) / jnp.sqrt(v + eps)

def _scatter_add(tgt, idx, src, axis=0):
    return tgt.at[idx].add(src)

def _segment_sum(src, seg, n):
    return jax.ops.segment_sum(src, seg, n)
kernel_name = 'mk_perceiver_d2_seqx_r2_c9a521'

def setup_inputs(seed: int=0):
    np.random.seed(seed)
    _w = jnp.asarray

    def _rec_inputs():
        import jax
        import jax.numpy as jnp
        _rk = jax.random.key(seed)
        x = -0.0002928 + 1 * jax.random.normal(jax.random.fold_in(_rk, 1), (8, 64, 512), jnp.float32)
        _lenS = 64 - jax.random.randint(jax.random.fold_in(_rk, 7), (8,), 0, max(1, 64 // 4) + 1, jnp.int32)
        _lenS2 = 512 - jax.random.randint(jax.random.fold_in(_rk, 8), (8,), 0, max(1, 512 // 4) + 1, jnp.int32)
        _ctx_1024P = jax.random.normal(jax.random.fold_in(_rk, 11), (8, 16, 512), jnp.float32)
        _ctx_1024c = jax.random.dirichlet(jax.random.fold_in(_rk, 511), 0.3 * jnp.ones((16,), jnp.float32), (8, 512))
        _ctx_1024t = jnp.einsum('bsk,bkd->bsd', _ctx_1024c, _ctx_1024P)
        _ctx_1024t = _ctx_1024t * jax.lax.rsqrt(jnp.mean(jnp.square(_ctx_1024t)) + 1e-12) * 0.953939
        ctx_1024 = 4.13588e-05 + 0.999923 * (_ctx_1024t + 0.3 * jax.random.normal(jax.random.fold_in(_rk, 611), (8, 512, 512), jnp.float32))
        _validS = jnp.arange(64)[None, :] < _lenS[:, None]
        _validS2 = jnp.arange(512)[None, :] < _lenS2[:, None]
        _causal = jnp.tril(jnp.ones((64, 64), dtype=bool))
        mask_BxS2_ik0 = jnp.where(jnp.broadcast_to(_validS2[:, :], (8, 512)), 0, 1).astype(jnp.int32)
        return (x, ctx_1024, mask_BxS2_ik0)
    x, ctx_1024, mask_BxS2_ik0 = _rec_inputs()

    def _L0_xattn_setup():
        import jax, jax.numpy as jnp
        import numpy as np
        DIM = 512
        NUM_HEADS = 16
        DIM_HEAD = 64
        INNER = NUM_HEADS * DIM_HEAD
        SCALE = DIM_HEAD ** (-0.5)

        def _layernorm(x, gamma, beta, eps=1e-05):
            mu = jnp.mean(x, axis=-1, keepdims=True)
            var = jnp.mean(jnp.square(x - mu), axis=-1, keepdims=True)
            return (x - mu) * jax.lax.rsqrt(var + eps) * gamma + beta
        key = jax.random.key(seed)
        ks = jax.random.split(key, 8)
        B, SQ, SK = (2, 1024, 2048)
        x = jax.random.normal(ks[0], (B, SQ, DIM), dtype=jnp.float32)
        context = jax.random.normal(ks[1], (B, SK, DIM), dtype=jnp.float32)
        ln_gamma = jnp.ones((DIM,), jnp.float32)
        ln_beta = jnp.zeros((DIM,), jnp.float32)
        w_q = jax.random.normal(ks[2], (DIM, INNER), dtype=jnp.float32) / np.sqrt(DIM)
        w_kv = jax.random.normal(ks[3], (DIM, 2 * INNER), dtype=jnp.float32) / np.sqrt(DIM)
        w_out = jax.random.normal(ks[4], (INNER, DIM), dtype=jnp.float32) / np.sqrt(INNER)
        b_out = jnp.zeros((DIM,), jnp.float32)
        gate = jnp.array([0.5], jnp.float32)
        return {'x': x, 'context': context, 'ln_gamma': ln_gamma, 'ln_beta': ln_beta, 'w_q': w_q, 'w_kv': w_kv, 'w_out': w_out, 'b_out': b_out, 'gate': gate}
    _L0_xattn_all = _L0_xattn_setup()
    _L0_xattn_in = {k: v for k, v in _L0_xattn_all.items() if k in ('ln_gamma', 'ln_beta', 'w_q', 'w_kv', 'w_out', 'b_out', 'gate')}
    del _L0_xattn_all

    def _L0_attn_setup():
        import jax, jax.numpy as jnp
        import numpy as np
        import math
        B, T, D, H = (4, 512, 512, 16)
        DK = D // H
        EPS = 1e-12
        key = jax.random.key(seed)
        ks = jax.random.split(key, 6)
        xav = math.sqrt(6.0 / (D + D))
        x = jax.random.normal(ks[0], (B, T, D), dtype=jnp.float32)
        Wq = jax.random.uniform(ks[1], (D, D), jnp.float32, -xav, xav)
        Wk = jax.random.uniform(ks[2], (D, D), jnp.float32, -xav, xav)
        Wv = jax.random.uniform(ks[3], (D, D), jnp.float32, -xav, xav)
        Wo = jax.random.uniform(ks[4], (D, D), jnp.float32, -xav, xav)
        logit_g = math.log(0.9 / 0.1)
        logit_l = math.log(0.1 / 0.9)
        W_gamma = jnp.zeros((H,), jnp.float32)
        b_gamma = jnp.full((H,), logit_g, jnp.float32)
        W_lambda = jnp.zeros((H,), jnp.float32)
        b_lambda = jnp.full((H,), logit_l, jnp.float32)
        return {'x': x, 'Wq': Wq, 'Wk': Wk, 'Wv': Wv, 'Wo': Wo, 'W_gamma': W_gamma, 'b_gamma': b_gamma, 'W_lambda': W_lambda, 'b_lambda': b_lambda}
    _L0_attn_all = _L0_attn_setup()
    _L0_attn_in = {k: v for k, v in _L0_attn_all.items() if k in ('Wq', 'Wk', 'Wv', 'Wo', 'W_gamma', 'b_gamma', 'W_lambda', 'b_lambda')}
    del _L0_attn_all

    def _L0_ffn_setup():
        import jax, jax.numpy as jnp
        import numpy as np
        B, S, D = (2, 512, 512)
        H, HD = (16, 64)
        E_R = 31
        K_ACT = 3
        INTER = 512
        EPS = 1e-05
        BASE = 10000.0

        def _rmsnorm(x, gamma):
            rms = jnp.sqrt(jnp.mean(x * x, axis=-1, keepdims=True) + EPS)
            return x / rms * gamma

        def _rope(x, theta):
            seq = x.shape[2]
            angles = jnp.arange(seq, dtype=theta.dtype)[:, None] * theta
            cos = jnp.cos(angles)[None, None]
            sin = jnp.sin(angles)[None, None]
            x1, x2 = (x[..., 0::2], x[..., 1::2])
            return jnp.concatenate([x1 * cos - x2 * sin, x1 * sin + x2 * cos], axis=-1)

        def _forward(x, theta, gamma1, gamma2, q_w, q_b, k_w, k_b, v_w, v_b, o_w, o_b, router_w, router_b, sh_w1, sh_b1, sh_w2, sh_b2, re_w1, re_b1, re_w2, re_b2):
            b, s, d = x.shape
            xn = _rmsnorm(x, gamma1)
            q = (xn @ q_w + q_b).reshape(b, s, H, HD).transpose(0, 2, 1, 3)
            k = (xn @ k_w + k_b).reshape(b, s, H, HD).transpose(0, 2, 1, 3)
            v = (xn @ v_w + v_b).reshape(b, s, H, HD).transpose(0, 2, 1, 3)
            q = _rope(q, theta)
            k = _rope(k, theta)
            scale = 1.0 / np.sqrt(HD)
            scores = jnp.einsum('bhqd,bhkd->bhqk', q, k) * scale
            causal = jnp.tril(jnp.ones((s, s), dtype=bool))
            scores = jnp.where(causal, scores, -jnp.inf)
            attn = jax.nn.softmax(scores, axis=-1)
            ctx = jnp.einsum('bhqk,bhkd->bhqd', attn, v)
            ctx = ctx.transpose(0, 2, 1, 3).reshape(b, s, H * HD)
            attn_out = ctx @ o_w + o_b + xn
            an = _rmsnorm(attn_out, gamma2)
            shared = jax.nn.gelu(an @ sh_w1 + sh_b1, approximate=False) @ sh_w2 + sh_b2
            logits = an @ router_w + router_b
            aff = jax.nn.softmax(logits, axis=-1)
            topv, topi = jax.lax.top_k(aff, K_ACT)
            gates = jnp.sum(jax.nn.one_hot(topi, E_R, dtype=aff.dtype) * topv[..., None], axis=-2)
            h = jax.nn.gelu(jnp.einsum('bsd,edh->besh', an, re_w1) + re_b1[None, :, None, :], approximate=False)
            routed = jnp.einsum('bse,besh,ehd->bsd', gates, h, re_w2) + jnp.einsum('bse,ed->bsd', gates, re_b2)
            return shared + routed + an + attn_out
        key = jax.random.key(seed)
        ks = jax.random.split(key, 24)
        s = 0.02
        theta = BASE ** (-jnp.arange(HD // 2, dtype=jnp.float32) * 2.0 / HD)
        inp = {'x': jax.random.normal(ks[0], (B, S, D), jnp.float32), 'positions': jnp.arange(S, dtype=jnp.int32), 'theta': theta, 'gamma1': jnp.ones((D,), jnp.float32), 'gamma2': jnp.ones((D,), jnp.float32), 'q_w': jax.random.normal(ks[1], (D, H * HD), jnp.float32) * s, 'q_b': jnp.zeros((H * HD,), jnp.float32), 'k_w': jax.random.normal(ks[2], (D, H * HD), jnp.float32) * s, 'k_b': jnp.zeros((H * HD,), jnp.float32), 'v_w': jax.random.normal(ks[3], (D, H * HD), jnp.float32) * s, 'v_b': jnp.zeros((H * HD,), jnp.float32), 'o_w': jax.random.normal(ks[4], (H * HD, D), jnp.float32) * s, 'o_b': jnp.zeros((D,), jnp.float32), 'router_w': jax.random.normal(ks[5], (D, E_R), jnp.float32) * s, 'router_b': jnp.zeros((E_R,), jnp.float32), 'sh_w1': jax.random.normal(ks[6], (D, INTER), jnp.float32) * s, 'sh_b1': jnp.zeros((INTER,), jnp.float32), 'sh_w2': jax.random.normal(ks[7], (INTER, D), jnp.float32) * s, 'sh_b2': jnp.zeros((D,), jnp.float32), 're_w1': jax.random.normal(ks[8], (E_R, D, INTER), jnp.float32) * s, 're_b1': jnp.zeros((E_R, INTER), jnp.float32), 're_w2': jax.random.normal(ks[9], (E_R, INTER, D), jnp.float32) * s, 're_b2': jnp.zeros((E_R, D), jnp.float32)}
        return inp
    _L0_ffn_all = _L0_ffn_setup()
    _L0_ffn_in = {k: v for k, v in _L0_ffn_all.items() if k in ('positions', 'theta', 'gamma1', 'gamma2', 'q_w', 'q_b', 'k_w', 'k_b', 'v_w', 'v_b', 'o_w', 'o_b', 'router_w', 'router_b', 'sh_w1', 'sh_b1', 'sh_w2', 'sh_b2', 're_w1', 're_b1', 're_w2', 're_b2')}
    del _L0_ffn_all

    def _L1_xattn_setup():
        import jax, jax.numpy as jnp
        import numpy as np
        EMBED = 512
        HEADS = 16
        HEAD_DIM = EMBED // HEADS
        B, S = (4, 1024)
        key = jax.random.key(seed)
        ks = jax.random.split(key, 12)
        sc = 1.0 / np.sqrt(EMBED)
        inp = {'query': jax.random.normal(ks[0], (B, S, EMBED), jnp.float32), 'keys': jax.random.normal(ks[1], (B, S, EMBED), jnp.float32), 'values': jax.random.normal(ks[2], (B, S, EMBED), jnp.float32), 'mask': jax.random.randint(ks[3], (B, S), 0, 2, jnp.int32), 'Wq': jax.random.normal(ks[4], (EMBED, EMBED), jnp.float32) * sc, 'bq': jnp.zeros((EMBED,), jnp.float32), 'Wk': jax.random.normal(ks[5], (EMBED, EMBED), jnp.float32) * sc, 'bk': jnp.zeros((EMBED,), jnp.float32), 'Wv': jax.random.normal(ks[6], (EMBED, EMBED), jnp.float32) * sc, 'bv': jnp.zeros((EMBED,), jnp.float32), 'Wo': jax.random.normal(ks[7], (EMBED, EMBED), jnp.float32) * sc, 'bo': jnp.zeros((EMBED,), jnp.float32)}
        return inp
    _L1_xattn_all = _L1_xattn_setup()
    _L1_xattn_in = {k: v for k, v in _L1_xattn_all.items() if k in ('Wq', 'bq', 'Wk', 'bk', 'Wv', 'bv', 'Wo', 'bo')}
    del _L1_xattn_all

    def _L1_attn_setup():
        import jax, jax.numpy as jnp
        import numpy as np
        E = 512
        NH = 4
        DH = E // NH
        GATE_SOFT_CAP = 15.0
        NORM_EPS = 1e-06
        BACKEND_EPS = 1e-06

        def soft_cap(x, cap):
            return cap * jnp.tanh(x / cap)

        def mlstm_parallel(q, k, v, ig, fg):
            q = q.transpose(0, 2, 1, 3)
            k = k.transpose(0, 2, 1, 3)
            v = v.transpose(0, 2, 1, 3)
            ig = ig.squeeze(-1).transpose(0, 2, 1)
            fg = fg.squeeze(-1).transpose(0, 2, 1)
            S = q.shape[2]
            log_fg = jax.nn.log_sigmoid(fg)
            lf_cum = jnp.cumsum(log_fg, axis=-1)
            fg_mat = lf_cum[..., :, None] - lf_cum[..., None, :]
            causal = jnp.tril(jnp.ones((S, S), dtype=bool))
            neg_inf = jnp.finfo(q.dtype).min
            log_D = jnp.where(causal, fg_mat + ig[..., None, :], neg_inf)
            m = jnp.max(log_D, axis=-1, keepdims=True)
            D = jnp.exp(log_D - m)
            scores = jnp.einsum('bhid,bhjd->bhij', q, k) / jnp.sqrt(jnp.float32(DH))
            C = scores * D
            n = jnp.maximum(jnp.abs(C.sum(axis=-1, keepdims=True)), jnp.exp(-m))
            h = jnp.einsum('bhij,bhjd->bhid', C, v) / (n + BACKEND_EPS)
            return h.transpose(0, 2, 1, 3)

        def multi_head_norm(h, w, eps):
            mu = h.mean(axis=-1, keepdims=True)
            var = ((h - mu) ** 2).mean(axis=-1, keepdims=True)
            return (h - mu) * jax.lax.rsqrt(var + eps) * w
        key = jax.random.key(seed)
        ks = jax.random.split(key, 12)
        B, S = (2, 1024)
        sd = 1.0 / np.sqrt(E)
        x = jax.random.normal(ks[0], (B, S, E), jnp.float32)
        Wq = jax.random.normal(ks[1], (E, E), jnp.float32) * sd
        Wk = jax.random.normal(ks[2], (E, E), jnp.float32) * sd
        Wv = jax.random.normal(ks[3], (E, E), jnp.float32) * sd
        Wo = jax.random.normal(ks[4], (E, E), jnp.float32) * sd
        Wig = jax.random.normal(ks[5], (E, NH), jnp.float32) * 0.01
        big = jax.random.normal(ks[6], (NH,), jnp.float32) * 0.1 - 10.0
        Wfg = jax.random.normal(ks[7], (E, NH), jnp.float32) * 0.01
        bfg = jnp.linspace(3.0, 6.0, NH, dtype=jnp.float32)
        norm_w = jnp.ones((NH, DH), jnp.float32)
        Wdown = jax.random.normal(ks[8], (E, E), jnp.float32) * sd
        return {'x': x, 'Wq': Wq, 'Wk': Wk, 'Wv': Wv, 'Wo': Wo, 'Wig': Wig, 'big': big, 'Wfg': Wfg, 'bfg': bfg, 'norm_w': norm_w, 'Wdown': Wdown}
    _L1_attn_all = _L1_attn_setup()
    _L1_attn_in = {k: v for k, v in _L1_attn_all.items() if k in ('Wq', 'Wk', 'Wv', 'Wo', 'Wig', 'big', 'Wfg', 'bfg', 'norm_w', 'Wdown')}
    del _L1_attn_all

    def _L1_ffn_setup():
        import jax, jax.numpy as jnp
        import numpy as np
        DIM = 512
        INTER = 704
        N_EXPERTS = 16
        TOPK = 2
        N_SHARED = 2
        SHARED_INTER = N_SHARED * INTER
        ROUTE_SCALE = 1.0
        key = jax.random.key(seed)
        ks = jax.random.split(key, 16)
        s = 0.02
        return {'x': jax.random.normal(ks[0], (2, 1024, DIM), dtype=jnp.float32), 'gate_w': jax.random.normal(ks[1], (DIM, N_EXPERTS), dtype=jnp.float32) * s, 'gate_b': jnp.zeros((N_EXPERTS,), dtype=jnp.float32), 'w1': jax.random.normal(ks[2], (N_EXPERTS, DIM, INTER), dtype=jnp.float32) * s, 'b1': jnp.zeros((N_EXPERTS, INTER), dtype=jnp.float32), 'w3': jax.random.normal(ks[3], (N_EXPERTS, DIM, INTER), dtype=jnp.float32) * s, 'b3': jnp.zeros((N_EXPERTS, INTER), dtype=jnp.float32), 'w2': jax.random.normal(ks[4], (N_EXPERTS, INTER, DIM), dtype=jnp.float32) * s, 'b2': jnp.zeros((N_EXPERTS, DIM), dtype=jnp.float32), 'sw1': jax.random.normal(ks[5], (DIM, SHARED_INTER), dtype=jnp.float32) * s, 'sb1': jax.random.normal(ks[6], (SHARED_INTER,), dtype=jnp.float32) * s, 'sw3': jax.random.normal(ks[7], (DIM, SHARED_INTER), dtype=jnp.float32) * s, 'sb3': jax.random.normal(ks[8], (SHARED_INTER,), dtype=jnp.float32) * s, 'sw2': jax.random.normal(ks[9], (SHARED_INTER, DIM), dtype=jnp.float32) * s, 'sb2': jax.random.normal(ks[10], (DIM,), dtype=jnp.float32) * s}
    _L1_ffn_all = _L1_ffn_setup()
    _L1_ffn_in = {k: v for k, v in _L1_ffn_all.items() if k in ('gate_w', 'gate_b', 'w1', 'b1', 'w3', 'b3', 'w2', 'b2', 'sw1', 'sb1', 'sw3', 'sb3', 'sw2', 'sb2')}
    del _L1_ffn_all
    return {'x': x, 'ctx_1024': ctx_1024, 'mask_BxS2_ik0': mask_BxS2_ik0, 'L0_xattn_ln_gamma': _L0_xattn_in['ln_gamma'], 'L0_xattn_ln_beta': _L0_xattn_in['ln_beta'], 'L0_xattn_w_q': _L0_xattn_in['w_q'], 'L0_xattn_w_kv': _L0_xattn_in['w_kv'], 'L0_xattn_w_out': _L0_xattn_in['w_out'], 'L0_xattn_b_out': _L0_xattn_in['b_out'], 'L0_xattn_gate': _L0_xattn_in['gate'], 'L0_attn_Wq': _L0_attn_in['Wq'], 'L0_attn_Wk': _L0_attn_in['Wk'], 'L0_attn_Wv': _L0_attn_in['Wv'], 'L0_attn_Wo': _L0_attn_in['Wo'], 'L0_attn_W_gamma': _L0_attn_in['W_gamma'], 'L0_attn_b_gamma': _L0_attn_in['b_gamma'], 'L0_attn_W_lambda': _L0_attn_in['W_lambda'], 'L0_attn_b_lambda': _L0_attn_in['b_lambda'], 'L0_ffn_positions': _L0_ffn_in['positions'], 'L0_ffn_theta': _L0_ffn_in['theta'], 'L0_ffn_gamma1': _L0_ffn_in['gamma1'], 'L0_ffn_gamma2': _L0_ffn_in['gamma2'], 'L0_ffn_q_w': _L0_ffn_in['q_w'], 'L0_ffn_q_b': _L0_ffn_in['q_b'], 'L0_ffn_k_w': _L0_ffn_in['k_w'], 'L0_ffn_k_b': _L0_ffn_in['k_b'], 'L0_ffn_v_w': _L0_ffn_in['v_w'], 'L0_ffn_v_b': _L0_ffn_in['v_b'], 'L0_ffn_o_w': _L0_ffn_in['o_w'], 'L0_ffn_o_b': _L0_ffn_in['o_b'], 'L0_ffn_router_w': _L0_ffn_in['router_w'], 'L0_ffn_router_b': _L0_ffn_in['router_b'], 'L0_ffn_sh_w1': _L0_ffn_in['sh_w1'], 'L0_ffn_sh_b1': _L0_ffn_in['sh_b1'], 'L0_ffn_sh_w2': _L0_ffn_in['sh_w2'], 'L0_ffn_sh_b2': _L0_ffn_in['sh_b2'], 'L0_ffn_re_w1': _L0_ffn_in['re_w1'], 'L0_ffn_re_b1': _L0_ffn_in['re_b1'], 'L0_ffn_re_w2': _L0_ffn_in['re_w2'], 'L0_ffn_re_b2': _L0_ffn_in['re_b2'], 'L1_xattn_Wq': _L1_xattn_in['Wq'], 'L1_xattn_bq': _L1_xattn_in['bq'], 'L1_xattn_Wk': _L1_xattn_in['Wk'], 'L1_xattn_bk': _L1_xattn_in['bk'], 'L1_xattn_Wv': _L1_xattn_in['Wv'], 'L1_xattn_bv': _L1_xattn_in['bv'], 'L1_xattn_Wo': _L1_xattn_in['Wo'], 'L1_xattn_bo': _L1_xattn_in['bo'], 'L1_attn_Wq': _L1_attn_in['Wq'], 'L1_attn_Wk': _L1_attn_in['Wk'], 'L1_attn_Wv': _L1_attn_in['Wv'], 'L1_attn_Wo': _L1_attn_in['Wo'], 'L1_attn_Wig': _L1_attn_in['Wig'], 'L1_attn_big': _L1_attn_in['big'], 'L1_attn_Wfg': _L1_attn_in['Wfg'], 'L1_attn_bfg': _L1_attn_in['bfg'], 'L1_attn_norm_w': _L1_attn_in['norm_w'], 'L1_attn_Wdown': _L1_attn_in['Wdown'], 'L1_ffn_gate_w': _L1_ffn_in['gate_w'], 'L1_ffn_gate_b': _L1_ffn_in['gate_b'], 'L1_ffn_w1': _L1_ffn_in['w1'], 'L1_ffn_b1': _L1_ffn_in['b1'], 'L1_ffn_w3': _L1_ffn_in['w3'], 'L1_ffn_b3': _L1_ffn_in['b3'], 'L1_ffn_w2': _L1_ffn_in['w2'], 'L1_ffn_b2': _L1_ffn_in['b2'], 'L1_ffn_sw1': _L1_ffn_in['sw1'], 'L1_ffn_sb1': _L1_ffn_in['sb1'], 'L1_ffn_sw3': _L1_ffn_in['sw3'], 'L1_ffn_sb3': _L1_ffn_in['sb3'], 'L1_ffn_sw2': _L1_ffn_in['sw2'], 'L1_ffn_sb2': _L1_ffn_in['sb2']}

def reference(x, ctx_1024, mask_BxS2_ik0, L0_xattn_ln_gamma, L0_xattn_ln_beta, L0_xattn_w_q, L0_xattn_w_kv, L0_xattn_w_out, L0_xattn_b_out, L0_xattn_gate, L0_attn_Wq, L0_attn_Wk, L0_attn_Wv, L0_attn_Wo, L0_attn_W_gamma, L0_attn_b_gamma, L0_attn_W_lambda, L0_attn_b_lambda, L0_ffn_positions, L0_ffn_theta, L0_ffn_gamma1, L0_ffn_gamma2, L0_ffn_q_w, L0_ffn_q_b, L0_ffn_k_w, L0_ffn_k_b, L0_ffn_v_w, L0_ffn_v_b, L0_ffn_o_w, L0_ffn_o_b, L0_ffn_router_w, L0_ffn_router_b, L0_ffn_sh_w1, L0_ffn_sh_b1, L0_ffn_sh_w2, L0_ffn_sh_b2, L0_ffn_re_w1, L0_ffn_re_b1, L0_ffn_re_w2, L0_ffn_re_b2, L1_xattn_Wq, L1_xattn_bq, L1_xattn_Wk, L1_xattn_bk, L1_xattn_Wv, L1_xattn_bv, L1_xattn_Wo, L1_xattn_bo, L1_attn_Wq, L1_attn_Wk, L1_attn_Wv, L1_attn_Wo, L1_attn_Wig, L1_attn_big, L1_attn_Wfg, L1_attn_bfg, L1_attn_norm_w, L1_attn_Wdown, L1_ffn_gate_w, L1_ffn_gate_b, L1_ffn_w1, L1_ffn_b1, L1_ffn_w3, L1_ffn_b3, L1_ffn_w2, L1_ffn_b2, L1_ffn_sw1, L1_ffn_sb1, L1_ffn_sw3, L1_ffn_sb3, L1_ffn_sw2, L1_ffn_sb2):
    import jax
    import jax.numpy as jnp

    def _L0_xattn_ref(x, context, ln_gamma, ln_beta, w_q, w_kv, w_out, b_out, gate):
        import jax, jax.numpy as jnp
        import numpy as np
        DIM = 512
        NUM_HEADS = 16
        DIM_HEAD = 64
        INNER = NUM_HEADS * DIM_HEAD
        SCALE = DIM_HEAD ** (-0.5)

        def _layernorm(x, gamma, beta, eps=1e-05):
            mu = jnp.mean(x, axis=-1, keepdims=True)
            var = jnp.mean(jnp.square(x - mu), axis=-1, keepdims=True)
            return (x - mu) * jax.lax.rsqrt(var + eps) * gamma + beta
        B, SQ, _ = x.shape
        SK = context.shape[1]
        xn = _layernorm(x, ln_gamma, ln_beta)
        q = (xn @ w_q).reshape(B, SQ, NUM_HEADS, DIM_HEAD)
        kv = context @ w_kv
        k, v = jnp.split(kv, 2, axis=-1)
        k = k.reshape(B, SK, NUM_HEADS, DIM_HEAD)
        v = v.reshape(B, SK, NUM_HEADS, DIM_HEAD)
        scores = jnp.einsum('bqhd,bkhd->bhqk', q * SCALE, k)
        attn = jax.nn.softmax(scores, axis=-1)
        out = jnp.einsum('bhqk,bkhd->bqhd', attn, v).reshape(B, SQ, INNER)
        out = out @ w_out + b_out
        return out * jnp.tanh(gate[0])

    def _L0_attn_ref(x, Wq, Wk, Wv, Wo, W_gamma, b_gamma, W_lambda, b_lambda):
        import jax, jax.numpy as jnp
        import numpy as np
        import math
        B, T, D, H = (4, 512, 512, 16)
        DK = D // H
        EPS = 1e-12
        b, t, d = x.shape

        def proj(W):
            return jnp.einsum('btd,ed->bte', x, W).reshape(b, t, H, DK).transpose(1, 0, 2, 3)
        q = proj(Wq)
        k = proj(Wk)
        v = proj(Wv)
        k = k / jnp.maximum(jnp.linalg.norm(k, axis=-1, keepdims=True), EPS)
        k_bar = k.mean(axis=-1)
        gamma = jax.nn.sigmoid(W_gamma * k_bar + b_gamma)
        lam = jax.nn.sigmoid(W_lambda * k_bar + b_lambda)
        rho = (1.0 - lam) * gamma
        S0 = jnp.zeros((b, H, DK, DK), x.dtype)

        def step(S, inp):
            q_t, k_t, v_t, rho_t = inp
            r = rho_t[..., None, None]
            S = r * S + (1.0 - r) * jnp.einsum('bhv,bhk->bhvk', v_t, k_t)
            y_t = jnp.einsum('bhv,bhvk->bhk', q_t, S)
            return (S, y_t)
        _, ys = jax.lax.scan(step, S0, (q, k, v, rho))
        out = ys.transpose(1, 0, 2, 3).reshape(b, t, d)
        return jnp.einsum('btd,ed->bte', out, Wo)

    def _L0_ffn_ref(x, positions, theta, gamma1, gamma2, q_w, q_b, k_w, k_b, v_w, v_b, o_w, o_b, router_w, router_b, sh_w1, sh_b1, sh_w2, sh_b2, re_w1, re_b1, re_w2, re_b2):
        import jax, jax.numpy as jnp
        import numpy as np
        B, S, D = (2, 512, 512)
        H, HD = (16, 64)
        E_R = 31
        K_ACT = 3
        INTER = 512
        EPS = 1e-05
        BASE = 10000.0

        def _rmsnorm(x, gamma):
            rms = jnp.sqrt(jnp.mean(x * x, axis=-1, keepdims=True) + EPS)
            return x / rms * gamma

        def _rope(x, theta):
            seq = x.shape[2]
            angles = jnp.arange(seq, dtype=theta.dtype)[:, None] * theta
            cos = jnp.cos(angles)[None, None]
            sin = jnp.sin(angles)[None, None]
            x1, x2 = (x[..., 0::2], x[..., 1::2])
            return jnp.concatenate([x1 * cos - x2 * sin, x1 * sin + x2 * cos], axis=-1)

        def _forward(x, theta, gamma1, gamma2, q_w, q_b, k_w, k_b, v_w, v_b, o_w, o_b, router_w, router_b, sh_w1, sh_b1, sh_w2, sh_b2, re_w1, re_b1, re_w2, re_b2):
            b, s, d = x.shape
            xn = _rmsnorm(x, gamma1)
            q = (xn @ q_w + q_b).reshape(b, s, H, HD).transpose(0, 2, 1, 3)
            k = (xn @ k_w + k_b).reshape(b, s, H, HD).transpose(0, 2, 1, 3)
            v = (xn @ v_w + v_b).reshape(b, s, H, HD).transpose(0, 2, 1, 3)
            q = _rope(q, theta)
            k = _rope(k, theta)
            scale = 1.0 / np.sqrt(HD)
            scores = jnp.einsum('bhqd,bhkd->bhqk', q, k) * scale
            causal = jnp.tril(jnp.ones((s, s), dtype=bool))
            scores = jnp.where(causal, scores, -jnp.inf)
            attn = jax.nn.softmax(scores, axis=-1)
            ctx = jnp.einsum('bhqk,bhkd->bhqd', attn, v)
            ctx = ctx.transpose(0, 2, 1, 3).reshape(b, s, H * HD)
            attn_out = ctx @ o_w + o_b + xn
            an = _rmsnorm(attn_out, gamma2)
            shared = jax.nn.gelu(an @ sh_w1 + sh_b1, approximate=False) @ sh_w2 + sh_b2
            logits = an @ router_w + router_b
            aff = jax.nn.softmax(logits, axis=-1)
            topv, topi = jax.lax.top_k(aff, K_ACT)
            gates = jnp.sum(jax.nn.one_hot(topi, E_R, dtype=aff.dtype) * topv[..., None], axis=-2)
            h = jax.nn.gelu(jnp.einsum('bsd,edh->besh', an, re_w1) + re_b1[None, :, None, :], approximate=False)
            routed = jnp.einsum('bse,besh,ehd->bsd', gates, h, re_w2) + jnp.einsum('bse,ed->bsd', gates, re_b2)
            return shared + routed + an + attn_out
        del positions
        return _forward(x, theta, gamma1, gamma2, q_w, q_b, k_w, k_b, v_w, v_b, o_w, o_b, router_w, router_b, sh_w1, sh_b1, sh_w2, sh_b2, re_w1, re_b1, re_w2, re_b2)

    def _L1_xattn_ref(query, keys, values, mask, Wq, bq, Wk, bk, Wv, bv, Wo, bo):
        import jax, jax.numpy as jnp
        import numpy as np
        EMBED = 512
        HEADS = 16
        HEAD_DIM = EMBED // HEADS
        B, S = (4, 1024)
        N, Lq, _ = query.shape
        Lk = keys.shape[1]
        q = (query @ Wq.T + bq).reshape(N, Lq, HEADS, HEAD_DIM).transpose(0, 2, 1, 3)
        k = (keys @ Wk.T + bk).reshape(N, Lk, HEADS, HEAD_DIM).transpose(0, 2, 1, 3)
        v = (values @ Wv.T + bv).reshape(N, Lk, HEADS, HEAD_DIM).transpose(0, 2, 1, 3)
        energy = jnp.einsum('bhqd,bhkd->bhqk', q, k)
        energy = jnp.where(mask[:, None, None, :] == 0, jnp.float32(-1e+20), energy)
        attention = jax.nn.softmax(energy / np.sqrt(HEAD_DIM), axis=-1)
        out = jnp.einsum('bhqk,bhkd->bhqd', attention, v)
        out = out.transpose(0, 2, 1, 3).reshape(N, Lq, EMBED)
        return out @ Wo.T + bo

    def _L1_attn_ref(x, Wq, Wk, Wv, Wo, Wig, big, Wfg, bfg, norm_w, Wdown):
        import jax, jax.numpy as jnp
        import numpy as np
        E = 512
        NH = 4
        DH = E // NH
        GATE_SOFT_CAP = 15.0
        NORM_EPS = 1e-06
        BACKEND_EPS = 1e-06

        def soft_cap(x, cap):
            return cap * jnp.tanh(x / cap)

        def mlstm_parallel(q, k, v, ig, fg):
            q = q.transpose(0, 2, 1, 3)
            k = k.transpose(0, 2, 1, 3)
            v = v.transpose(0, 2, 1, 3)
            ig = ig.squeeze(-1).transpose(0, 2, 1)
            fg = fg.squeeze(-1).transpose(0, 2, 1)
            S = q.shape[2]
            log_fg = jax.nn.log_sigmoid(fg)
            lf_cum = jnp.cumsum(log_fg, axis=-1)
            fg_mat = lf_cum[..., :, None] - lf_cum[..., None, :]
            causal = jnp.tril(jnp.ones((S, S), dtype=bool))
            neg_inf = jnp.finfo(q.dtype).min
            log_D = jnp.where(causal, fg_mat + ig[..., None, :], neg_inf)
            m = jnp.max(log_D, axis=-1, keepdims=True)
            D = jnp.exp(log_D - m)
            scores = jnp.einsum('bhid,bhjd->bhij', q, k) / jnp.sqrt(jnp.float32(DH))
            C = scores * D
            n = jnp.maximum(jnp.abs(C.sum(axis=-1, keepdims=True)), jnp.exp(-m))
            h = jnp.einsum('bhij,bhjd->bhid', C, v) / (n + BACKEND_EPS)
            return h.transpose(0, 2, 1, 3)

        def multi_head_norm(h, w, eps):
            mu = h.mean(axis=-1, keepdims=True)
            var = ((h - mu) ** 2).mean(axis=-1, keepdims=True)
            return (h - mu) * jax.lax.rsqrt(var + eps) * w
        B, S, _ = x.shape
        q = (x @ Wq).reshape(B, S, NH, DH)
        k = (x @ Wk).reshape(B, S, NH, DH)
        v = (x @ Wv).reshape(B, S, NH, DH)
        o = x @ Wo
        ig = soft_cap(x @ Wig + big, GATE_SOFT_CAP)[..., None]
        fg = soft_cap(x @ Wfg + bfg, GATE_SOFT_CAP)[..., None]
        h = mlstm_parallel(q, k, v, ig, fg)
        hn = multi_head_norm(h, norm_w, NORM_EPS).reshape(B, S, -1)
        h_out = jax.nn.sigmoid(o) * hn
        return h_out @ Wdown

    def _L1_ffn_ref(x, gate_w, gate_b, w1, b1, w3, b3, w2, b2, sw1, sb1, sw3, sb3, sw2, sb2):
        import jax, jax.numpy as jnp
        import numpy as np
        DIM = 512
        INTER = 704
        N_EXPERTS = 16
        TOPK = 2
        N_SHARED = 2
        SHARED_INTER = N_SHARED * INTER
        ROUTE_SCALE = 1.0
        shape = x.shape
        xf = x.reshape(-1, DIM)
        logits = xf @ gate_w + gate_b
        scores = jax.nn.softmax(logits.astype(jnp.float32), axis=-1)
        top_vals, top_idx = jax.lax.top_k(scores, TOPK)
        weights = (top_vals * ROUTE_SCALE).astype(x.dtype)
        cw = (jax.nn.one_hot(top_idx, N_EXPERTS, dtype=x.dtype) * weights[..., None]).sum(axis=1)
        h = jnp.einsum('td,edh->teh', xf, w1) + b1
        g = jnp.einsum('td,edh->teh', xf, w3) + b3
        a = jax.nn.silu(h) * g
        y = jnp.einsum('teh,ehd,te->td', a, w2, cw) + cw @ b2
        z = jax.nn.silu(xf @ sw1 + sb1) * (xf @ sw3 + sb3) @ sw2 + sb2
        return (y + z).reshape(shape)
    x = x + _L0_xattn_ref(_layernorm(x, axis=-1), ctx_1024, L0_xattn_ln_gamma, L0_xattn_ln_beta, L0_xattn_w_q, L0_xattn_w_kv, L0_xattn_w_out, L0_xattn_b_out, L0_xattn_gate)
    x = x + _L0_attn_ref(_layernorm(x, axis=-1), L0_attn_Wq, L0_attn_Wk, L0_attn_Wv, L0_attn_Wo, L0_attn_W_gamma, L0_attn_b_gamma, L0_attn_W_lambda, L0_attn_b_lambda)
    x = x + _L0_ffn_ref(_layernorm(x, axis=-1), L0_ffn_positions, L0_ffn_theta, L0_ffn_gamma1, L0_ffn_gamma2, L0_ffn_q_w, L0_ffn_q_b, L0_ffn_k_w, L0_ffn_k_b, L0_ffn_v_w, L0_ffn_v_b, L0_ffn_o_w, L0_ffn_o_b, L0_ffn_router_w, L0_ffn_router_b, L0_ffn_sh_w1, L0_ffn_sh_b1, L0_ffn_sh_w2, L0_ffn_sh_b2, L0_ffn_re_w1, L0_ffn_re_b1, L0_ffn_re_w2, L0_ffn_re_b2)
    x = x + _L1_xattn_ref(_layernorm(x, axis=-1), ctx_1024, ctx_1024, mask_BxS2_ik0, L1_xattn_Wq, L1_xattn_bq, L1_xattn_Wk, L1_xattn_bk, L1_xattn_Wv, L1_xattn_bv, L1_xattn_Wo, L1_xattn_bo)
    x = x + _L1_attn_ref(_layernorm(x, axis=-1), L1_attn_Wq, L1_attn_Wk, L1_attn_Wv, L1_attn_Wo, L1_attn_Wig, L1_attn_big, L1_attn_Wfg, L1_attn_bfg, L1_attn_norm_w, L1_attn_Wdown)
    x = x + _L1_ffn_ref(_layernorm(x, axis=-1), L1_ffn_gate_w, L1_ffn_gate_b, L1_ffn_w1, L1_ffn_b1, L1_ffn_w3, L1_ffn_b3, L1_ffn_w2, L1_ffn_b2, L1_ffn_sw1, L1_ffn_sb1, L1_ffn_sw3, L1_ffn_sb3, L1_ffn_sw2, L1_ffn_sb2)
    return x

_drawn_inputs = setup_inputs


def setup_inputs(seed=0):
    import zlib

    import numpy as np

    out = dict(_drawn_inputs(seed))
    spreads = {'L0_xattn_ln_gamma': (1.0, 0.6),
     'L0_xattn_ln_beta': (0.0, 0.763),
     'L0_xattn_b_out': (0.0, 0.1),
     'L0_attn_W_gamma': (0.0, 0.8),
     'L0_attn_b_gamma': (2.1972246170043945, 0.2),
     'L0_attn_W_lambda': (0.0, 0.8),
     'L0_attn_b_lambda': (-2.1972246170043945, 0.2),
     'L0_ffn_gamma1': (1.0, 0.2),
     'L0_ffn_gamma2': (1.0, 0.2),
     'L0_ffn_q_b': (0.0, 0.8),
     'L0_ffn_k_b': (0.0, 0.8),
     'L0_ffn_v_b': (0.0, 0.1),
     'L0_ffn_o_b': (0.0, 0.1),
     'L0_ffn_router_b': (0.0, 0.8),
     'L0_ffn_sh_b1': (0.0, 0.8),
     'L0_ffn_sh_b2': (0.0, 0.1),
     'L0_ffn_re_b1': (0.0, 0.8),
     'L0_ffn_re_b2': (0.0, 0.8),
     'L1_xattn_bq': (0.0, 0.8),
     'L1_xattn_bk': (0.0, 2.0),
     'L1_xattn_bv': (0.0, 0.1),
     'L1_xattn_bo': (0.0, 0.1),
     'L1_attn_norm_w': (1.0, 0.6),
     'L1_ffn_gate_b': (0.0, 0.8),
     'L1_ffn_b1': (0.0, 0.8),
     'L1_ffn_b3': (0.0, 0.8),
     'L1_ffn_b2': (0.0, 2.0)}
    factors = {'L0_ffn_theta': 8.0,
     'L0_ffn_q_w': 6.07,
     'L0_ffn_k_w': 5.768,
     'L0_ffn_router_w': 8.0,
     'L0_ffn_re_w1': 8.0,
     'L0_ffn_re_w2': 8.0,
     'L1_attn_Wig': 35.968,
     'L1_attn_big': 64.0,
     'L1_attn_Wfg': 64.0,
     'L1_ffn_gate_w': 8.0,
     'L1_ffn_w1': 8.0,
     'L1_ffn_w3': 8.0,
     'L1_ffn_w2': 8.0,
     'L1_ffn_sb1': 64.0,
     'L1_ffn_sb3': 64.0,
     'L1_ffn_sb2': 187.392,
     'L1_attn_Wq': 8.0,
     'L1_attn_Wk': 8.0,
     'L1_attn_Wv': 8.0,
     'L1_attn_Wo': 8.0,
     'L1_attn_bfg': 8.0,
     'L1_attn_Wdown': 8.0,
     'L1_ffn_sw1': 8.0,
     'L1_ffn_sw3': 8.0,
     'L1_ffn_sw2': 8.0}
    for name, (base, spread) in spreads.items():
        noise = np.random.default_rng([zlib.crc32(name.encode()), seed]).standard_normal(out[name].shape)
        drawn = base * np.exp(spread * noise) if base else spread * noise
        out[name] = jnp.asarray(drawn.astype(out[name].dtype))
    for name, factor in factors.items():
        out[name] = (out[name] * factor).astype(out[name].dtype)
    return out
```

```python
from contextlib import ExitStack

import concourse.bass as bass
from concourse import mybir
import numpy as np

P = 128
F32 = mybir.dt.float32
I32 = mybir.dt.int32
ALU = mybir.AluOpType
ACT = mybir.ActivationFunctionType
AX_X = mybir.AxisListType.X

NSEQ, SEQ, DIM, CTX = 8, 64, 512, 512
TOK = NSEQ * SEQ
NT = TOK // P
KT = DIM // P
HEADS = 16
E0, TOP0 = 31, 3
E1, TOP1 = 16, 2
INTER1 = 704
SHARED1 = 1408
GROUPS1 = E1 * INTER1 // DIM
MASKED = -1.0e30
MASK_ENERGY = -1.0e20
EPS_LN = 1e-5
SLOT = KT * DIM

COLS = {}
_n = 0
for _name, _w in [("ln_gamma", 4), ("ln_beta", 4), ("q_b1", 4), ("q_b2", 4), ("k_b1", 4), ("k_b2", 4),
                  ("v_b", 8), ("theta", 1), ("sh_b1", 4), ("re_b1", 4 * E0), ("bq", 4), ("bk", 4), ("bv", 4),
                  ("b1", 4 * GROUPS1), ("b3", 4 * GROUPS1), ("sb1", 11), ("sb3", 11)]:
    COLS[_name] = (_n, _w)
    _n += _w
NCOLS = _n

ROWS = {}
_n = 0
for _name, _w in [("b_out", 512), ("gate", 1), ("W_gamma", 16), ("b_gamma", 16), ("W_lambda", 16),
                  ("b_lambda", 16), ("gamma1", 512), ("gamma2", 512), ("o_b", 512), ("sh_b2", 512),
                  ("router_b", E0), ("bo", 512), ("norm_w", 512), ("b_ifg", 8), ("sb2", 512), ("gate_b", E1)]:
    ROWS[_name] = (_n, _w)
    _n += _w
NROWS = _n


class Step:

    def __init__(self, queue, emit, after):
        self.queue, self.emit, self.after = queue, emit, after
        self.awaited, self.count = False, None


class Queue:

    def __init__(self, sem):
        self.sem, self.steps = sem, []

    def __call__(self, emit, *after):
        step = Step(self, emit, [s for s in after if s is not None])
        for s in step.after:
            s.awaited = True
        self.steps.append(step)
        return step

    def number(self):
        n = 0
        for s in self.steps:
            if s.queue is self and s.awaited:
                n += 1
                s.count = n

    def run(self, eng):
        seen = {}
        for s in self.steps:
            for a in s.after:
                if seen.get(id(a.queue), 0) < a.count:
                    eng.wait_ge(a.queue.sem, a.count)
                    seen[id(a.queue)] = a.count
            ins = s.emit(eng)
            if isinstance(s, Transfer):
                ins.then_inc(s.stream.sem, 16)
            elif s.awaited:
                ins.then_inc(self.sem, 1)


class Stream:

    def __init__(self, sem):
        self.sem, self.total = sem, 0


class Transfer(Step):

    def __init__(self, issuer, stream, emit, after):
        Step.__init__(self, stream, emit, after)
        stream.total += 16
        self.stream, self.count = stream, stream.total


def transfer(issuer, stream, emit, *after):
    t = Transfer(issuer, stream, emit, [s for s in after if s is not None])
    for s in t.after:
        s.awaited = True
    issuer.steps.append(t)
    return t


class Ring:

    def __init__(self, buffers):
        self.buffers, self.read, self.n = buffers, [None] * len(buffers), 0

    def take(self):
        i = self.n % len(self.buffers)
        self.n += 1
        return i, self.buffers[i], self.read[i]

    def free(self, i, step):
        self.read[i] = step


def build_program(nc, A, out_dram):
    ctx = ExitStack()

    def sbuf(name, shape, dt=F32):
        return ctx.enter_context(nc.sbuf_tensor(name, shape, dt))

    x = sbuf("x_tok", [P, NT, DIM])
    xn = sbuf("xn_tok", [P, NT, DIM])
    xnT = sbuf("xnT", [P, KT, TOK])
    cols = sbuf("cols", [P, NCOLS])
    rows = sbuf("rows", [P, NROWS])
    ident = sbuf("ident", [P, P])
    mask_ij = sbuf("mask_ij", [P, P])
    mask_ji = sbuf("mask_ji", [P, P])
    upto = sbuf("upto", [P, P])
    small = sbuf("small", [P, 1024])
    NW = 8
    wslots = [sbuf(f"weights{i}", [P, SLOT]) for i in range(NW)]
    ARENA = 24064
    arena = sbuf("arena", [P, ARENA])
    banks = [ctx.enter_context(nc.psum_tensor(f"bank{i}", [P, 512], F32)) for i in range(8)]

    def sem(name):
        return ctx.enter_context(nc.semaphore(name))

    pe, dve, act, pool, sp = (Queue(sem("s_" + n)) for n in ("tensor", "vector", "scalar", "gpsimd", "sync"))
    compute = (pe, dve, act, pool)

    def col(name, j=0, n=1, lo=0, hi=P):
        a = COLS[name][0] + j
        return cols[lo:hi, a:a + n]

    def row(name, j=0, n=None):
        a, w = ROWS[name]
        return rows[:, a + j:a + j + (w if n is None else n)]

    def over_last(ap, n):
        return ap.unsqueeze(2).to_broadcast([ap.shape[0], ap.shape[1], n])

    def over_middle(ap, n):
        return ap.unsqueeze(1).to_broadcast([ap.shape[0], n, ap.shape[1]])

    class Layout:

        def __init__(self, first=0):
            self.at = first

        def __call__(self, *shape):
            n = 1
            for d in shape:
                n *= d
            assert self.at + n <= ARENA, (self.at, n)
            v = arena[:, self.at:self.at + n]
            self.at += n
            if len(shape) == 2:
                v = v.rearrange("p (a b) -> p a b", a=shape[0])
            if len(shape) == 3:
                v = v.rearrange("p (a b c) -> p a b c", a=shape[0], b=shape[1])
            return v

    def stage_end():
        last = [q.steps[-1] for q in compute if q.steps]
        fence.clear()
        fence.extend(last)

        for q in compute:
            q(lambda e: e.nop(), *last)

    fence = []

    small_at, used = {}, [0]

    def small_reset():
        small_at.clear()
        used[0] = 0

    def small_buf(name, *shape):
        n = int(np.prod(shape))
        if name not in small_at:
            small_at[name] = used[0]
            used[0] += n
            assert used[0] <= 1024
        v = small[:, small_at[name]:small_at[name] + n]
        if len(shape) == 2:
            v = v.rearrange("p (a b) -> p a b", a=shape[0])
        return v

    wstreams = [Stream(sem(f"s_weights{i}")) for i in range(NW)]
    wring = Ring(wslots)

    class Weight:

        def __init__(self, name, chunk):
            self.i, buf, read = wring.take()
            assert read != "held", name
            self.view = buf[:, :].rearrange("p (k n) -> p k n", k=KT)
            src = A[name][chunk]
            self.landed = transfer(sp, wstreams[self.i], lambda e: e.dma_start(buf[:, :], src), read)
            wring.free(self.i, "held")

        def release(self, step):
            wring.free(self.i, step)

    def project_into(bank, weight, j0, m, rhs, free, *after, nk=KT, start=True, stop=True):
        s = None
        for k in range(nk):
            s = pe(lambda e, k=k: e.matmul(bank, weight.view[:, k, j0:j0 + m], rhs(k),
                                           start=(start and k == 0), stop=(stop and k == nk - 1)),
                   *((free, weight.landed) + after if k == 0 else ()))
        return s

    def project_tokens(bank, lhs, weight, j0, n, free, *after, k0=0, start=True, stop=True):
        s = None
        for k in range(KT):
            s = pe(lambda e, k=k: e.matmul(bank, lhs(k0 + k), weight.view[:, k, j0:j0 + n],
                                           start=(start and k == 0), stop=(stop and k == KT - 1)),
                   *((free, weight.landed) + after if k == 0 else ()))
        return s

    load_cols = transfer(act, Stream(sem("s_cols")), lambda e: e.dma_start(cols[:, :], A["cols"]))
    load_rows = transfer(act, Stream(sem("s_rows")),
                         lambda e: e.dma_start(rows[:, :], A["rows"].to_broadcast([P, NROWS])))
    load_x = transfer(sp, Stream(sem("s_x")), lambda e: e.dma_start(x[:, :, :], A["x"]))

    pool(lambda e: e.memset(ident[:, :], 0.0))
    zeroed = pool(lambda e: e.memset(mask_ij[:, :], 0.0))
    zeroed2 = pool(lambda e: e.memset(mask_ji[:, :], 0.0))
    ident_ready = pool(lambda e: e.affine_select(out=ident[:, :], in_=ident[:, :], compare_op=ALU.not_equal,
                                                 fill=1.0, base=0, pattern=[[-1, P]], channel_multiplier=1),
                       zeroed2)
    a = pool(lambda e: e.affine_select(out=mask_ij[:, :], in_=mask_ij[:, :], compare_op=ALU.is_ge,
                                       fill=MASKED, base=0, pattern=[[-1, P]], channel_multiplier=1), zeroed)
    b = pool(lambda e: e.affine_select(out=mask_ij[:, 0:SEQ], in_=mask_ij[:, 0:SEQ], compare_op=ALU.is_ge,
                                       fill=MASKED, base=SEQ - 1, pattern=[[0, SEQ]], channel_multiplier=-1), a)
    a = pool(lambda e: e.affine_select(out=mask_ji[:, :], in_=mask_ji[:, :], compare_op=ALU.is_ge,
                                       fill=MASKED, base=0, pattern=[[1, P]], channel_multiplier=-1), zeroed2)
    b = pool(lambda e: e.affine_select(out=mask_ji[:, SEQ:P], in_=mask_ji[:, SEQ:P], compare_op=ALU.is_ge,
                                       fill=MASKED, base=-SEQ, pattern=[[0, SEQ]], channel_multiplier=1), a, b)
    masks_ready = b
    upto_ready = dve(lambda e: e.tensor_scalar(upto[:, :], mask_ji[:, :], 0.0, None, ALU.is_equal), masks_ready)

    def inverse_root(dst, src, eps, *after):
        a = dve(lambda e: e.tensor_scalar(dst, src, eps, None, ALU.add), *after)
        a = act(lambda e: e.activation(dst, dst, ACT.Sqrt), a)
        return dve(lambda e: e.reciprocal(dst, dst), a)

    def layer_norm(src, dst, eps, *after):
        stats, mv, rstd = small_buf("stats", NT, 6), small_buf("mv", NT, 2), small_buf("rstd", NT)
        st = [dve(lambda e, i=i: e.bn_stats(stats[:, i, :], src[:, i, :]), *after) for i in range(NT)]
        ag = [dve(lambda e, i=i: e.bn_aggr(mv[:, i, :], stats[:, i, :]), st[i]) for i in range(NT)]
        r = inverse_root(rstd[:, :], mv[:, :, 1], eps, ag[-1])
        return [dve(lambda e, i=i: e.tensor_scalar(dst[:, i, :], src[:, i, :], mv[:, i, 0:1], rstd[:, i:i + 1],
                                                   ALU.subtract, ALU.mult), r) for i in range(NT)]

    def rms_norm(src, dst, gamma, square, *after):
        ssq, rms = small_buf("ssq", NT), small_buf("rms", NT)
        sq = None
        for i in range(NT):
            sq = dve(lambda e, i=i: e.tensor_tensor_reduce(out=square, in0=src[:, i, :], in1=src[:, i, :],
                                                           scale=1.0 / DIM, scalar=0.0, op0=ALU.mult, op1=ALU.add,
                                                           accum_out=ssq[:, i:i + 1]), sq, *after)
        r = inverse_root(rms[:, :], ssq[:, :], EPS_LN, sq)
        return [dve(lambda e, i=i: e.scalar_tensor_tensor(out=dst[:, i, :], in0=src[:, i, :],
                                                          scalar=rms[:, i:i + 1], in1=gamma,
                                                          op0=ALU.mult, op1=ALU.mult), r) for i in range(NT)]

    def to_feature_major(src, dst, ring, written, reader, affine=False):
        last = []
        for k in range(KT):
            bi, bank, free = ring.take()
            for i in range(NT):
                t = pe(lambda e, i=i, k=k, bank=bank: e.transpose(bank[:, i * P:(i + 1) * P],
                                                                  src[:, i, k * P:(k + 1) * P], ident[:, :]),
                       written[i], ident_ready, free if i == 0 else None)
            if affine:
                c = dve(lambda e, k=k, bank=bank: e.tensor_scalar(dst[:, k, :], bank[:, :], col("ln_gamma", k),
                                                                  col("ln_beta", k), ALU.mult, ALU.add),
                        t, load_cols, reader)
            elif k % 2:
                c = act(lambda e, k=k, bank=bank: e.copy(dst[:, k, :], bank[:, :]), t, reader)
            else:
                c = dve(lambda e, k=k, bank=bank: e.tensor_copy(dst[:, k, :], bank[:, :]), t, reader)
            ring.free(bi, c)
            last.append(c)
        return last

    def add_product_to_x(srcT, nk, weights, ring, finish, *after):
        out = []
        for i in range(NT):
            bi, bank, free = ring.take()
            for w, weight in enumerate(weights):
                s = project_tokens(bank[:, :], lambda k, i=i: srcT[:, k, i * P:(i + 1) * P], weight, 0, DIM,
                                   free, *after, k0=w * KT, start=(w == 0), stop=(w == len(weights) - 1))
            f = finish(i, bank, s)
            ring.free(bi, f)
            out.append(f)
        for weight in weights:
            weight.release(s)
        return out

    ctx_streams = [Stream(sem("s_ctx0")), Stream(sem("s_ctx1"))]
    mask_streams = [Stream(sem("s_mask0")), Stream(sem("s_mask1"))]

    def cross_attention(layer, head_dim, scale, w_q, w_k, w_v, q_affine, masked, xnT_ready):
        L = Layout()
        tiles = HEADS * head_dim // P
        nv = HEADS * head_dim // DIM
        qT = L(tiles, TOK)
        kT = [L(tiles, CTX) for _ in range(2)]
        v = [L(CTX // P, tiles * P) for _ in range(2)]
        if layer == 0:
            ctxT = [xnT[:, :, :], L(KT, CTX)]
        else:
            ctxT = [L(KT, CTX) for _ in range(2)]
        qblk = [L(P) for _ in range(2)]
        scores = [L(CTX) for _ in range(2)] if masked else []
        prob = [xn[:, i, :] for i in range(2)]
        probT = [xn[:, i, :].rearrange("p (a b) -> p a b", a=CTX // P) for i in range(2, 4)]
        keep = [L(CTX) for _ in range(2)] if masked else None
        banks_p, banks_s = Ring(banks[0:3]), Ring(banks[3:5])
        banks_t, banks_o = Ring(banks[5:6]), Ring(banks[6:8])

        zero = [pool(lambda e, z=z: e.memset(z, 0.0)) for z in qblk]

        q_done, s = [], None
        for m in range(tiles):
            bi, bank, free = banks_p.take()
            w = w_q[m // 4]
            s = project_into(bank[:, :], w, (m % 4) * P, P, lambda k: xnT[:, k, :], free, *xnT_ready)
            if q_affine:
                c = act(lambda e, m=m, bank=bank: e.activation(qT[:, m, :], bank[:, :], ACT.Identity,
                                                               bias=col("bq", m)), s, load_cols)
            else:
                c = act(lambda e, m=m, bank=bank: e.copy(qT[:, m, :], bank[:, :]), s)
            banks_p.free(bi, c)
            q_done.append(c)
            w.release(s)
        q_projected = s

        def load_context(b, reader):
            t = transfer(sp, ctx_streams[b % 2], lambda e: e.dma_start(ctxT[b % 2], A["ctxT"][b]), reader, *fence)
            mk = None
            if masked:
                raw = keep[b % 2].bitcast(I32)
                mk = transfer(sp, mask_streams[b % 2],
                              lambda e: e.dma_start(raw, A["mask"][b:b + 1, :].to_broadcast([P, CTX])),
                              mask_read[b - 2] if b >= 2 else None, *fence)
            return t, mk

        mask_read, mask_made = {}, {}

        def make_mask(b, landed):
            raw = keep[b % 2].bitcast(I32)
            mask_made[b] = dve(lambda e: e.tensor_scalar(keep[b % 2], raw, 0, MASK_ENERGY, ALU.is_equal, ALU.mult),
                               landed)

        kv_ready = {}

        last_pv = {}

        def kv_groups(b, landed):
            done = []

            def key_group(m):
                bi, bank, free = banks_p.take()
                s = project_into(bank[:, :], w_k[m // 4], (m % 4) * P, P, lambda k: ctxT[b % 2][:, k, :], free,
                                 landed)
                if q_affine:
                    c = act(lambda e: e.activation(kT[b % 2][:, m, :], bank[:, :], ACT.Identity,
                                                   bias=col("bk", m)), s, last_pv.get(b - 2), load_cols)
                else:
                    c = act(lambda e: e.copy(kT[b % 2][:, m, :], bank[:, :]), s, last_pv.get(b - 2))
                banks_p.free(bi, c)
                done.append(c)
                return s

            def value_group(t, n):
                bi, bank, free = banks_p.take()
                s = project_tokens(bank[:, :], lambda k: ctxT[b % 2][:, k, t * P:(t + 1) * P], w_v[n], 0, DIM, free,
                                   landed)
                c = dve(lambda e: e.tensor_copy(v[b % 2][:, t, n * DIM:(n + 1) * DIM], bank[:, :]), s,
                        last_pv.get(b - 2))
                banks_p.free(bi, c)
                done.append(c)
                return s

            kv_ready[b] = done
            todo = [lambda m=m: key_group(m) for m in range(tiles)]
            todo += [lambda t=t, n=n: value_group(t, n) for t in range(CTX // P) for n in range(nv)]
            return todo

        stat = small_buf("xstat", 2, 8)
        per_tile = P // head_dim // 2
        state = {}
        blk_ring, score_ring, prob_ring, probT_ring = Ring(qblk), Ring(scores), Ring(prob), Ring(probT)

        def unit_scores(b, u):
            m, r0 = u // per_tile, (u % per_tile) * 2 * head_dim
            ji, blk, free = blk_ring.take()
            r1 = r0 + head_dim
            c0 = pool(lambda e: e.tensor_copy(blk[r0:r1, 0:SEQ], qT[r0:r1, m, b * SEQ:(b + 1) * SEQ]),
                      q_done[m], free, zero[ji])
            c = pool(lambda e: e.tensor_copy(blk[r1:r1 + head_dim, SEQ:P],
                                             qT[r1:r1 + head_dim, m, b * SEQ:(b + 1) * SEQ]),
                     q_done[m], free, zero[ji], c0)
            si, bank, sfree = banks_s.take()
            ready = kv_ready[b] if u == 0 else ()
            s = pe(lambda e: e.matmul(bank[:, :], blk[r0:r1 + head_dim, :], kT[b % 2][r0:r1 + head_dim, m, :],
                                      start=True, stop=True), c, sfree, *ready)
            blk_ring.free(ji, s)
            st = stat[:, u % 2, :]
            if masked:
                ri, sc, rfree = score_ring.take()
                g = dve(lambda e: e.tensor_tensor_reduce(out=sc, in0=bank[:, :], in1=keep[b % 2], scale=1.0,
                                                         scalar=-3.0e38, op0=ALU.add, op1=ALU.max,
                                                         accum_out=st[:, 0:1]), s, mask_made[b], rfree)
                mask_read[b] = g
                banks_s.free(si, g)
                source = sc
            else:
                g = dve(lambda e: e.reduce_max(st[:, 0:1], bank[:, :], AX_X), s)
                source = bank[:, :]
            n = dve(lambda e: e.tensor_scalar(st[:, 1:2], st[:, 0:1], -scale, None, ALU.mult), g)
            pi, pr, pfree = prob_ring.take()
            ex = act(lambda e: e.activation(pr, source, ACT.Exp, bias=st[:, 1:2], scale=scale,
                                            accum_out=st[:, 2:3]), n, pfree)
            if masked:
                score_ring.free(ri, ex)
            else:
                banks_s.free(si, ex)
            rc = dve(lambda e: e.reciprocal(st[:, 3:4], st[:, 2:3]), ex)
            nm = dve(lambda e: e.tensor_scalar(pr, pr, st[:, 3:4], None, ALU.mult), rc)
            state[b, u] = (pi, pr, nm)

        def unit_transpose(b, u):
            pi, pr, nm = state[b, u]
            ti, bank, free = banks_t.take()
            for t in range(CTX // P):
                s = pe(lambda e, t=t: e.transpose(bank[:, t * P:(t + 1) * P], pr[:, t * P:(t + 1) * P],
                                                  ident[:, :]), nm, free if t == 0 else None)
            prob_ring.free(pi, s)
            qi, pt, tfree = probT_ring.take()
            c = act(lambda e: e.copy(pt, bank[:, :].rearrange("p (a b) -> p a b", a=CTX // P)), s, tfree)
            banks_t.free(ti, c)
            state[b, u] = (qi, pt, c)

        def unit_values(b, u):
            qi, pt, c = state.pop((b, u))
            m, r0 = u // per_tile, (u % per_tile) * 2 * head_dim
            oi, bank, free = banks_o.take()
            rows2 = 2 * head_dim
            for t in range(CTX // P):
                s = pe(lambda e, t=t: e.matmul(bank[r0:r0 + rows2, 0:P], v[b % 2][:, t, u * rows2:(u + 1) * rows2],
                                               pt[:, t, :], start=(t == 0), stop=(t == CTX // P - 1)),
                       c, free if t == 0 else None)
            probT_ring.free(qi, s)
            for h in range(2):
                lo = r0 + h * head_dim
                hi = lo + head_dim
                dst = qT[lo:hi, m, b * SEQ:(b + 1) * SEQ]
                src = bank[lo:hi, h * SEQ:(h + 1) * SEQ]
                if q_affine:
                    o = dve(lambda e, dst=dst, src=src, lo=lo, hi=hi: e.tensor_scalar(
                        dst, src, col("bv", m, 1, lo, hi), None, ALU.add), s, load_cols)
                else:
                    o = dve(lambda e, dst=dst, src=src: e.tensor_copy(dst, src), s)
            banks_o.free(oi, o)
            return s, o

        UNITS = HEADS // 2
        landed, mk = load_context(0, q_projected)
        if masked:
            make_mask(0, mk)
        for g in kv_groups(0, landed):
            kv_ctx_read[0] = g()
        order = [(b, u) for b in range(NSEQ) for u in range(UNITS)]
        todo, last_o = [], None
        for n in range(len(order) + 2):
            b, u = order[n] if n < len(order) else (NSEQ, UNITS)
            if u == 0 and b + 1 < NSEQ:
                landed, mk = load_context(b + 1, kv_ctx_read.get(b - 1))
                if masked:
                    make_mask(b + 1, mk)
                todo = kv_groups(b + 1, landed)
                per_unit = -(-len(todo) // (UNITS - 2))
            groups = min(per_unit, len(todo)) if u >= 2 else 0
            if n < len(order):
                unit_scores(b, u)
            for _ in range(groups // 2):
                kv_ctx_read[b + 1] = todo.pop(0)()
            if 1 <= n <= len(order):
                unit_transpose(*order[n - 1])
            for _ in range(groups - groups // 2):
                kv_ctx_read[b + 1] = todo.pop(0)()
            if 2 <= n:
                last_pv[order[n - 2][0]], last_o = unit_values(*order[n - 2])
        for w in list(w_k) + list(w_v):
            w.release(kv_ctx_read[NSEQ - 1])
        kv_ctx_read.clear()
        return qT, last_o

    kv_ctx_read = {}
    all_banks = Ring(banks)

    def self_attention_inputs(weights, feature_major, token_major, ring, xnT_ready):
        done = {}
        for n, dst in feature_major.items():
            w = weights[n]
            for m in range(KT):
                bi, bank, free = ring.take()
                s = project_into(bank[:, :], w, m * P, P, lambda k: xnT[:, k, :], free, *xnT_ready)
                c = act(lambda e, m=m, bank=bank, dst=dst: e.copy(dst[:, m, :], bank[:, :]), s)
                ring.free(bi, c)
                done[n] = c
            w.release(s)
        for n, dst in token_major.items():
            w = weights[n]
            for i in range(NT):
                bi, bank, free = ring.take()
                s = project_tokens(bank[:, :], lambda k, i=i: xnT[:, k, i * P:(i + 1) * P], w, 0, DIM, free,
                                   *xnT_ready)
                c = dve(lambda e, i=i, bank=bank, dst=dst: e.tensor_copy(dst[:, i, :], bank[:, :]), s)
                ring.free(bi, c)
                done[n] = c
            w.release(s)
        return done

    def broadcast_rows(bank_view, column, *after):
        return pe(lambda e: e.matmul(bank_view, column.to_broadcast([P, P]), ident[:, :], start=True, stop=True),
                  *after)

    def finish_plain(i, bank, s):
        return dve(lambda e: e.tensor_tensor(x[:, i, :], bank[:, :], x[:, i, :], ALU.add), s)

    b2_stream = Stream(sem("s_b2"))

    def route(experts, chosen, weight, bias, srcT, src_ready, ring, gates, gatesT):
        bi, bank, free = ring.take()
        for i in range(NT):
            s = project_tokens(bank[:, i * experts:(i + 1) * experts], lambda k, i=i: srcT[:, k, i * P:(i + 1) * P],
                               weight, 0, experts, free, *src_ready)
        weight.release(s)
        r3 = bank[:, 0:NT * experts].rearrange("p (i x) -> p i x", i=NT)
        aff, top = small_buf(f"aff{experts}", NT, experts), small_buf("top", NT, 8)
        one = small_buf("route1", NT)
        rest = small_buf(f"rest{experts}", NT, experts)
        a = dve(lambda e: e.tensor_tensor(aff, r3, over_middle(bias, NT), ALU.add), s)
        ring.free(bi, a)
        a = dve(lambda e: e.tensor_reduce(one, aff, AX_X, ALU.max), a)
        a = dve(lambda e: e.tensor_tensor(aff, aff, over_last(one, experts), ALU.subtract), a)
        a = act(lambda e: e.activation(aff, aff, ACT.Exp), a)
        a = dve(lambda e: e.tensor_reduce(one, aff, AX_X, ALU.add), a)
        a = dve(lambda e: e.reciprocal(one, one), a)
        a = dve(lambda e: e.tensor_tensor(aff, aff, over_last(one, experts), ALU.mult), a)
        t = [dve(lambda e, i=i: e.max(top[:, i, :], aff[:, i, :]), a) for i in range(NT)]
        a = dve(lambda e: e.memset(top[:, :, chosen:8], -1.0), t[-1])
        t = [dve(lambda e, i=i: e.match_replace(rest[:, i, :], top[:, i, :], aff[:, i, :], 0.0), a)
             for i in range(NT)]
        g_ready = dve(lambda e: e.tensor_tensor(gates, aff, rest, ALU.subtract), t[-1])
        bi, bank, free = ring.take()
        for i in range(NT):
            s = pe(lambda e, i=i, bank=bank: e.transpose(bank[0:experts, i * P:(i + 1) * P], gates[:, i, :],
                                                         ident[:, :]), g_ready, free)
        gt = act(lambda e, bank=bank: e.copy(gatesT[0:experts, :], bank[0:experts, :]), s)
        ring.free(bi, gt)
        return g_ready, gt

    def layer0_cross_attention():
        small_reset()
        w_q = [Weight("L0_xattn_w_q", c) for c in range(2)]
        w_kv = [Weight("L0_xattn_w_kv", c) for c in range(4)]
        w_out = [Weight("L0_xattn_w_out", c) for c in range(2)]
        a = layer_norm(x, xn, EPS_LN, load_x)
        a = layer_norm(xn, xn, EPS_LN, a[-1])
        xnT_ready = to_feature_major(xn, xnT, all_banks, a, None, affine=True)
        oT, o_ready = cross_attention(0, 64, 64 ** -0.5, w_q, w_kv[0:2], w_kv[2:4], False, False,
                                      xnT_ready)
        tanh_gate = small_buf("tanh_gate", 1)
        tg = act(lambda e: e.activation(tanh_gate[:, :], row("gate"), ACT.Tanh), load_rows)

        def finish_gated(i, bank, s):
            a = dve(lambda e: e.tensor_tensor(xn[:, i, :], bank[:, :], row("b_out"), ALU.add), s, load_rows)
            return dve(lambda e: e.scalar_tensor_tensor(out=x[:, i, :], in0=xn[:, i, :], scalar=tanh_gate[:, 0:1],
                                                        in1=x[:, i, :], op0=ALU.mult, op1=ALU.add), a, tg)

        x_ready = add_product_to_x(oT, 8, w_out, Ring(banks[0:3]), finish_gated, o_ready)
        stage_end()
        return x_ready

    def layer0_linear_attention(x_ready):
        small_reset()
        W = {n: Weight("L0_attn_" + n, 0) for n in ("Wk", "Wq", "Wv", "Wo")}
        a = layer_norm(x, xn, EPS_LN, *x_ready)
        ring = Ring(banks)
        xnT_ready = to_feature_major(xn, xnT, ring, a, None)
        L = Layout()
        qT, vT, k_tok, yT = L(KT, TOK), L(KT, TOK), L(NT, DIM), L(KT, TOK)
        ksq = L(NT, DIM)
        done = self_attention_inputs(W, {}, {"Wk": k_tok}, ring, xnT_ready)
        G = NT * HEADS
        g = {n: small_buf("g_" + n, G) for n in ("n2", "rn", "sum", "kbar", "zg", "zl", "log", "one_rho", "L", "tmp")}

        def by_head(buf):
            return buf[:, :, :].rearrange("p i (h d) -> p (i h) d", h=HEADS)

        a = pool(lambda e: e.tensor_tensor(ksq[:, :, :], k_tok[:, :, :], k_tok[:, :, :], ALU.mult), done["Wk"])
        a = dve(lambda e: e.tensor_reduce(g["n2"][:, :], by_head(ksq), AX_X, ALU.add), a)
        a = act(lambda e: e.activation(g["rn"][:, :], g["n2"][:, :], ACT.Sqrt), a)
        a = dve(lambda e: e.tensor_scalar(g["rn"][:, :], g["rn"][:, :], 1e-12, None, ALU.max), a)
        a = dve(lambda e: e.reciprocal(g["rn"][:, :], g["rn"][:, :]), a)
        k_ready = dve(lambda e: e.tensor_tensor(by_head(k_tok), by_head(k_tok), over_last(g["rn"], 32), ALU.mult), a)
        a = dve(lambda e: e.tensor_reduce(g["sum"][:, :], by_head(k_tok), AX_X, ALU.add), k_ready)
        done = self_attention_inputs(W, {"Wq": qT, "Wv": vT}, {}, ring, xnT_ready)

        def gate_logit(dst, w, b, a):
            d3 = dst[:, :].rearrange("p (i h) -> p i h", i=NT)
            s3 = g["sum"][:, :].rearrange("p (i h) -> p i h", i=NT)
            a = dve(lambda e: e.tensor_tensor(d3, s3, over_middle(row(w), NT), ALU.mult), a, load_rows)
            return dve(lambda e: e.scalar_tensor_tensor(out=d3, in0=d3, scalar=1.0 / 32, in1=over_middle(row(b), NT),
                                                        op0=ALU.mult, op1=ALU.add), a)

        b = gate_logit(g["zg"], "W_gamma", "b_gamma", a)
        a = gate_logit(g["zl"], "W_lambda", "b_lambda", a)
        a = act(lambda e: e.activation(g["zl"][:, :], g["zl"][:, :], ACT.Exp), a)
        b = act(lambda e: e.activation(g["zg"][:, :], g["zg"][:, :], ACT.Exp, scale=-1.0), b)
        a = dve(lambda e: e.tensor_scalar(g["zl"][:, :], g["zl"][:, :], 1.0, None, ALU.add), a)
        b = dve(lambda e: e.tensor_scalar(g["zg"][:, :], g["zg"][:, :], 1.0, None, ALU.add), b)
        a = dve(lambda e: e.tensor_tensor(g["tmp"][:, :], g["zl"][:, :], g["zg"][:, :], ALU.mult), a, b)
        b = dve(lambda e: e.reciprocal(g["one_rho"][:, :], g["tmp"][:, :]), a)
        b = dve(lambda e: e.tensor_scalar(g["one_rho"][:, :], g["one_rho"][:, :], -1.0, 1.0, ALU.mult, ALU.add), b)
        a = act(lambda e: e.activation(g["log"][:, :], g["tmp"][:, :], ACT.Ln), a)
        bi, bank, free = ring.take()
        s = pe(lambda e, bank=bank: e.matmul(bank[:, 0:G], upto[:, :], g["log"][:, :], start=True, stop=True), a, free,
               upto_ready)
        Lc = dve(lambda e, bank=bank: e.tensor_copy(g["L"][:, :], bank[:, 0:G]), s)
        ring.free(bi, Lc)

        ring_a, ring_l, ring_y = Ring(banks[0:3]), Ring(banks[3:6]), Ring(banks[6:8])
        decay_ring = Ring([L(KT, P) for _ in range(3)])
        mask_b = over_middle(mask_ji[:, :], KT)
        for i in range(NT):
            for j in range(4):
                r = 32 * j
                heads = slice(i * HEADS + j, (i + 1) * HEADS, 4)
                li, lbank, lfree = ring_l.take()
                for hm in range(KT):
                    c = i * HEADS + 4 * hm + j
                    s = broadcast_rows(lbank[:, hm * P:(hm + 1) * P], g["L"][:, c:c + 1], Lc, lfree)
                ai, abank, afree = ring_a.take()
                for hm in range(KT):
                    s2 = pe(lambda e, hm=hm, abank=abank, r=r, i=i: e.matmul(
                        abank[:, hm * P:(hm + 1) * P], vT[r:r + 32, hm, i * P:(i + 1) * P],
                        qT[r:r + 32, hm, i * P:(i + 1) * P], start=True, stop=True),
                            afree, done["Wq"], done["Wv"])
                l3 = lbank[:, :].rearrange("p (a b) -> p a b", a=KT)
                a3 = abank[:, :].rearrange("p (a b) -> p a b", a=KT)
                di, dec, dfree = decay_ring.take()
                a = dve(lambda e, dec=dec, l3=l3: e.scalar_tensor_tensor(out=dec, in0=l3, scalar=-1.0, in1=mask_b,
                                                                         op0=ALU.mult, op1=ALU.add), s, dfree,
                        masks_ready)
                ring_l.free(li, a)
                a = pool(lambda e, dec=dec, heads=heads: e.tensor_tensor(dec, dec, over_last(g["L"][:, heads], P),
                                                                        ALU.add), a, Lc)
                a = act(lambda e, dec=dec: e.activation(dec, dec, ACT.Exp), a)
                a = pool(lambda e, dec=dec, heads=heads: e.tensor_tensor(dec, dec, over_last(g["one_rho"][:, heads], P),
                                                                        ALU.mult), a, b)
                a = dve(lambda e, dec=dec, a3=a3: e.tensor_tensor(dec, a3, dec, ALU.mult), a, s2)
                ring_a.free(ai, a)
                yi, ybank, yfree = ring_y.take()
                for hm in range(KT):
                    h = 4 * hm + j
                    s = pe(lambda e, hm=hm, h=h, ybank=ybank, dec=dec, r=r, i=i: e.matmul(
                        ybank[r:r + 32, hm * P:(hm + 1) * P], k_tok[:, i, 32 * h:32 * h + 32], dec[:, hm, :],
                        start=True, stop=True), a, k_ready, yfree)
                decay_ring.free(di, s)
                y_ready = act(lambda e, ybank=ybank, r=r, i=i: e.copy(
                    yT[r:r + 32, :, i * P:(i + 1) * P],
                    ybank[r:r + 32, :].rearrange("p (a b) -> p a b", a=KT)), s)
                ring_y.free(yi, y_ready)

        stage_end()
        x_ready = add_product_to_x(yT, 4, [W["Wo"]], Ring(banks), finish_plain, y_ready)
        stage_end()
        return x_ready

    def layer0_self_attention(x_ready):
        small_reset()
        W = {n: Weight("L0_ffn_" + n, 0) for n in ("q1", "q2", "k1", "k2")}
        W_v = [Weight("L0_ffn_v", c) for c in range(2)]
        W_o = [Weight("L0_ffn_o", c) for c in range(2)]
        L = Layout()
        attn_out = xn
        q1, q2, k1, k2 = (L(KT, TOK) for _ in range(4))
        v_tok = L(NT, 2 * DIM)
        cos, sin, ang = L(SEQ), L(SEQ), L(SEQ)
        square = L(DIM)
        rope_ring = Ring([[L(DIM) for _ in range(4)]])
        soft_ring = Ring([L(KT, P) for _ in range(2)])
        probT_ring = Ring([L(KT, P) for _ in range(2)])
        pos = L(SEQ)
        a = pool(lambda e: e.iota(ang.bitcast(I32), pattern=[[1, SEQ]], base=0, channel_multiplier=0))
        a = dve(lambda e: e.tensor_copy(pos, ang.bitcast(I32)), a)
        ang_done = dve(lambda e: e.tensor_scalar(ang, pos, col("theta"), None, ALU.mult), a, load_cols)
        PI = float(np.pi)
        ROUND = 1.5 * 2.0 ** 23
        C1 = float(np.float32(6.28125))
        C2 = float(np.frombuffer((np.frombuffer(np.float32(2 * np.pi - C1).tobytes(), np.uint32)
                                  & np.uint32(0xFFFFF000)).tobytes(), np.float32)[0])
        C3 = float(np.float32(2 * np.pi - C1 - C2))
        turns = L(SEQ)

        def sine(dst, shift, a):
            a = dve(lambda e: e.tensor_scalar(turns, ang, 1.0 / (2 * PI), shift / (2 * PI), ALU.mult, ALU.add), a)
            a = dve(lambda e: e.tensor_scalar(turns, turns, ROUND, None, ALU.add), a)
            a = dve(lambda e: e.tensor_scalar(turns, turns, -ROUND, None, ALU.add), a)
            src = ang
            for c in (C1, C2, C3):
                a = dve(lambda e, c=c, src=src: e.scalar_tensor_tensor(out=dst, in0=turns, scalar=-c, in1=src,
                                                                       op0=ALU.mult, op1=ALU.add), a)
                src = dst
            if shift:
                a = dve(lambda e: e.tensor_scalar(dst, dst, shift, None, ALU.add), a)
            a = dve(lambda e: e.tensor_scalar(dst, dst, PI, -PI, ALU.min, ALU.max), a)
            return act(lambda e: e.activation(dst, dst, ACT.Sin), a), a

        sin_ready, a = sine(sin, 0.0, ang_done)
        cos_ready, a = sine(cos, PI / 2, a)

        a = layer_norm(x, xn, EPS_LN, *x_ready)
        a = rms_norm(xn, xn, row("gamma1"), square, a[-1], load_rows)
        ring = Ring(banks)
        xnT_ready = to_feature_major(xn, xnT, ring, a, None)

        rope_cos, rope_sin = over_middle(cos, NSEQ), over_middle(sin, NSEQ)

        def by_seq(ap):
            return ap.rearrange("p (b s) -> p b s", b=NSEQ)

        for wa, wb, o1, o2, ba, bb in (("q1", "q2", q1, q2, "q_b1", "q_b2"), ("k1", "k2", k1, k2, "k_b1", "k_b2")):
            for m in range(KT):
                ai, abank, free = ring.take()
                s1 = project_into(abank[:, :], W[wa], m * P, P, lambda k: xnT[:, k, :], free, *xnT_ready)
                bi, bbank, free = ring.take()
                s2 = project_into(bbank[:, :], W[wb], m * P, P, lambda k: xnT[:, k, :], free, *xnT_ready)
                W[wa].release(s1)
                W[wb].release(s2)
                ri, (ta, tb, tc, td), rfree = rope_ring.take()
                e1 = act(lambda e, m=m, abank=abank, ta=ta, ba=ba: e.activation(ta, abank[:, :], ACT.Identity,
                                                                                bias=col(ba, m)), s1, rfree, load_cols)
                e2 = act(lambda e, m=m, bbank=bbank, tb=tb, bb=bb: e.activation(tb, bbank[:, :], ACT.Identity,
                                                                                bias=col(bb, m)), s2)
                ring.free(ai, e1)
                ring.free(bi, e2)
                c1 = dve(lambda e, m=m, o1=o1, ta=ta: e.tensor_tensor(by_seq(o1[:, m, :]), by_seq(ta), rope_cos,
                                                                      ALU.mult), e1, cos_ready)
                c2 = pool(lambda e, tb=tb, tc=tc: e.tensor_tensor(by_seq(tc), by_seq(tb), rope_sin, ALU.mult), e2,
                          sin_ready, rfree)
                c3 = dve(lambda e, m=m, o2=o2, ta=ta: e.tensor_tensor(by_seq(o2[:, m, :]), by_seq(ta), rope_sin,
                                                                      ALU.mult), e1, sin_ready)
                c4 = pool(lambda e, tb=tb, td=td: e.tensor_tensor(by_seq(td), by_seq(tb), rope_cos, ALU.mult), e2,
                          cos_ready)
                c5 = dve(lambda e, m=m, o1=o1, tc=tc: e.tensor_tensor(o1[:, m, :], o1[:, m, :], tc, ALU.subtract), c1,
                         c2)
                qk_ready = dve(lambda e, m=m, o2=o2, td=td: e.tensor_tensor(o2[:, m, :], o2[:, m, :], td, ALU.add), c3,
                               c4)
                rope_ring.free(ri, qk_ready)
        for i in range(NT):
            for n in range(2):
                bi, bank, free = ring.take()
                s = project_tokens(bank[:, :], lambda k, i=i: xnT[:, k, i * P:(i + 1) * P], W_v[n], 0, DIM, free,
                                   *xnT_ready)
                v_ready = act(lambda e, i=i, n=n, bank=bank: e.copy(v_tok[:, i, n * DIM:(n + 1) * DIM], bank[:, :]), s)
                ring.free(bi, v_ready)
                W_v[n].release(s)
        stage_end()
        oT = L(8, TOK)
        mx, sm = small_buf("mx", 2, 4), small_buf("sm", 2, 4)
        ring_s, ring_t, ring_o = Ring(banks[0:3]), Ring(banks[3:5]), Ring(banks[5:8])
        mask_q = over_middle(mask_ij[:, :], KT)
        pending = []

        def attend(i, j, pi, pr, done):
            ti, tbank, tfree = ring_t.take()
            for hm in range(KT):
                s = pe(lambda e, hm=hm: e.transpose(tbank[:, hm * P:(hm + 1) * P], pr[:, hm, :], ident[:, :]), done,
                       tfree)
            soft_ring.free(pi, s)
            qi, pt, qfree = probT_ring.take()
            c = act(lambda e: e.copy(pt, tbank[:, :].rearrange("p (a b) -> p a b", a=KT)), s, qfree)
            ring_t.free(ti, c)
            oi, obank, ofree = ring_o.take()
            r = (j % 2) * 64
            for hm in range(KT):
                h = 4 * hm + j
                s = pe(lambda e, hm=hm, h=h: e.matmul(obank[r:r + 64, hm * P:(hm + 1) * P],
                                                      v_tok[:, i, 64 * h:64 * h + 64], pt[:, hm, :],
                                                      start=True, stop=True), c, ofree, v_ready)
            probT_ring.free(qi, s)
            o3 = oT[r:r + 64, j // 2::2, i * P:(i + 1) * P]
            vb = cols[r:r + 64, COLS["v_b"][0] + j // 2:COLS["v_b"][0] + 8:2]
            o = dve(lambda e: e.tensor_tensor(o3, obank[r:r + 64, :].rearrange("p (a b) -> p a b", a=KT),
                                              over_last(vb, P), ALU.add), s)
            ring_o.free(oi, o)
            return o

        for i in range(NT):
            for j in range(4):
                r = 32 * j
                si, sbank, sfree = ring_s.take()
                for hm in range(KT):
                    for half, (qq, kk) in enumerate(((q1, k1), (q2, k2))):
                        s = pe(lambda e, hm=hm, qq=qq, kk=kk, half=half, sbank=sbank, r=r, i=i: e.matmul(
                            sbank[:, hm * P:(hm + 1) * P], qq[r:r + 32, hm, i * P:(i + 1) * P],
                            kk[r:r + 32, hm, i * P:(i + 1) * P], start=(half == 0), stop=(half == 1)),
                               sfree, qk_ready)
                pi, pr, pfree = soft_ring.take()
                s3 = sbank[:, :].rearrange("p (a b) -> p a b", a=KT)
                u = (i * 4 + j) % 2
                a = dve(lambda e, pr=pr, s3=s3: e.tensor_tensor(pr, s3, mask_q, ALU.add), s, pfree)
                ring_s.free(si, a)
                a = dve(lambda e, pr=pr, u=u: e.tensor_reduce(mx[:, u, :], pr, AX_X, ALU.max), a)
                a = pool(lambda e, pr=pr, u=u: e.tensor_tensor(pr, pr, over_last(mx[:, u, :], P), ALU.subtract), a)
                a = act(lambda e, pr=pr: e.activation(pr, pr, ACT.Exp, scale=64 ** -0.5), a)
                a = dve(lambda e, pr=pr, u=u: e.tensor_reduce(sm[:, u, :], pr, AX_X, ALU.add), a)
                a = dve(lambda e, u=u: e.reciprocal(sm[:, u, :], sm[:, u, :]), a)
                a = pool(lambda e, pr=pr, u=u: e.tensor_tensor(pr, pr, over_last(sm[:, u, :], P), ALU.mult), a)
                if pending:
                    o_ready = attend(*pending.pop())
                pending.append((i, j, pi, pr, a))
        o_ready = attend(*pending.pop())

        def finish_attention(i, bank, s):
            a = dve(lambda e: e.tensor_tensor(attn_out[:, i, :], bank[:, :], xn[:, i, :], ALU.add), s)
            return dve(lambda e: e.tensor_tensor(attn_out[:, i, :], attn_out[:, i, :], row("o_b"), ALU.add), a)

        ao_ready = add_product_to_x(oT, 8, W_o, Ring(banks[0:3]), finish_attention, o_ready)
        stage_end()
        return x_ready, ao_ready

    def layer0_experts(x_ready, ao_ready):
        small_reset()
        W_sh = [Weight("L0_ffn_sh_w1", 0), Weight("L0_ffn_sh_w2", 0)]
        router_w = Weight("router_w", 0)
        L = Layout()
        attn_out, an, anT = xn, L(NT, DIM), xnT
        hid = [L(KT, TOK) for _ in range(2)]
        square = L(DIM)
        an_ready = rms_norm(attn_out, an, row("gamma2"), square, *ao_ready)
        ring = Ring(banks)
        anT_ready = to_feature_major(an, anT, ring, an_ready, None)
        for i in range(NT):
            a = pool(lambda e, i=i: e.tensor_tensor(attn_out[:, i, :], attn_out[:, i, :], an[:, i, :], ALU.add),
                     an_ready[i])
            a = pool(lambda e, i=i: e.tensor_tensor(x[:, i, :], attn_out[:, i, :], x[:, i, :], ALU.add), a)
            x_ready = pool(lambda e, i=i: e.tensor_tensor(x[:, i, :], x[:, i, :], row("sh_b2"), ALU.add), a)

        gates = small_buf("gates", NT, E0)
        gatesT = L(TOK)

        g_ready, gt_ready = route(E0, TOP0, router_w, row("router_b"), anT, anT_ready, ring, gates, gatesT)
        b2 = L(DIM)
        b2_landed = transfer(sp, b2_stream, lambda e: e.dma_start(b2[0:E0, :], A["L0_ffn_re_b2"]), *fence)
        for i in range(NT):
            bi, bank, free = ring.take()
            s = pe(lambda e, i=i, bank=bank: e.matmul(bank[:, :], gatesT[0:E0, i * P:(i + 1) * P], b2[0:E0, :],
                                                      start=True, stop=True), gt_ready, b2_landed, free)
            x_ready = dve(lambda e, i=i, bank=bank: e.tensor_tensor(x[:, i, :], bank[:, :], x[:, i, :], ALU.add), s,
                          x_ready)
            ring.free(bi, x_ready)

        up_ring, down_ring, hid_ring = Ring(banks[0:4]), Ring(banks[4:8]), Ring(hid)
        pend = None

        def down0(hi, h, h_ready, w2, gate):
            for i in range(NT):
                bi, bank, free = down_ring.take()
                s = project_tokens(bank[:, :], lambda k, i=i: h[:, k, i * P:(i + 1) * P], w2, 0, DIM, free, *h_ready)
                if gate is None:
                    c = dve(lambda e, i=i, bank=bank: e.tensor_tensor(x[:, i, :], bank[:, :], x[:, i, :], ALU.add), s)
                else:
                    c = dve(lambda e, i=i, bank=bank: e.scalar_tensor_tensor(
                        out=x[:, i, :], in0=bank[:, :], scalar=gates[:, i, gate:gate + 1], in1=x[:, i, :],
                        op0=ALU.mult, op1=ALU.add), s)
                down_ring.free(bi, c)
            w2.release(s)
            hid_ring.free(hi, s)
            return c

        stage_end()
        for ex in range(-1, E0):
            if ex < 0:
                w1, w2, bias, gate = W_sh[0], W_sh[1], ("sh_b1", 0), None
            else:
                w1, w2 = Weight("L0_ffn_re_w1", ex), Weight("L0_ffn_re_w2", ex)
                bias, gate = ("re_b1", 4 * ex), ex
            hi, h, hfree = hid_ring.take()
            h_ready = []
            for m in range(KT):
                bi, bank, free = up_ring.take()
                s = project_into(bank[:, :], w1, m * P, P, lambda k: anT[:, k, :], free)
                c = act(lambda e, m=m, bank=bank, h=h, bias=bias: e.activation(h[:, m, :], bank[:, :], ACT.Gelu,
                                                                              bias=col(bias[0], bias[1] + m)),
                        s, hfree)
                up_ring.free(bi, c)
                h_ready.append(c)
            w1.release(s)
            if pend:
                down0(*pend)
            pend = (hi, h, h_ready, w2, gate)
        x_ready = down0(*pend)
        stage_end()
        return [x_ready]

    def layer1_cross_attention(x_ready):
        small_reset()
        X = {n: Weight("L1_xattn_" + n, 0) for n in ("Wq", "Wk", "Wv", "Wo")}
        a = layer_norm(x, xn, EPS_LN)
        xnT_ready = to_feature_major(xn, xnT, Ring(banks), a, None)
        oT, o_ready = cross_attention(1, 32, 32 ** -0.5, [X["Wq"]], [X["Wk"]], [X["Wv"]], True, True,
                                      xnT_ready)

        def finish_bias(i, bank, s):
            a = dve(lambda e: e.tensor_tensor(xn[:, i, :], bank[:, :], row("bo"), ALU.add), s)
            return dve(lambda e: e.tensor_tensor(x[:, i, :], xn[:, i, :], x[:, i, :], ALU.add), a)

        x_ready = add_product_to_x(oT, 4, [X["Wo"]], Ring(banks[0:3]), finish_bias, o_ready)
        stage_end()
        return x_ready

    def layer1_lstm(x_ready):
        small_reset()
        W = {n: Weight("L1_attn_" + n, 0) for n in ("Wq", "Wk", "Wv", "Wo", "Wifg", "Wdown")}
        L = Layout()
        qT, kT, v_tok, o_tok, h_tok = L(4, TOK), L(4, TOK), L(NT, DIM), L(NT, DIM), L(NT, DIM)
        a = layer_norm(x, xn, EPS_LN, *x_ready)
        ring = Ring(banks)
        xnT_ready = to_feature_major(xn, xnT, ring, a, None)
        NH, CAP = 4, 15.0
        ifg = small_buf("ifg", NT, 8)
        bi, bank, free = ring.take()
        for i in range(NT):
            s = project_tokens(bank[:, i * 8:(i + 1) * 8], lambda k, i=i: xnT[:, k, i * P:(i + 1) * P], W["Wifg"], 0, 8,
                               free, *xnT_ready)
        W["Wifg"].release(s)
        b3 = bank[:, 0:8 * NT].rearrange("p (i x) -> p i x", i=NT)
        a = dve(lambda e: e.tensor_tensor(ifg, b3, over_middle(row("b_ifg"), NT), ALU.add), s)
        ring.free(bi, a)
        a = act(lambda e: e.activation(ifg, ifg, ACT.Tanh, scale=1.0 / CAP), a)
        ifg_ready = dve(lambda e: e.tensor_scalar(ifg, ifg, CAP, None, ALU.mult), a)
        lsf = small_buf("lsf", NT, NH)
        a = act(lambda e: e.activation(lsf, ifg[:, :, 4:8], ACT.Exp, scale=-1.0), ifg_ready)
        a = dve(lambda e: e.tensor_scalar(lsf, lsf, 1.0, None, ALU.add), a)
        a = act(lambda e: e.activation(lsf, lsf, ACT.Ln), a)
        bi, bank, free = ring.take()
        s = pe(lambda e, bank=bank: e.matmul(bank[:, 0:NT * NH], upto[:, :], lsf.rearrange("p i h -> p (i h)"),
                                             start=True, stop=True), a, free)
        nlf, gj = small_buf("nlf", NT, NH), small_buf("gj", NT, NH)
        nlf_ready = dve(lambda e, bank=bank: e.tensor_copy(nlf.rearrange("p i h -> p (i h)"), bank[:, 0:NT * NH]), s)
        ring.free(bi, nlf_ready)
        gj_ready = dve(lambda e: e.tensor_tensor(gj, ifg[:, :, 0:4], nlf, ALU.add), nlf_ready)
        done = self_attention_inputs(W, {"Wq": qT, "Wk": kT}, {"Wv": v_tok}, ring, xnT_ready)
        for i in range(NT):
            bi, bank, free = ring.take()
            s = project_tokens(bank[:, :], lambda k, i=i: xnT[:, k, i * P:(i + 1) * P], W["Wo"], 0, DIM, free)
            o_done = act(lambda e, i=i, bank=bank: e.activation(o_tok[:, i, :], bank[:, :], ACT.Sigmoid), s)
            ring.free(bi, o_done)
        W["Wo"].release(s)
        stage_end()
        D_ring, C_ring, CT_ring = (Ring([L(P) for _ in range(2)]) for _ in range(3))
        ring_g, ring_s, ring_t, ring_h = Ring(banks[0:2]), Ring(banks[2:4]), Ring(banks[4:6]), Ring(banks[6:8])
        NSTAT = 12
        mst = small_buf("mst", NT * NH, NSTAT)
        head_mv, head_rstd = small_buf("head_mv", NT * NH, 2), small_buf("head_rstd", NT * NH)
        for i in range(NT):
            for h in range(NH):
                st = mst[:, i * NH + h, :]

                def c1(n, st=st):
                    return st[:, n:n + 1]

                gi, gbank, gfree = ring_g.take()
                s = broadcast_rows(gbank[:, 0:P], gj[:, i, h:h + 1], gj_ready, gfree)
                si, sbank, sfree = ring_s.take()
                s2 = pe(lambda e, i=i, h=h, sbank=sbank: e.matmul(sbank[:, 0:P], qT[:, h, i * P:(i + 1) * P],
                                                                  kT[:, h, i * P:(i + 1) * P], start=True, stop=True),
                        sfree, done["Wq"], done["Wk"])
                di, D, dfree = D_ring.take()
                a = dve(lambda e, D=D, gbank=gbank, c1=c1: e.tensor_tensor_reduce(
                    out=D, in0=gbank[:, 0:P], in1=mask_ij[:, :], scale=1.0, scalar=-3.0e38, op0=ALU.add, op1=ALU.max,
                    accum_out=c1(0)), s, dfree)
                ring_g.free(gi, a)
                a = dve(lambda e, c1=c1: e.tensor_scalar(c1(1), c1(0), -1.0, None, ALU.mult), a)
                d = act(lambda e, D=D, c1=c1: e.activation(D, D, ACT.Exp, bias=c1(1)), a)
                a = dve(lambda e, i=i, h=h, c1=c1: e.tensor_tensor(c1(2), c1(1), nlf[:, i, h:h + 1], ALU.add), a)
                m = act(lambda e, c1=c1: e.activation(c1(2), c1(2), ACT.Exp), a)
                ci, C, cfree = C_ring.take()
                a = dve(lambda e, C=C, D=D, sbank=sbank, c1=c1: e.tensor_tensor_reduce(
                    out=C, in0=sbank[:, 0:P], in1=D, scale=128 ** -0.5, scalar=0.0, op0=ALU.mult, op1=ALU.add,
                    accum_out=c1(3)), d, s2, cfree)
                c_ready = a
                D_ring.free(di, a)
                ring_s.free(si, a)
                a = dve(lambda e, c1=c1: e.scalar_tensor_tensor(
                    out=c1(4), in0=c1(3), scalar=-1.0, in1=c1(3), op0=ALU.mult, op1=ALU.max), a)
                a = dve(lambda e, c1=c1: e.tensor_tensor(c1(4), c1(4), c1(2), ALU.max), a, m)
                a = dve(lambda e, c1=c1: e.tensor_scalar(c1(4), c1(4), 1e-6, None, ALU.add), a)
                rn = dve(lambda e, c1=c1: e.reciprocal(c1(5), c1(4)), a)
                ti, tbank, tfree = ring_t.take()
                s = pe(lambda e, C=C, tbank=tbank: e.transpose(tbank[:, 0:P], C, ident[:, :]), c_ready, tfree)
                C_ring.free(ci, s)
                ui, CT, ufree = CT_ring.take()
                c = act(lambda e, CT=CT, tbank=tbank: e.copy(CT, tbank[:, 0:P]), s, ufree)
                ring_t.free(ti, c)
                hi, hbank, hfree = ring_h.take()
                s = pe(lambda e, i=i, h=h, CT=CT, hbank=hbank: e.matmul(hbank[:, 0:P], CT, v_tok[:, i, h * P:(h + 1) * P],
                                                                       start=True, stop=True), c, hfree, done["Wv"])
                CT_ring.free(ui, s)
                hv = h_tok[:, i, h * P:(h + 1) * P]
                a = dve(lambda e, hv=hv, hbank=hbank, c1=c1: e.tensor_scalar(hv, hbank[:, 0:P], c1(5), None, ALU.mult),
                        s, rn)
                ring_h.free(hi, a)
                a = dve(lambda e, hv=hv, st=st: e.bn_stats(st[:, 6:12], hv), a)
                h_stats = dve(lambda e, i=i, h=h, st=st: e.bn_aggr(head_mv[:, i * NH + h, :], st[:, 6:12]), a)
        r = inverse_root(head_rstd[:, :], head_mv[:, :, 1], 1e-6, h_stats)
        ho_ready = []
        for i in range(NT):
            for h in range(NH):
                hv, n = h_tok[:, i, h * P:(h + 1) * P], i * NH + h
                a = dve(lambda e, hv=hv, n=n: e.tensor_scalar(hv, hv, head_mv[:, n, 0:1], head_rstd[:, n:n + 1],
                                                              ALU.subtract, ALU.mult), r)
            a = pool(lambda e, i=i: e.tensor_tensor(h_tok[:, i, :], h_tok[:, i, :], row("norm_w"), ALU.mult), a)
            a = pool(lambda e, i=i: e.tensor_tensor(h_tok[:, i, :], h_tok[:, i, :], o_tok[:, i, :], ALU.mult), a)
            ho_ready.append(a)
        hT = L(4, TOK)
        hT_ready = to_feature_major(h_tok, hT, Ring(banks[0:2]), ho_ready, None)
        stage_end()
        x_ready = add_product_to_x(hT, 4, [W["Wdown"]], Ring(banks), finish_plain)
        stage_end()
        return x_ready

    def layer1_experts(x_ready):
        small_reset()
        gate_w = Weight("gate_w", 0)
        L = Layout()
        a = layer_norm(x, xn, EPS_LN)
        ring = Ring(banks)
        xnT_ready = to_feature_major(xn, xnT, ring, a, None)
        gates1 = small_buf("gates1", NT, E1)
        gatesT = L(TOK)
        g_ready, gt_ready = route(E1, TOP1, gate_w, row("gate_b"), xnT, xnT_ready, ring, gates1, gatesT)
        b2 = L(DIM)
        b2_landed = transfer(sp, b2_stream, lambda e: e.dma_start(b2[0:E1, :], A["L1_ffn_b2"]), *fence)
        for i in range(NT):
            bi, bank, free = ring.take()
            s = pe(lambda e, i=i, bank=bank: e.matmul(bank[:, :], gatesT[0:E1, i * P:(i + 1) * P], b2[0:E1, :],
                                                      start=True, stop=True), gt_ready, b2_landed, free)
            c = dve(lambda e, i=i, bank=bank: e.tensor_tensor(x[:, i, :], bank[:, :], x[:, i, :], ALU.add), s)
            ring.free(bi, c)
            x_ready = dve(lambda e, i=i: e.tensor_tensor(x[:, i, :], x[:, i, :], row("sb2"), ALU.add), c)
        stage_end()
        up_ring, down_ring = Ring(banks[0:4]), Ring(banks[4:8])
        NHID = 16
        hid_ring = Ring([L(TOK) for _ in range(NHID)])
        silu_ring = Ring([L(TOK) for _ in range(3)])

        def hidden_tile(w1, w3, j, b1, b3):
            ai, abank, afree = up_ring.take()
            s1 = project_into(abank[:, :], w1, j * P, P, lambda k: xnT[:, k, :], afree)
            bi, bbank, bfree = up_ring.take()
            s2 = project_into(bbank[:, :], w3, j * P, P, lambda k: xnT[:, k, :], bfree)
            ti, tmp, tfree = silu_ring.take()
            c1 = act(lambda e: e.activation(tmp, abank[:, :], ACT.Silu, bias=b1), s1, tfree)
            up_ring.free(ai, c1)
            hi, h, hfree = hid_ring.take()
            c2 = dve(lambda e: e.scalar_tensor_tensor(out=h, in0=bbank[:, :], scalar=b3, in1=tmp, op0=ALU.add,
                                                      op1=ALU.mult), s2, c1, hfree)
            up_ring.free(bi, c2)
            silu_ring.free(ti, c2)
            return hi, h, c2, s2

        uses = {}

        def down1(parts, gate):
            for i in range(NT):
                bi, bank, free = down_ring.take()
                for n, (hi, h, ready, w2, j, lo, up) in enumerate(parts):
                    s = pe(lambda e, n=n, h=h, w2=w2, j=j, lo=lo, up=up, i=i, bank=bank: e.matmul(
                        bank[:, :], h[lo:up, i * P:(i + 1) * P], w2.view[lo:up, j, :],
                        start=(n == 0), stop=(n == len(parts) - 1)), free, ready, w2.landed)
                    if i == NT - 1:
                        hid_ring.free(hi, s)
                        uses[w2] -= 1
                        if not uses[w2]:
                            w2.release(s)
                if gate is None:
                    c = dve(lambda e, i=i, bank=bank: e.tensor_tensor(x[:, i, :], bank[:, :], x[:, i, :], ALU.add), s)
                else:
                    c = dve(lambda e, i=i, bank=bank: e.scalar_tensor_tensor(
                        out=x[:, i, :], in0=bank[:, :], scalar=gates1[:, i, gate:gate + 1], in1=x[:, i, :],
                        op0=ALU.mult, op1=ALU.add), s)
                down_ring.free(bi, c)
            return c

        pend = None
        for gidx in range(3):
            w1, w3, w2 = (Weight("L1_ffn_" + n, gidx) for n in ("sw1", "sw3", "sw2"))
            uses[w2] = 4 if gidx < 2 else 3
            parts = []
            for j in range(4 if gidx < 2 else 3):
                t = 4 * gidx + j
                hi, h, ready, s = hidden_tile(w1, w3, j, col("sb1", t), col("sb3", t))
                parts.append((hi, h, ready, w2, j, 0, P))
            w1.release(s)
            w3.release(s)
            if pend:
                down1(*pend)
            pend = (parts, None)
        down1(*pend)
        pend = None
        halves = INTER1 // 64
        open_parts = {e: [] for e in range(E1)}
        for gidx in range(GROUPS1):
            w1, w3, w2 = (Weight("L1_ffn_" + n, gidx) for n in ("w1", "w3", "w2"))
            uses[w2] = sum(1 + ((2 * t) // halves != (2 * t + 1) // halves) for t in range(4 * gidx, 4 * gidx + 4))
            for j in range(4):
                t = 4 * gidx + j
                hi, h, ready, s = hidden_tile(w1, w3, j, col("b1", t), col("b3", t))
                e_lo, e_hi = 2 * t // halves, (2 * t + 1) // halves
                if e_lo == e_hi:
                    open_parts[e_lo].append((hi, h, ready, w2, j, 0, P))
                else:
                    open_parts[e_lo].append((hi, h, ready, w2, j, 0, 64))
                    open_parts[e_hi].append((hi, h, ready, w2, j, 64, P))
                if pend:
                    lag -= 1
                    if lag == 0:
                        x_ready = down1(*pend)
                        pend = None
                if (2 * t + 2) % halves == 0 or e_lo != e_hi:
                    assert not pend
                    pend, lag = (open_parts[e_lo], e_lo), 2
            w1.release(s)
            w3.release(s)
        x_ready = down1(*pend)
        return [x_ready]

    x_ready = layer0_cross_attention()
    x_ready = layer0_linear_attention(x_ready)
    x_ready, ao_ready = layer0_self_attention(x_ready)
    x_ready = layer0_experts(x_ready, ao_ready)
    x_ready = layer1_cross_attention(x_ready)
    x_ready = layer1_lstm(x_ready)
    x_ready = layer1_experts(x_ready)

    stored = transfer(sp, Stream(sem("s_out")), lambda e: e.dma_start(out_dram, x[:, :, :]), *x_ready)
    sp(lambda e: e.nop(), stored)

    for q in (pe, dve, act, pool, sp):
        q.number()
    block = ctx.enter_context(nc.Block())

    @block.sync
    def _(e):
        sp.run(e)

    @block.tensor
    def _(e):
        pe.run(e)

    @block.vector
    def _(e):
        dve.run(e)

    @block.scalar
    def _(e):
        act.run(e)

    @block.gpsimd
    def _(e):
        pool.run(e)

    ctx.close()


def lay_out(I):
    def slots(w):
        r, c = w.shape
        return np.ascontiguousarray(w.reshape(4, P, c // 512, 512).transpose(2, 1, 0, 3)).reshape(-1, P, SLOT)

    def row_slots(w):
        return np.ascontiguousarray(w.reshape(-1, 4, P, 512).transpose(0, 2, 1, 3)).reshape(-1, P, SLOT)

    def padded(w, columns):
        return np.concatenate([w, np.zeros((w.shape[0], columns - w.shape[1]), w.dtype)], 1)

    def column(v):
        return v.reshape(-1, P).T

    def rope_half(w, half):
        return w.reshape(w.shape[:-1] + (HEADS, 32, 2))[..., half].reshape(w.shape[:-1] + (512,))

    A = {}
    A["x"] = I["x"].reshape(NT, P, DIM).transpose(1, 0, 2)
    A["ctxT"] = I["ctx_1024"].reshape(NSEQ, CTX, KT, P).transpose(0, 3, 2, 1).reshape(NSEQ, P, KT, CTX)
    A["mask"] = I["mask_BxS2_ik0"]
    for n in ("L0_xattn_w_q", "L0_xattn_w_kv", "L0_ffn_sh_w1", "L0_ffn_sh_w2"):
        A[n] = slots(I[n])
    A["L0_xattn_w_out"] = row_slots(I["L0_xattn_w_out"])
    for n in ("Wq", "Wk", "Wv", "Wo"):
        A["L0_attn_" + n] = slots(I["L0_attn_" + n].T)
        A["L1_xattn_" + n] = slots(I["L1_xattn_" + n].T)
        A["L1_attn_" + n] = slots(I["L1_attn_" + n])
    A["L1_attn_Wdown"] = slots(I["L1_attn_Wdown"])
    A["L1_attn_Wifg"] = slots(padded(np.concatenate([I["L1_attn_Wig"], I["L1_attn_Wfg"]], 1), 512))
    for h in range(2):
        A[f"L0_ffn_q{h + 1}"] = slots(rope_half(I["L0_ffn_q_w"], h))
        A[f"L0_ffn_k{h + 1}"] = slots(rope_half(I["L0_ffn_k_w"], h))
    A["L0_ffn_v"] = slots(I["L0_ffn_v_w"])
    A["L0_ffn_o"] = row_slots(I["L0_ffn_o_w"])
    A["router_w"] = slots(padded(I["L0_ffn_router_w"], 512))
    A["gate_w"] = slots(padded(I["L1_ffn_gate_w"], 512))
    for n in ("L0_ffn_re_w1", "L0_ffn_re_w2"):
        A[n] = row_slots(I[n].reshape(-1, 512))
    for n in ("w1", "w3"):
        A["L1_ffn_" + n] = slots(I["L1_ffn_" + n].transpose(1, 0, 2).reshape(DIM, E1 * INTER1))
        A["L1_ffn_s" + n] = slots(padded(I["L1_ffn_s" + n], 1536))
    A["L1_ffn_w2"] = row_slots(I["L1_ffn_w2"].reshape(-1, 512))
    sw2 = I["L1_ffn_sw2"]
    A["L1_ffn_sw2"] = row_slots(np.concatenate([sw2, np.zeros((1536 - SHARED1, 512), sw2.dtype)], 0))
    A["L0_ffn_re_b2"], A["L1_ffn_b2"] = I["L0_ffn_re_b2"], I["L1_ffn_b2"]
    col_values = {
        "ln_gamma": column(I["L0_xattn_ln_gamma"]), "ln_beta": column(I["L0_xattn_ln_beta"]),
        "q_b1": column(rope_half(I["L0_ffn_q_b"], 0)), "q_b2": column(rope_half(I["L0_ffn_q_b"], 1)),
        "k_b1": column(rope_half(I["L0_ffn_k_b"], 0)), "k_b2": column(rope_half(I["L0_ffn_k_b"], 1)),
        "v_b": column(I["L0_ffn_v_b"]), "theta": np.tile(I["L0_ffn_theta"], 4)[:, None],
        "sh_b1": column(I["L0_ffn_sh_b1"]), "re_b1": column(I["L0_ffn_re_b1"].reshape(-1)),
        "bq": column(I["L1_xattn_bq"]), "bk": column(I["L1_xattn_bk"]), "bv": column(I["L1_xattn_bv"]),
        "b1": column(I["L1_ffn_b1"].reshape(-1)), "b3": column(I["L1_ffn_b3"].reshape(-1)),
        "sb1": column(I["L1_ffn_sb1"]), "sb3": column(I["L1_ffn_sb3"])}
    A["cols"] = np.concatenate([col_values[n] for n in COLS], 1)
    row_values = {
        "b_out": I["L0_xattn_b_out"], "gate": I["L0_xattn_gate"], "W_gamma": I["L0_attn_W_gamma"],
        "b_gamma": I["L0_attn_b_gamma"], "W_lambda": I["L0_attn_W_lambda"], "b_lambda": I["L0_attn_b_lambda"],
        "gamma1": I["L0_ffn_gamma1"], "gamma2": I["L0_ffn_gamma2"], "o_b": I["L0_ffn_o_b"],
        "sh_b2": I["L0_ffn_sh_b2"], "router_b": I["L0_ffn_router_b"], "bo": I["L1_xattn_bo"],
        "norm_w": I["L1_attn_norm_w"].reshape(-1),
        "b_ifg": np.concatenate([I["L1_attn_big"], I["L1_attn_bfg"]]), "sb2": I["L1_ffn_sb2"],
        "gate_b": I["L1_ffn_gate_b"]}
    A["rows"] = np.concatenate([row_values[n] for n in ROWS])[None, :]
    return {n: np.ascontiguousarray(a) for n, a in A.items()}


def kernel(**inputs):
    import concourse.bacc as bacc
    from concourse.bass_utils import run_bass_kernel_spmd

    arrays = lay_out({n: np.asarray(a) for n, a in inputs.items()})
    nc = bacc.Bacc("TRN2", target_bir_lowering=False, num_devices=1)
    A = {n: nc.dram_tensor("in_" + n, a.shape, mybir.dt.from_np(a.dtype), kind="ExternalInput").ap()
         for n, a in arrays.items()}
    out = nc.dram_tensor("out_x", (P, NT, DIM), F32, kind="ExternalOutput").ap()
    build_program(nc, A, out)
    r = run_bass_kernel_spmd(nc, [{"in_" + n: a for n, a in arrays.items()}], core_ids=[0])
    got = r.results[0]["out_x"]
    return np.ascontiguousarray(got.transpose(1, 0, 2)).reshape(NSEQ, SEQ, DIM)
```

```python
from contextlib import ExitStack

import concourse.bass as bass
from concourse import mybir
import numpy as np

P = 128
F32 = mybir.dt.float32
I32 = mybir.dt.int32
U32 = mybir.dt.uint32
ALU = mybir.AluOpType
ACT = mybir.ActivationFunctionType
AX_X = mybir.AxisListType.X

NSEQ, SEQ, DIM, CTX = 8, 64, 512, 512
TOK = NSEQ * SEQ
NT = TOK // P
KT = DIM // P
HEADS = 16
E0, TOP0 = 31, 3
E1, TOP1 = 16, 2
INTER1 = 704
SHARED1 = 1408
HT0, HT1 = 4, 6
LAST1 = INTER1 - (HT1 - 1) * P
CAP = TOK
CHUNKS = CAP // P
MASKED = -1.0e30
MASK_ENERGY = -1.0e20
EPS_LN = 1e-5
SLOT = KT * DIM

COLS = {}
_n = 0
for _name, _w in [("ln_gamma", 4), ("ln_beta", 4), ("q_b1", 4), ("q_b2", 4), ("k_b1", 4), ("k_b2", 4),
                  ("v_b", 8), ("theta", 1), ("sh_b1", 4), ("re_b1", 4 * E0), ("bq", 4), ("bk", 4), ("bv", 4),
                  ("b1", HT1 * E1), ("b3", HT1 * E1), ("sb1", 11), ("sb3", 11)]:
    COLS[_name] = (_n, _w)
    _n += _w
NCOLS = _n

ROWS = {}
_n = 0
for _name, _w in [("b_out", 512), ("gate", 1), ("W_gamma", 16), ("b_gamma", 16), ("W_lambda", 16),
                  ("b_lambda", 16), ("gamma1", 512), ("gamma2", 512), ("o_b", 512), ("sh_b2", 512),
                  ("router_b", E0), ("bo", 512), ("norm_w", 512), ("b_ifg", 8), ("sb2", 512), ("gate_b", E1)]:
    ROWS[_name] = (_n, _w)
    _n += _w
NROWS = _n


class Step:

    def __init__(self, queue, emit, after):
        self.queue, self.emit, self.after = queue, emit, after
        self.awaited, self.count = False, None


class Queue:

    def __init__(self, sem):
        self.sem, self.steps = sem, []

    def __call__(self, emit, *after):
        step = Step(self, emit, [s for s in after if s is not None])
        for s in step.after:
            s.awaited = True
        self.steps.append(step)
        return step

    def number(self):
        n = 0
        for s in self.steps:
            if s.queue is self and s.awaited:
                n += 1
                s.count = n
            s.reached = n

    def run(self, eng):
        self._run(eng, 0, {})

    def _wait(self, eng, after, seen):
        for a in after:
            if seen.get(id(a.queue), 0) < a.count:
                eng.wait_ge(a.queue.sem, a.count)
                seen[id(a.queue)] = a.count

    def _run(self, eng, at, seen):
        while at < len(self.steps):
            s = self.steps[at]
            if isinstance(s, EndIf):
                return at
            self._wait(eng, s.after, seen)
            if isinstance(s, BeginIf):
                n = eng.value_load(s.emit, min_val=0, max_val=CAP)
                with eng.If(n > 0):
                    end = self._run(eng, at + 1, dict(seen))
                with eng.Else():
                    self._skip(eng, at, end, dict(seen))
                at = end + 1
                continue
            ins = s.emit(eng)
            if isinstance(s, Transfer):
                ins.then_inc(s.stream.sem, 16)
            elif s.awaited:
                ins.then_inc(self.sem, 1)
            at += 1
        return at

    def _skip(self, eng, begin, end, seen):
        before, skipped = self.steps[begin].reached, self.steps[end].reached - self.steps[begin].reached
        if skipped:
            if before:
                eng.wait_ge(self.sem, before)
            eng.sem_inc(self.sem, skipped)
        streams = {}
        for s in self.steps[begin:end]:
            if isinstance(s, Transfer) and s.stand_in is None and not s.local:
                streams.setdefault(id(s.stream), []).append(s)
            elif isinstance(s, Transfer) and s.stand_in and self.steps[begin].inner:
                self._wait(eng, s.after, seen)
                s.stand_in(eng).then_inc(s.stream.sem, 16)
        for ts in streams.values():
            if ts[0].count > 16:
                eng.wait_ge(ts[0].stream.sem, ts[0].count - 16)
            eng.sem_inc(ts[0].stream.sem, 16 * len(ts))


class BeginIf(Step):

    inner = False


class EndIf(Step):
    pass


class Stream:

    def __init__(self, sem):
        self.sem, self.total = sem, 0


class Transfer(Step):

    def __init__(self, issuer, stream, emit, after):
        Step.__init__(self, stream, emit, after)
        stream.total += 16
        self.stream, self.count = stream, stream.total
        self.stand_in = None
        self.local = False


def transfer(issuer, stream, emit, *after):
    t = Transfer(issuer, stream, emit, [s for s in after if s is not None])
    for s in t.after:
        s.awaited = True
    issuer.steps.append(t)
    return t


class Ring:

    def __init__(self, buffers):
        self.buffers, self.read, self.n = buffers, [None] * len(buffers), 0

    def take(self):
        i = self.n % len(self.buffers)
        self.n += 1
        return i, self.buffers[i], self.read[i]

    def free(self, i, step):
        self.read[i] = step


def build_program(nc, A, out_dram):
    ctx = ExitStack()

    def sbuf(name, shape, dt=F32):
        return ctx.enter_context(nc.sbuf_tensor(name, shape, dt))

    x = sbuf("x_tok", [P, NT, DIM])
    xn = sbuf("xn_tok", [P, NT, DIM])
    xnT = sbuf("xnT", [P, KT, TOK])
    cols = sbuf("cols", [P, NCOLS])
    rows = sbuf("rows", [P, NROWS])
    ident = sbuf("ident", [P, P])
    mask_ij = sbuf("mask_ij", [P, P])
    mask_ji = sbuf("mask_ji", [P, P])
    upto = sbuf("upto", [P, P])
    small = sbuf("small", [P, 1024])
    NW = 8
    wmem = sbuf("weights", [P, NW * SLOT])
    wslots = [wmem[:, i * SLOT:(i + 1) * SLOT] for i in range(NW)]
    ARENA = 24064
    arena = sbuf("arena", [P, ARENA])
    banks = [ctx.enter_context(nc.psum_tensor(f"bank{i}", [P, 512], F32)) for i in range(8)]

    def sem(name):
        return ctx.enter_context(nc.semaphore(name))

    pe, dve, act, pool, sp = (Queue(sem("s_" + n)) for n in ("tensor", "vector", "scalar", "gpsimd", "sync"))
    compute = (pe, dve, act, pool)

    def col(name, j=0, n=1, lo=0, hi=P):
        a = COLS[name][0] + j
        return cols[lo:hi, a:a + n]

    def row(name, j=0, n=None):
        a, w = ROWS[name]
        return rows[:, a + j:a + j + (w if n is None else n)]

    def over_last(ap, n):
        return ap.unsqueeze(2).to_broadcast([ap.shape[0], ap.shape[1], n])

    def over_middle(ap, n):
        return ap.unsqueeze(1).to_broadcast([ap.shape[0], n, ap.shape[1]])

    class Layout:

        def __init__(self, first=0):
            self.at = first

        def __call__(self, *shape):
            n = 1
            for d in shape:
                n *= d
            assert self.at + n <= ARENA, (self.at, n)
            v = arena[:, self.at:self.at + n]
            self.at += n
            if len(shape) == 2:
                v = v.rearrange("p (a b) -> p a b", a=shape[0])
            if len(shape) == 3:
                v = v.rearrange("p (a b c) -> p a b c", a=shape[0], b=shape[1])
            return v

    def stage_end():
        last = [next(s for s in reversed(q.steps) if not isinstance(s, (BeginIf, EndIf))) for q in compute]
        fence.clear()
        fence.extend(last)

        for q in compute:
            q(lambda e: e.nop(), *last)

    fence = []

    class only_if:

        def __init__(self, flag, *after, inner=False):
            self.flag, self.after, self.inner = flag, after, inner

        def __enter__(self):
            for q in compute + (sp,):
                for a in self.after:
                    a.awaited = True
                q.steps.append(BeginIf(q, self.flag, list(self.after)))
                q.steps[-1].inner = self.inner

        def __exit__(self, *exc):
            for q in compute + (sp,):
                q.steps.append(EndIf(q, None, []))

    small_at, used = {}, [0]

    def small_reset():
        small_at.clear()
        used[0] = 0

    def small_buf(name, *shape):
        n = int(np.prod(shape))
        if name not in small_at:
            small_at[name] = used[0]
            used[0] += n
            assert used[0] <= 1024
        v = small[:, small_at[name]:small_at[name] + n]
        if len(shape) == 2:
            v = v.rearrange("p (a b) -> p a b", a=shape[0])
        return v

    wstreams = [Stream(sem(f"s_weights{i}")) for i in range(NW)]
    wring = Ring(wslots)

    class Weight:

        def __init__(self, name, chunk):
            self.i, buf, read = wring.take()
            assert read != "held", name
            self.view = buf.rearrange("p (k n) -> p k n", k=KT)
            src = A[name][chunk]
            self.landed = transfer(sp, wstreams[self.i], lambda e: e.dma_start(buf, src), read)
            wring.free(self.i, "held")

        def release(self, step):
            wring.free(self.i, step)

    def project_into(bank, weight, j0, m, rhs, free, *after, nk=KT, start=True, stop=True):
        s = None
        for k in range(nk):
            s = pe(lambda e, k=k: e.matmul(bank, weight.view[:, k, j0:j0 + m], rhs(k),
                                           start=(start and k == 0), stop=(stop and k == nk - 1)),
                   *((free, weight.landed) + after if k == 0 else ()))
        return s

    def project_tokens(bank, lhs, weight, j0, n, free, *after, k0=0, start=True, stop=True):
        s = None
        for k in range(KT):
            s = pe(lambda e, k=k: e.matmul(bank, lhs(k0 + k), weight.view[:, k, j0:j0 + n],
                                           start=(start and k == 0), stop=(stop and k == KT - 1)),
                   *((free, weight.landed) + after if k == 0 else ()))
        return s

    load_cols = transfer(act, Stream(sem("s_cols")), lambda e: e.dma_start(cols[:, :], A["cols"]))
    load_rows = transfer(act, Stream(sem("s_rows")),
                         lambda e: e.dma_start(rows[:, :], A["rows"].to_broadcast([P, NROWS])))
    load_x = transfer(sp, Stream(sem("s_x")), lambda e: e.dma_start(x[:, :, :], A["x"]))

    pool(lambda e: e.memset(ident[:, :], 0.0))
    zeroed = pool(lambda e: e.memset(mask_ij[:, :], 0.0))
    zeroed2 = pool(lambda e: e.memset(mask_ji[:, :], 0.0))
    ident_ready = pool(lambda e: e.affine_select(out=ident[:, :], in_=ident[:, :], compare_op=ALU.not_equal,
                                                 fill=1.0, base=0, pattern=[[-1, P]], channel_multiplier=1),
                       zeroed2)
    a = pool(lambda e: e.affine_select(out=mask_ij[:, :], in_=mask_ij[:, :], compare_op=ALU.is_ge,
                                       fill=MASKED, base=0, pattern=[[-1, P]], channel_multiplier=1), zeroed)
    b = pool(lambda e: e.affine_select(out=mask_ij[:, 0:SEQ], in_=mask_ij[:, 0:SEQ], compare_op=ALU.is_ge,
                                       fill=MASKED, base=SEQ - 1, pattern=[[0, SEQ]], channel_multiplier=-1), a)
    a = pool(lambda e: e.affine_select(out=mask_ji[:, :], in_=mask_ji[:, :], compare_op=ALU.is_ge,
                                       fill=MASKED, base=0, pattern=[[1, P]], channel_multiplier=-1), zeroed2)
    b = pool(lambda e: e.affine_select(out=mask_ji[:, SEQ:P], in_=mask_ji[:, SEQ:P], compare_op=ALU.is_ge,
                                       fill=MASKED, base=-SEQ, pattern=[[0, SEQ]], channel_multiplier=1), a, b)
    masks_ready = b
    upto_ready = dve(lambda e: e.tensor_scalar(upto[:, :], mask_ji[:, :], 0.0, None, ALU.is_equal), masks_ready)

    tri, ones = sbuf("tri", [P, P]), sbuf("ones", [P, P])
    expert_no, token_no = sbuf("expert_no", [P, E0]), sbuf("token_no", [P, NT], I32)
    expert_int = sbuf("expert_int", [P, E0], I32)
    zero_words = sbuf("zero_words", [E0 * CHUNKS, P], I32)
    a = pool(lambda e: e.memset(ones[:, :], 1.0))
    ones_ready = a
    tri_ready = pool(lambda e: e.affine_select(out=tri[:, :], in_=ones[:, :], compare_op=ALU.is_ge, fill=0.0,
                                               base=0, pattern=[[1, P]], channel_multiplier=-1), a)
    a = pool(lambda e: e.iota(expert_int[:, :], pattern=[[1, E0]], base=0, channel_multiplier=0))
    expert_no_ready = dve(lambda e: e.tensor_copy(expert_no[:, :], expert_int[:, :]), a)
    token_no_ready = pool(lambda e: e.iota(token_no[:, :], pattern=[[P, NT]], base=0, channel_multiplier=1))
    zero_words_ready = pool(lambda e: e.memset(zero_words[:, :], 0))
    ids, expert_out, expert_rest, cleared = {}, {}, {}, {}
    token_rows = nc.dram_tensor("token_rows", (TOK, DIM), F32, kind="Internal").ap()
    for layer, n in ((0, E0), (1, E1)):
        ids[layer] = nc.dram_tensor(f"ids{layer}", (n * CAP, 1), I32, kind="Internal").ap()
        expert_out[layer] = nc.dram_tensor(f"expert_out{layer}", (n * P, DIM), F32, kind="Internal").ap()
        expert_rest[layer] = nc.dram_tensor(f"expert_rest{layer}", (n * (CAP - P), DIM), F32, kind="Internal").ap()
        cleared[layer] = transfer(act, Stream(sem(f"s_cleared{layer}")), lambda e, n=n, layer=layer: e.dma_start(
            ids[layer].rearrange("(c p) o -> c (p o)", p=P), zero_words[0:n * CHUNKS, :]), zero_words_ready)

    def inverse_root(dst, src, eps, *after):
        a = dve(lambda e: e.tensor_scalar(dst, src, eps, None, ALU.add), *after)
        a = act(lambda e: e.activation(dst, dst, ACT.Sqrt), a)
        return dve(lambda e: e.reciprocal(dst, dst), a)

    def layer_norm(src, dst, eps, *after):
        stats, mv, rstd = small_buf("stats", NT, 6), small_buf("mv", NT, 2), small_buf("rstd", NT)
        st = [dve(lambda e, i=i: e.bn_stats(stats[:, i, :], src[:, i, :]), *after) for i in range(NT)]
        ag = [dve(lambda e, i=i: e.bn_aggr(mv[:, i, :], stats[:, i, :]), st[i]) for i in range(NT)]
        r = inverse_root(rstd[:, :], mv[:, :, 1], eps, ag[-1])
        return [dve(lambda e, i=i: e.tensor_scalar(dst[:, i, :], src[:, i, :], mv[:, i, 0:1], rstd[:, i:i + 1],
                                                   ALU.subtract, ALU.mult), r) for i in range(NT)]

    def rms_norm(src, dst, gamma, square, *after):
        ssq, rms = small_buf("ssq", NT), small_buf("rms", NT)
        sq = None
        for i in range(NT):
            sq = dve(lambda e, i=i: e.tensor_tensor_reduce(out=square, in0=src[:, i, :], in1=src[:, i, :],
                                                           scale=1.0 / DIM, scalar=0.0, op0=ALU.mult, op1=ALU.add,
                                                           accum_out=ssq[:, i:i + 1]), sq, *after)
        r = inverse_root(rms[:, :], ssq[:, :], EPS_LN, sq)
        return [dve(lambda e, i=i: e.scalar_tensor_tensor(out=dst[:, i, :], in0=src[:, i, :],
                                                          scalar=rms[:, i:i + 1], in1=gamma,
                                                          op0=ALU.mult, op1=ALU.mult), r) for i in range(NT)]

    def to_feature_major(src, dst, ring, written, reader, affine=False):
        last = []
        for k in range(KT):
            bi, bank, free = ring.take()
            for i in range(NT):
                t = pe(lambda e, i=i, k=k, bank=bank: e.transpose(bank[:, i * P:(i + 1) * P],
                                                                  src[:, i, k * P:(k + 1) * P], ident[:, :]),
                       written[i], ident_ready, free if i == 0 else None)
            if affine:
                c = dve(lambda e, k=k, bank=bank: e.tensor_scalar(dst[:, k, :], bank[:, :], col("ln_gamma", k),
                                                                  col("ln_beta", k), ALU.mult, ALU.add),
                        t, load_cols, reader)
            elif k % 2:
                c = act(lambda e, k=k, bank=bank: e.copy(dst[:, k, :], bank[:, :]), t, reader)
            else:
                c = dve(lambda e, k=k, bank=bank: e.tensor_copy(dst[:, k, :], bank[:, :]), t, reader)
            ring.free(bi, c)
            last.append(c)
        return last

    def add_product_to_x(srcT, nk, weights, ring, finish, *after):
        out = []
        for i in range(NT):
            bi, bank, free = ring.take()
            for w, weight in enumerate(weights):
                s = project_tokens(bank[:, :], lambda k, i=i: srcT[:, k, i * P:(i + 1) * P], weight, 0, DIM,
                                   free, *after, k0=w * KT, start=(w == 0), stop=(w == len(weights) - 1))
            f = finish(i, bank, s)
            ring.free(bi, f)
            out.append(f)
        for weight in weights:
            weight.release(s)
        return out

    ctx_streams = [Stream(sem("s_ctx0")), Stream(sem("s_ctx1"))]
    mask_streams = [Stream(sem("s_mask0")), Stream(sem("s_mask1"))]

    def cross_attention(layer, head_dim, scale, w_q, w_k, w_v, q_affine, masked, xnT_ready):
        L = Layout()
        tiles = HEADS * head_dim // P
        nv = HEADS * head_dim // DIM
        qT = L(tiles, TOK)
        kT = [L(tiles, CTX) for _ in range(2)]
        v = [L(CTX // P, tiles * P) for _ in range(2)]
        if layer == 0:
            ctxT = [xnT[:, :, :], L(KT, CTX)]
        else:
            ctxT = [L(KT, CTX) for _ in range(2)]
        qblk = [L(P) for _ in range(2)]
        scores = [L(CTX) for _ in range(2)] if masked else []
        prob = [xn[:, i, :] for i in range(2)]
        probT = [xn[:, i, :].rearrange("p (a b) -> p a b", a=CTX // P) for i in range(2, 4)]
        keep = [L(CTX) for _ in range(2)] if masked else None
        banks_p, banks_s = Ring(banks[0:3]), Ring(banks[3:5])
        banks_t, banks_o = Ring(banks[5:6]), Ring(banks[6:8])

        zero = [pool(lambda e, z=z: e.memset(z, 0.0)) for z in qblk]

        q_done, s = [], None
        for m in range(tiles):
            bi, bank, free = banks_p.take()
            w = w_q[m // 4]
            s = project_into(bank[:, :], w, (m % 4) * P, P, lambda k: xnT[:, k, :], free, *xnT_ready)
            if q_affine:
                c = act(lambda e, m=m, bank=bank: e.activation(qT[:, m, :], bank[:, :], ACT.Identity,
                                                               bias=col("bq", m)), s, load_cols)
            else:
                c = act(lambda e, m=m, bank=bank: e.copy(qT[:, m, :], bank[:, :]), s)
            banks_p.free(bi, c)
            q_done.append(c)
            w.release(s)
        q_projected = s

        def load_context(b, reader):
            t = transfer(sp, ctx_streams[b % 2], lambda e: e.dma_start(ctxT[b % 2], A["ctxT"][b]), reader, *fence)
            mk = None
            if masked:
                raw = keep[b % 2].bitcast(I32)
                mk = transfer(sp, mask_streams[b % 2],
                              lambda e: e.dma_start(raw, A["mask"][b:b + 1, :].to_broadcast([P, CTX])),
                              mask_read[b - 2] if b >= 2 else None, *fence)
            return t, mk

        mask_read, mask_made = {}, {}

        def make_mask(b, landed):
            raw = keep[b % 2].bitcast(I32)
            mask_made[b] = dve(lambda e: e.tensor_scalar(keep[b % 2], raw, 0, MASK_ENERGY, ALU.is_equal, ALU.mult),
                               landed)

        kv_ready = {}

        last_pv = {}

        def kv_groups(b, landed):
            done = []

            def key_group(m):
                bi, bank, free = banks_p.take()
                s = project_into(bank[:, :], w_k[m // 4], (m % 4) * P, P, lambda k: ctxT[b % 2][:, k, :], free,
                                 landed)
                if q_affine:
                    c = act(lambda e: e.activation(kT[b % 2][:, m, :], bank[:, :], ACT.Identity,
                                                   bias=col("bk", m)), s, last_pv.get(b - 2), load_cols)
                else:
                    c = act(lambda e: e.copy(kT[b % 2][:, m, :], bank[:, :]), s, last_pv.get(b - 2))
                banks_p.free(bi, c)
                done.append(c)
                return s

            def value_group(t, n):
                bi, bank, free = banks_p.take()
                s = project_tokens(bank[:, :], lambda k: ctxT[b % 2][:, k, t * P:(t + 1) * P], w_v[n], 0, DIM, free,
                                   landed)
                c = dve(lambda e: e.tensor_copy(v[b % 2][:, t, n * DIM:(n + 1) * DIM], bank[:, :]), s,
                        last_pv.get(b - 2))
                banks_p.free(bi, c)
                done.append(c)
                return s

            kv_ready[b] = done
            todo = [lambda m=m: key_group(m) for m in range(tiles)]
            todo += [lambda t=t, n=n: value_group(t, n) for t in range(CTX // P) for n in range(nv)]
            return todo

        stat = small_buf("xstat", 2, 8)
        per_tile = P // head_dim // 2
        state = {}
        blk_ring, score_ring, prob_ring, probT_ring = Ring(qblk), Ring(scores), Ring(prob), Ring(probT)

        def unit_scores(b, u):
            m, r0 = u // per_tile, (u % per_tile) * 2 * head_dim
            ji, blk, free = blk_ring.take()
            r1 = r0 + head_dim
            c0 = pool(lambda e: e.tensor_copy(blk[r0:r1, 0:SEQ], qT[r0:r1, m, b * SEQ:(b + 1) * SEQ]),
                      q_done[m], free, zero[ji])
            c = pool(lambda e: e.tensor_copy(blk[r1:r1 + head_dim, SEQ:P],
                                             qT[r1:r1 + head_dim, m, b * SEQ:(b + 1) * SEQ]),
                     q_done[m], free, zero[ji], c0)
            si, bank, sfree = banks_s.take()
            ready = kv_ready[b] if u == 0 else ()
            s = pe(lambda e: e.matmul(bank[:, :], blk[r0:r1 + head_dim, :], kT[b % 2][r0:r1 + head_dim, m, :],
                                      start=True, stop=True), c, sfree, *ready)
            blk_ring.free(ji, s)
            st = stat[:, u % 2, :]
            if masked:
                ri, sc, rfree = score_ring.take()
                g = dve(lambda e: e.tensor_tensor_reduce(out=sc, in0=bank[:, :], in1=keep[b % 2], scale=1.0,
                                                         scalar=-3.0e38, op0=ALU.add, op1=ALU.max,
                                                         accum_out=st[:, 0:1]), s, mask_made[b], rfree)
                mask_read[b] = g
                banks_s.free(si, g)
                source = sc
            else:
                g = dve(lambda e: e.reduce_max(st[:, 0:1], bank[:, :], AX_X), s)
                source = bank[:, :]
            n = dve(lambda e: e.tensor_scalar(st[:, 1:2], st[:, 0:1], -scale, None, ALU.mult), g)
            pi, pr, pfree = prob_ring.take()
            ex = act(lambda e: e.activation(pr, source, ACT.Exp, bias=st[:, 1:2], scale=scale,
                                            accum_out=st[:, 2:3]), n, pfree)
            if masked:
                score_ring.free(ri, ex)
            else:
                banks_s.free(si, ex)
            rc = dve(lambda e: e.reciprocal(st[:, 3:4], st[:, 2:3]), ex)
            nm = dve(lambda e: e.tensor_scalar(pr, pr, st[:, 3:4], None, ALU.mult), rc)
            state[b, u] = (pi, pr, nm)

        def unit_transpose(b, u):
            pi, pr, nm = state[b, u]
            ti, bank, free = banks_t.take()
            for t in range(CTX // P):
                s = pe(lambda e, t=t: e.transpose(bank[:, t * P:(t + 1) * P], pr[:, t * P:(t + 1) * P],
                                                  ident[:, :]), nm, free if t == 0 else None)
            prob_ring.free(pi, s)
            qi, pt, tfree = probT_ring.take()
            c = act(lambda e: e.copy(pt, bank[:, :].rearrange("p (a b) -> p a b", a=CTX // P)), s, tfree)
            banks_t.free(ti, c)
            state[b, u] = (qi, pt, c)

        def unit_values(b, u):
            qi, pt, c = state.pop((b, u))
            m, r0 = u // per_tile, (u % per_tile) * 2 * head_dim
            oi, bank, free = banks_o.take()
            rows2 = 2 * head_dim
            for t in range(CTX // P):
                s = pe(lambda e, t=t: e.matmul(bank[r0:r0 + rows2, 0:P], v[b % 2][:, t, u * rows2:(u + 1) * rows2],
                                               pt[:, t, :], start=(t == 0), stop=(t == CTX // P - 1)),
                       c, free if t == 0 else None)
            probT_ring.free(qi, s)
            for h in range(2):
                lo = r0 + h * head_dim
                hi = lo + head_dim
                dst = qT[lo:hi, m, b * SEQ:(b + 1) * SEQ]
                src = bank[lo:hi, h * SEQ:(h + 1) * SEQ]
                if q_affine:
                    o = dve(lambda e, dst=dst, src=src, lo=lo, hi=hi: e.tensor_scalar(
                        dst, src, col("bv", m, 1, lo, hi), None, ALU.add), s, load_cols)
                else:
                    o = dve(lambda e, dst=dst, src=src: e.tensor_copy(dst, src), s)
            banks_o.free(oi, o)
            return s, o

        UNITS = HEADS // 2
        landed, mk = load_context(0, q_projected)
        if masked:
            make_mask(0, mk)
        for g in kv_groups(0, landed):
            kv_ctx_read[0] = g()
        order = [(b, u) for b in range(NSEQ) for u in range(UNITS)]
        todo, last_o = [], None
        for n in range(len(order) + 2):
            b, u = order[n] if n < len(order) else (NSEQ, UNITS)
            if u == 0 and b + 1 < NSEQ:
                landed, mk = load_context(b + 1, kv_ctx_read.get(b - 1))
                if masked:
                    make_mask(b + 1, mk)
                todo = kv_groups(b + 1, landed)
                per_unit = -(-len(todo) // (UNITS - 2))
            groups = min(per_unit, len(todo)) if u >= 2 else 0
            if n < len(order):
                unit_scores(b, u)
            for _ in range(groups // 2):
                kv_ctx_read[b + 1] = todo.pop(0)()
            if 1 <= n <= len(order):
                unit_transpose(*order[n - 1])
            for _ in range(groups - groups // 2):
                kv_ctx_read[b + 1] = todo.pop(0)()
            if 2 <= n:
                last_pv[order[n - 2][0]], last_o = unit_values(*order[n - 2])
        for w in list(w_k) + list(w_v):
            w.release(kv_ctx_read[NSEQ - 1])
        kv_ctx_read.clear()
        return qT, last_o

    kv_ctx_read = {}
    all_banks = Ring(banks)

    def pipeline(items):
        second = fourth = result = None
        for item in items + [None, None]:
            third = second() if second else None
            second = item() if item else None
            after_third = third() if third else None
            if fourth:
                result = fourth()
            fourth = after_third
        return result

    def self_attention_inputs(weights, feature_major, token_major, ring, xnT_ready):
        done = {}
        for n, dst in feature_major.items():
            w = weights[n]
            for m in range(KT):
                bi, bank, free = ring.take()
                s = project_into(bank[:, :], w, m * P, P, lambda k: xnT[:, k, :], free, *xnT_ready)
                c = act(lambda e, m=m, bank=bank, dst=dst: e.copy(dst[:, m, :], bank[:, :]), s)
                ring.free(bi, c)
                done[n] = c
            w.release(s)
        for n, dst in token_major.items():
            w = weights[n]
            for i in range(NT):
                bi, bank, free = ring.take()
                s = project_tokens(bank[:, :], lambda k, i=i: xnT[:, k, i * P:(i + 1) * P], w, 0, DIM, free,
                                   *xnT_ready)
                c = dve(lambda e, i=i, bank=bank, dst=dst: e.tensor_copy(dst[:, i, :], bank[:, :]), s)
                ring.free(bi, c)
                done[n] = c
            w.release(s)
        return done

    def broadcast_rows(bank_view, column, *after):
        return pe(lambda e: e.matmul(bank_view, column.to_broadcast([P, P]), ident[:, :], start=True, stop=True),
                  *after)

    def finish_plain(i, bank, s):
        return dve(lambda e: e.tensor_tensor(x[:, i, :], bank[:, :], x[:, i, :], ALU.add), s)

    b2_stream = Stream(sem("s_b2"))

    class Experts:

        def __init__(self, layer, n, chosen, hidden_tiles, last_rows, L):
            self.layer, self.n, self.chosen = layer, n, chosen
            self.ht, self.last_rows = hidden_tiles, last_rows
            self.rows_of = [P] * (hidden_tiles - 1) + [last_rows]
            self.aff, self.top = small_buf("aff", NT, n), small_buf("top", NT, 8)
            self.pick, self.used, self.work = (small_buf(s, NT, n) for s in ("pick", "used", "work"))
            self.red = small_buf("red", NT)
            self.choice, self.choice_i = small_buf("choice", NT, 8), small_buf("choice_i", NT, 8).bitcast(U32)
            self.slot_f = small_buf("slot_f", NT, chosen)
            self.slot = small_buf("slot", NT, chosen).bitcast(I32)
            self.rank, self.is_first, self.base, self.at_f = (small_buf(s, NT, chosen) for s in
                                                              ("rank", "is_first", "base", "at_f"))
            self.first_at, self.rest_at = (small_buf(s, NT, chosen).bitcast(I32) for s in ("first_at", "rest_at"))
            self.first_gate, self.rest_gate = (small_buf(s, NT, chosen) for s in ("first_gate", "rest_gate"))
            self.over_f, self.over = small_buf("over_f", n + 1), small_buf("over", n + 1).bitcast(I32)
            self.gates = L(NT, n)
            self.gatesT, self.b2 = L(TOK), L(DIM)
            self.ids_row, self.ids = L(P), L(P)
            name = f"s_moe{layer}_"
            self.gather_streams = [Stream(sem(f"{name}gather{i}")) for i in range(4)]
            self.long_streams = [Stream(sem(f"{name}long{i}")) for i in range(3)]
            self.out_streams = [Stream(sem(f"{name}out{i}")) for i in range(3)]
            self.scatter_stream, self.ids_stream = Stream(sem(name + "scatter")), Stream(sem(name + "ids"))
            self.zero_stream = Stream(sem(name + "zero"))
            self.rows_stream = Stream(sem(name + "rows"))

        def store_rows(self, src, *after):
            return transfer(sp, self.rows_stream, lambda e: e.dma_start(
                token_rows.rearrange("(i p) d -> p i d", p=P), src[:, :, :]), *after)

        def route(self, weight, bias, srcT, src_ready, ring):
            n, aff, top, red = self.n, self.aff, self.top, self.red
            bi, bank, free = ring.take()
            for i in range(NT):
                s = project_tokens(bank[:, i * n:(i + 1) * n], lambda k, i=i: srcT[:, k, i * P:(i + 1) * P],
                                   weight, 0, n, free, *src_ready)
            weight.release(s)
            r3 = bank[:, 0:NT * n].rearrange("p (i x) -> p i x", i=NT)
            a = dve(lambda e: e.tensor_tensor(aff, r3, over_middle(bias, NT), ALU.add), s, load_rows)
            ring.free(bi, a)
            a = dve(lambda e: e.tensor_reduce(red, aff, AX_X, ALU.max), a)
            a = dve(lambda e: e.tensor_tensor(aff, aff, over_last(red, n), ALU.subtract), a)
            a = act(lambda e: e.activation(aff, aff, ACT.Exp), a)
            a = dve(lambda e: e.tensor_reduce(red, aff, AX_X, ALU.add), a)
            a = dve(lambda e: e.reciprocal(red, red), a)
            a = dve(lambda e: e.tensor_tensor(aff, aff, over_last(red, n), ALU.mult), a)
            t = [dve(lambda e, i=i: e.max(top[:, i, :], aff[:, i, :]), a) for i in range(NT)]
            t = [dve(lambda e, i=i: e.max_index(self.choice_i[:, i, :], top[:, i, :], aff[:, i, :]), t[-1])
                 for i in range(NT)]
            a = dve(lambda e: e.tensor_copy(self.choice, self.choice_i), t[-1])
            numbers = over_middle(expert_no[:, 0:n], NT)
            for k in range(self.chosen):
                a = dve(lambda e, k=k: e.tensor_tensor(self.pick, numbers, over_last(self.choice[:, :, k], n),
                                                       ALU.is_equal), a, expert_no_ready)
                if k == 0:
                    u = dve(lambda e: e.tensor_copy(self.used, self.pick), a)
                    a = dve(lambda e: e.tensor_tensor(self.gates, self.pick, over_last(top[:, :, 0], n), ALU.mult), a)
                else:
                    u = dve(lambda e: e.tensor_tensor(self.used, self.used, self.pick, ALU.add), a, u)
                    a = dve(lambda e, k=k: e.tensor_tensor(self.pick, self.pick, over_last(top[:, :, k], n),
                                                           ALU.mult), a, u)
                    a = dve(lambda e: e.tensor_tensor(self.gates, self.gates, self.pick, ALU.add), a)
            return a, u

        def place(self, routed, ring):
            a, u = routed
            n, used = self.n, self.used
            bi, bank, free = ring.take()
            for i in range(NT):
                for j in range(i + 1):
                    s = pe(lambda e, i=i, j=j, bank=bank: e.matmul(
                        bank[:, i * n:(i + 1) * n], ones[:, :] if j < i else tri[:, :], used[:, j, :],
                        start=(j == 0), stop=(j == i)), u, free, tri_ready)
            count3 = bank[:, 0:NT * n].rearrange("p (i x) -> p i x", i=NT)
            numbers, top3 = over_middle(expert_no[:, 0:n], NT), self.top[:, :, 0:self.chosen]
            for k in range(self.chosen):
                a = dve(lambda e, k=k: e.tensor_tensor(self.pick, numbers, over_last(self.choice[:, :, k], n),
                                                       ALU.is_equal), a)
                a = dve(lambda e: e.tensor_tensor(self.work, count3, self.pick, ALU.mult), a, s)
                a = dve(lambda e: e.tensor_reduce(self.red, self.work, AX_X, ALU.add), a)
                a = dve(lambda e, k=k: e.tensor_scalar(self.rank[:, :, k], self.red, -1.0, None, ALU.add), a)
            ring.free(bi, a)
            chosen = self.choice[:, :, 0:self.chosen]
            a = dve(lambda e: e.scalar_tensor_tensor(out=self.slot_f, in0=chosen, scalar=float(CAP), in1=self.rank,
                                                     op0=ALU.mult, op1=ALU.add), a)
            self.slot_ready = dve(lambda e: e.tensor_copy(self.slot, self.slot_f), a)
            a = dve(lambda e: e.tensor_scalar(self.is_first, self.rank, float(P), None, ALU.is_lt), self.slot_ready)
            a = dve(lambda e: e.tensor_tensor(self.first_gate, self.is_first, top3, ALU.mult), a)
            a = dve(lambda e: e.tensor_tensor(self.rest_gate, top3, self.first_gate, ALU.subtract), a)
            a = dve(lambda e: e.tensor_scalar(self.base, self.rank, float(P - 1), None, ALU.min), a)
            a = dve(lambda e: e.scalar_tensor_tensor(out=self.at_f, in0=chosen, scalar=float(P), in1=self.base,
                                                     op0=ALU.mult, op1=ALU.add), a)
            a = dve(lambda e: e.tensor_copy(self.first_at, self.at_f), a)
            a = dve(lambda e: e.tensor_scalar(self.base, self.rank, -float(P), 0.0, ALU.add, ALU.max), a)
            a = dve(lambda e: e.scalar_tensor_tensor(out=self.at_f, in0=chosen, scalar=float(CAP - P), in1=self.base,
                                                     op0=ALU.mult, op1=ALU.add), a)
            self.at_ready = dve(lambda e: e.tensor_copy(self.rest_at, self.at_f), a)
            for i in range(NT):
                for k in range(self.chosen):
                    self.scattered = transfer(pool, self.scatter_stream, lambda e, i=i, k=k: e.indirect_dma_start(
                        out=ids[self.layer], out_offset=bass.IndirectOffsetOnAxis(ap=self.slot[:, i, k:k + 1], axis=0),
                        in_=token_no[:, i:i + 1], in_offset=None), self.slot_ready, token_no_ready,
                        cleared[self.layer])
            bi, bank, free = ring.take()
            for i in range(NT):
                s = pe(lambda e, i=i, bank=bank: e.matmul(bank[:, 0:n], ones[:, :], used[:, i, :], start=(i == 0),
                                                          stop=(i == NT - 1)), free)
            a = dve(lambda e, bank=bank: e.tensor_scalar(self.over_f[:, 0:n], bank[:, 0:n], -float(P), 0.0, ALU.add,
                                                         ALU.max), s)
            ring.free(bi, a)
            a = dve(lambda e: e.reduce_max(self.over_f[:, n:n + 1], self.over_f[:, 0:n], AX_X), a)
            self.over_ready = dve(lambda e: e.tensor_copy(self.over, self.over_f), a)
            bi, bank, free = ring.take()
            for i in range(NT):
                s = pe(lambda e, i=i, bank=bank: e.transpose(bank[0:n, i * P:(i + 1) * P], self.gates[:, i, :],
                                                             ident[:, :]), routed[0], free)
            self.gatesT_ready = act(lambda e, bank=bank: e.copy(self.gatesT[0:n, :], bank[0:n, :]), s)
            ring.free(bi, self.gatesT_ready)

        def second_bias(self, name, ring):
            landed = transfer(sp, b2_stream, lambda e: e.dma_start(self.b2[0:self.n, :], A[name]), *fence)
            for i in range(NT):
                bi, bank, free = ring.take()
                s = pe(lambda e, i=i, bank=bank: e.matmul(bank[:, :], self.gatesT[0:self.n, i * P:(i + 1) * P],
                                                          self.b2[0:self.n, :], start=True, stop=True),
                       self.gatesT_ready, landed, free)
                c = dve(lambda e, i=i, bank=bank: e.tensor_tensor(x[:, i, :], bank[:, :], x[:, i, :], ALU.add), s)
                ring.free(bi, c)
            self.b2_read = s

        def list_tokens(self, ring):
            n = self.n * CHUNKS
            words = self.ids_row.bitcast(I32)
            landed = transfer(sp, self.ids_stream, lambda e: e.dma_start(
                words[0:n, :], ids[self.layer].rearrange("(c p) o -> c (p o)", p=P)), self.scattered)
            ids_f = self.b2[:, 0:P]
            a = dve(lambda e: e.tensor_copy(ids_f[0:n, :], words[0:n, :]), landed, self.b2_read)
            bi, bank, free = ring.take()
            s = pe(lambda e: e.transpose(bank[:, 0:n], ids_f[0:n, :], ident[0:n, 0:n]), a, free)
            self.ids_ready = dve(lambda e: e.tensor_copy(self.ids.bitcast(I32)[:, 0:n], bank[:, 0:n]), s)
            ring.free(bi, self.ids_ready)

        def run(self, weights, activate, stored_rows, L):
            ht, layer = self.ht, self.layer
            self.gather = [L(DIM) for _ in range(4)]
            self.gather_long = [L(DIM) for _ in range(3)]
            self.out = [L(DIM) for _ in range(3)]
            self.tokT = [L(KT, P) for _ in range(2)]
            self.hid = [L(ht, P) for _ in range(2)]
            self.tokT_long, self.hid_long = L(KT, 3 * P), L(ht, 3 * P)
            ids_i = self.ids.bitcast(I32)
            ring_t, ring_up, ring_down = Ring(banks[0:2]), Ring(banks[2:6]), Ring(banks[6:8])
            gather_ring, out_ring, long_ring = Ring(list(range(4))), Ring(list(range(3))), Ring(list(range(3)))
            tok_ring, hid_ring = Ring(self.tokT), Ring(self.hid)
            stage_end()

            def gather(chunk):
                gi, _, free = gather_ring.take()
                dst = self.gather[gi]
                t = transfer(pool, self.gather_streams[gi], lambda e: e.indirect_dma_start(
                    out=dst, out_offset=None, in_=token_rows,
                    in_offset=bass.IndirectOffsetOnAxis(ap=ids_i[:, chunk:chunk + 1], axis=0)),
                    self.ids_ready, stored_rows, free)
                return gi, dst, t

            long_landed = [None] * 3

            def gather_long(chunk):
                gi, _, free = long_ring.take()
                dst = self.gather_long[gi]
                t = transfer(pool, self.long_streams[gi], lambda e: e.indirect_dma_start(
                    out=dst, out_offset=None, in_=token_rows,
                    in_offset=bass.IndirectOffsetOnAxis(ap=ids_i[:, chunk:chunk + 1], axis=0)),
                    free, long_landed[gi])
                long_landed[gi] = t
                t.stand_in = lambda e: e.dma_start(dst[0:1, 0:P], token_rows[0:1, 0:P])
                return gi, dst, t

            def transpose_rows(got, dst, free, gather_ring=gather_ring):
                gi, src, landed = got
                bi, bank, bfree = ring_t.take()
                for k in range(KT):
                    s = pe(lambda e, k=k: e.transpose(bank[:, k * P:(k + 1) * P], src[:, k * P:(k + 1) * P],
                                                      ident[:, :]), landed, bfree)
                gather_ring.free(gi, s)
                c = dve(lambda e: e.tensor_copy(dst, bank[:, :].rearrange("p (a b) -> p a b", a=KT)), s, free)
                ring_t.free(bi, c)
                return c

            def up(ex, w_up, tokT, tok_ready, hid, hid_free, width):
                per_bank = 512 // width
                done = []
                for m0 in range(0, ht, per_bank):
                    ms = list(range(m0, min(ht, m0 + per_bank)))
                    got = []
                    for w in w_up:
                        bi, bank, free = ring_up.take()
                        for m in ms:
                            o = (m - m0) * width
                            s = project_into(bank[0:self.rows_of[m], o:o + width], w, m * P, self.rows_of[m],
                                             lambda k: tokT[:, k, :], free, tok_ready)
                        got.append((bi, bank, s))
                    for m in ms:
                        o, r = (m - m0) * width, self.rows_of[m]
                        done.append(activate(hid[0:r, m, :], m, r, width, [b[0:r, o:o + width] for _, b, _ in got],
                                             [s for _, _, s in got], ex, hid_free))
                    for bi, _, _ in got:
                        ring_up.free(bi, done[-1])
                for w in w_up:
                    w.release(s)
                return done, s

            def down(ex, chunk, hid, o, ready, w2, zeroed=None):
                bi, bank, free = ring_down.take()
                for m in range(ht):
                    r = self.rows_of[m]
                    s = pe(lambda e, m=m, r=r: e.matmul(bank[:, :], hid[0:r, m, o:o + P], w2.view[0:r, m, :],
                                                        start=(m == 0), stop=(m == ht - 1)), free, w2.landed, *ready)
                oi, _, ofree = out_ring.take()
                buf = self.out[oi]
                c = act(lambda e: e.copy(buf, bank[:, :]), s, ofree)
                ring_down.free(bi, c)
                if chunk == 0:
                    dst = expert_out[layer][ex * P:(ex + 1) * P, :]
                else:
                    row0 = ex * (CAP - P) + (chunk - 1) * P
                    dst = expert_rest[layer][row0:row0 + P, :]
                t = transfer(act, self.out_streams[oi], lambda e: e.dma_start(dst, buf), c, zeroed)
                out_ring.free(oi, t)
                return s

            got = gather(0)
            ti, tokT, tfree = tok_ring.take()
            tok_ready = transpose_rows(got, tokT, tfree)
            ahead = {1: gather(CHUNKS), 2: gather(2 * CHUNKS)}
            pend = None
            for ex in range(self.n):
                w_up, w2 = weights(ex)
                hi, hid, hfree = hid_ring.take()
                done, s = up(ex, w_up, tokT, tok_ready, hid, hfree, P)
                tok_ring.free(ti, s)
                if ex + 3 < self.n:
                    ahead[ex + 3] = gather((ex + 3) * CHUNKS)
                if ex + 1 < self.n:
                    ti, tokT, tfree = tok_ring.take()
                    tok_ready = transpose_rows(ahead.pop(ex + 1), tokT, tfree)
                if pend:
                    s = down(*pend[:-1])
                    pend[5].release(s)
                    hid_ring.free(pend[6], s)
                pend = (ex, 0, hid, 0, done, w2, hi)
            s = down(*pend[:-1])
            pend[5].release(s)

            added = [None] * NT

            def combine(table, at, gate, ring, streams, bufs, *after):
                for k in range(self.chosen):
                    for i in range(NT):
                        gi, _, free = ring.take()
                        buf = bufs[gi]
                        t = transfer(pool, streams[gi], lambda e, i=i, k=k, buf=buf: e.indirect_dma_start(
                            out=buf, out_offset=None, in_=table,
                            in_offset=bass.IndirectOffsetOnAxis(ap=at[:, i, k:k + 1], axis=0)),
                            free, self.at_ready, long_landed[gi] if ring is long_ring else None, *after)
                        t.local = ring is long_ring
                        if t.local:
                            long_landed[gi] = t
                        c = dve(lambda e, i=i, k=k, buf=buf: e.scalar_tensor_tensor(
                            out=x[:, i, :], in0=buf, scalar=gate[:, i, k:k + 1], in1=x[:, i, :], op0=ALU.mult,
                            op1=ALU.add), t, added[i])
                        added[i] = c
                        ring.free(gi, c)
                return c

            def stored():
                return [t for t in out_ring.read if t is not None]

            with only_if(self.over[0:1, self.n:self.n + 1], self.over_ready):
                zero = self.b2
                a = dve(lambda e: e.memset(zero, 0.0))
                zeroed = transfer(sp, self.zero_stream, lambda e: e.dma_start(
                    expert_rest[layer].rearrange("(c p) d -> p c d", p=P),
                    zero.unsqueeze(1).to_broadcast([P, self.n * (CHUNKS - 1), DIM])), a)
                for ex in range(self.n):
                    with only_if(self.over[0:1, ex:ex + 1], inner=True):
                        w_up, w2 = weights(ex)
                        free = s
                        for c in range(1, CHUNKS):
                            o = (c - 1) * P
                            tok_ready = transpose_rows(gather_long(ex * CHUNKS + c),
                                                       self.tokT_long[:, :, o:o + P], free, long_ring)
                        done, _ = up(ex, w_up, self.tokT_long, tok_ready, self.hid_long, free, 3 * P)
                        for c in range(1, CHUNKS):
                            s = down(ex, c, self.hid_long, (c - 1) * P, done, w2, zeroed)
                        w2.release(s)
                combine(expert_rest[layer], self.rest_at, self.rest_gate, long_ring, self.long_streams,
                        self.gather_long, zeroed, *stored())

            c = combine(expert_out[layer], self.first_at, self.first_gate, gather_ring, self.gather_streams,
                        self.gather, *stored())
            stage_end()
            return [c]


    def layer0_cross_attention():
        small_reset()
        w_q = [Weight("L0_xattn_w_q", c) for c in range(2)]
        w_kv = [Weight("L0_xattn_w_kv", c) for c in range(4)]
        w_out = [Weight("L0_xattn_w_out", c) for c in range(2)]
        a = layer_norm(x, xn, EPS_LN, load_x)
        a = layer_norm(xn, xn, EPS_LN, a[-1])
        xnT_ready = to_feature_major(xn, xnT, all_banks, a, None, affine=True)
        oT, o_ready = cross_attention(0, 64, 64 ** -0.5, w_q, w_kv[0:2], w_kv[2:4], False, False,
                                      xnT_ready)
        tanh_gate = small_buf("tanh_gate", 1)
        tg = act(lambda e: e.activation(tanh_gate[:, :], row("gate"), ACT.Tanh), load_rows)

        def finish_gated(i, bank, s):
            a = dve(lambda e: e.tensor_tensor(xn[:, i, :], bank[:, :], row("b_out"), ALU.add), s, load_rows)
            return dve(lambda e: e.scalar_tensor_tensor(out=x[:, i, :], in0=xn[:, i, :], scalar=tanh_gate[:, 0:1],
                                                        in1=x[:, i, :], op0=ALU.mult, op1=ALU.add), a, tg)

        x_ready = add_product_to_x(oT, 8, w_out, Ring(banks[0:3]), finish_gated, o_ready)
        stage_end()
        return x_ready

    def layer0_linear_attention(x_ready):
        small_reset()
        W = {n: Weight("L0_attn_" + n, 0) for n in ("Wk", "Wq", "Wv", "Wo")}
        a = layer_norm(x, xn, EPS_LN, *x_ready)
        ring = Ring(banks)
        xnT_ready = to_feature_major(xn, xnT, ring, a, None)
        L = Layout()
        qT, vT, k_tok, yT = L(KT, TOK), L(KT, TOK), L(NT, DIM), L(KT, TOK)
        ksq = L(NT, DIM)
        done = self_attention_inputs(W, {}, {"Wk": k_tok}, ring, xnT_ready)
        G = NT * HEADS
        g = {n: small_buf("g_" + n, G) for n in ("n2", "rn", "sum", "kbar", "zg", "zl", "log", "one_rho", "L", "minus_L", "tmp")}

        def by_head(buf):
            return buf[:, :, :].rearrange("p i (h d) -> p (i h) d", h=HEADS)

        a = pool(lambda e: e.tensor_tensor(ksq[:, :, :], k_tok[:, :, :], k_tok[:, :, :], ALU.mult), done["Wk"])
        a = dve(lambda e: e.tensor_reduce(g["n2"][:, :], by_head(ksq), AX_X, ALU.add), a)
        a = act(lambda e: e.activation(g["rn"][:, :], g["n2"][:, :], ACT.Sqrt), a)
        a = dve(lambda e: e.tensor_scalar(g["rn"][:, :], g["rn"][:, :], 1e-12, None, ALU.max), a)
        a = dve(lambda e: e.reciprocal(g["rn"][:, :], g["rn"][:, :]), a)
        k_ready = dve(lambda e: e.tensor_tensor(by_head(k_tok), by_head(k_tok), over_last(g["rn"], 32), ALU.mult), a)
        a = dve(lambda e: e.tensor_reduce(g["sum"][:, :], by_head(k_tok), AX_X, ALU.add), k_ready)
        done = self_attention_inputs(W, {"Wq": qT, "Wv": vT}, {}, ring, xnT_ready)

        def gate_logit(dst, w, b, a):
            d3 = dst[:, :].rearrange("p (i h) -> p i h", i=NT)
            s3 = g["sum"][:, :].rearrange("p (i h) -> p i h", i=NT)
            a = dve(lambda e: e.tensor_tensor(d3, s3, over_middle(row(w), NT), ALU.mult), a, load_rows)
            return dve(lambda e: e.scalar_tensor_tensor(out=d3, in0=d3, scalar=1.0 / 32, in1=over_middle(row(b), NT),
                                                        op0=ALU.mult, op1=ALU.add), a)

        b = gate_logit(g["zg"], "W_gamma", "b_gamma", a)
        a = gate_logit(g["zl"], "W_lambda", "b_lambda", a)
        a = act(lambda e: e.activation(g["zl"][:, :], g["zl"][:, :], ACT.Exp), a)
        b = act(lambda e: e.activation(g["zg"][:, :], g["zg"][:, :], ACT.Exp, scale=-1.0), b)
        a = dve(lambda e: e.tensor_scalar(g["zl"][:, :], g["zl"][:, :], 1.0, None, ALU.add), a)
        b = dve(lambda e: e.tensor_scalar(g["zg"][:, :], g["zg"][:, :], 1.0, None, ALU.add), b)
        a = dve(lambda e: e.tensor_tensor(g["tmp"][:, :], g["zl"][:, :], g["zg"][:, :], ALU.mult), a, b)
        b = dve(lambda e: e.reciprocal(g["one_rho"][:, :], g["tmp"][:, :]), a)
        b = dve(lambda e: e.tensor_scalar(g["one_rho"][:, :], g["one_rho"][:, :], -1.0, 1.0, ALU.mult, ALU.add), b)
        a = act(lambda e: e.activation(g["log"][:, :], g["tmp"][:, :], ACT.Ln), a)
        bi, bank, free = ring.take()
        s = pe(lambda e, bank=bank: e.matmul(bank[:, 0:G], upto[:, :], g["log"][:, :], start=True, stop=True), a, free,
               upto_ready)
        minus_ready = dve(lambda e, bank=bank: e.tensor_copy(g["minus_L"][:, :], bank[:, 0:G]), s)
        L_ready = dve(lambda e: e.tensor_scalar(g["L"][:, :], g["minus_L"][:, :], -1.0, None, ALU.mult), minus_ready)
        ring.free(bi, minus_ready)
        k_ready = pool(lambda e: e.tensor_tensor(by_head(k_tok), by_head(k_tok), over_last(g["one_rho"], 32), ALU.mult),
                       b, k_ready)

        ring_a, ring_l, ring_y = Ring(banks[0:3]), Ring(banks[3:6]), Ring(banks[6:8])
        decay_ring = Ring([L(KT, P) for _ in range(4)])

        def values(i, r, j, di, dec, ready):
            yi, ybank, yfree = ring_y.take()
            for hm in range(KT):
                h = 4 * hm + j
                s = pe(lambda e, hm=hm, h=h: e.matmul(ybank[r:r + 32, hm * P:(hm + 1) * P],
                                                      k_tok[:, i, 32 * h:32 * h + 32], dec[:, hm, :],
                                                      start=True, stop=True), ready, k_ready, yfree)
            decay_ring.free(di, s)
            y_ready = act(lambda e: e.copy(yT[r:r + 32, :, i * P:(i + 1) * P],
                                           ybank[r:r + 32, :].rearrange("p (a b) -> p a b", a=KT)), s)
            ring_y.free(yi, y_ready)
            return y_ready

        def decayed(i, r, j, di, dec, ex, s2, ai, abank):
            a = dve(lambda e: e.tensor_tensor(dec, abank[:, :].rearrange("p (a b) -> p a b", a=KT), dec, ALU.mult),
                    ex, s2)
            ring_a.free(ai, a)
            return lambda: lambda: values(i, r, j, di, dec, a)

        def scores(i, j):
            r = 32 * j
            li, lbank, lfree = ring_l.take()
            for hm in range(KT):
                c = i * HEADS + 4 * hm + j
                s = broadcast_rows(lbank[:, hm * P:(hm + 1) * P], g["L"][:, c:c + 1], L_ready, lfree)
            ai, abank, afree = ring_a.take()
            for hm in range(KT):
                s2 = pe(lambda e, hm=hm: e.matmul(
                    abank[:, hm * P:(hm + 1) * P], vT[r:r + 32, hm, i * P:(i + 1) * P],
                    qT[r:r + 32, hm, i * P:(i + 1) * P], start=True, stop=True),
                        afree, done["Wq"], done["Wv"])
            di, dec, dfree = decay_ring.take()
            for hm in range(KT):
                c = i * HEADS + 4 * hm + j
                a = dve(lambda e, hm=hm, c=c: e.scalar_tensor_tensor(
                    out=dec[:, hm, :], in0=lbank[:, hm * P:(hm + 1) * P], scalar=g["minus_L"][:, c:c + 1],
                    in1=mask_ji[:, :], op0=ALU.add, op1=ALU.add), s, dfree, masks_ready, minus_ready)
            ring_l.free(li, a)
            ex = act(lambda e: e.activation(dec, dec, ACT.Exp), a)
            return lambda: decayed(i, r, j, di, dec, ex, s2, ai, abank)

        y_ready = pipeline([lambda i=i, j=j: scores(i, j) for i in range(NT) for j in range(4)])

        stage_end()
        x_ready = add_product_to_x(yT, 4, [W["Wo"]], Ring(banks), finish_plain, y_ready)
        stage_end()
        return x_ready

    def layer0_self_attention(x_ready):
        small_reset()
        W = {n: Weight("L0_ffn_" + n, 0) for n in ("q1", "q2", "k1", "k2")}
        W_v = [Weight("L0_ffn_v", c) for c in range(2)]
        W_o = [Weight("L0_ffn_o", c) for c in range(2)]
        L = Layout()
        attn_out = xn
        q1, q2, k1, k2 = (L(KT, TOK) for _ in range(4))
        v_tok = L(NT, 2 * DIM)
        cos, sin, ang = L(SEQ), L(SEQ), L(SEQ)
        square = L(DIM)
        rope_ring = Ring([[L(DIM) for _ in range(4)]])
        soft_ring = Ring([L(KT, P) for _ in range(3)])
        probT_ring = Ring([L(KT, P) for _ in range(2)])
        pos = L(SEQ)
        a = pool(lambda e: e.iota(ang.bitcast(I32), pattern=[[1, SEQ]], base=0, channel_multiplier=0))
        a = dve(lambda e: e.tensor_copy(pos, ang.bitcast(I32)), a)
        ang_done = dve(lambda e: e.tensor_scalar(ang, pos, col("theta"), None, ALU.mult), a, load_cols)
        PI = float(np.pi)
        ROUND = 1.5 * 2.0 ** 23
        C1 = float(np.float32(6.28125))
        C2 = float(np.frombuffer((np.frombuffer(np.float32(2 * np.pi - C1).tobytes(), np.uint32)
                                  & np.uint32(0xFFFFF000)).tobytes(), np.float32)[0])
        C3 = float(np.float32(2 * np.pi - C1 - C2))
        turns = L(SEQ)

        def sine(dst, shift, a):
            a = dve(lambda e: e.tensor_scalar(turns, ang, 1.0 / (2 * PI), shift / (2 * PI), ALU.mult, ALU.add), a)
            a = dve(lambda e: e.tensor_scalar(turns, turns, ROUND, None, ALU.add), a)
            a = dve(lambda e: e.tensor_scalar(turns, turns, -ROUND, None, ALU.add), a)
            src = ang
            for c in (C1, C2, C3):
                a = dve(lambda e, c=c, src=src: e.scalar_tensor_tensor(out=dst, in0=turns, scalar=-c, in1=src,
                                                                       op0=ALU.mult, op1=ALU.add), a)
                src = dst
            if shift:
                a = dve(lambda e: e.tensor_scalar(dst, dst, shift, None, ALU.add), a)
            a = dve(lambda e: e.tensor_scalar(dst, dst, PI, -PI, ALU.min, ALU.max), a)
            return act(lambda e: e.activation(dst, dst, ACT.Sin), a), a

        sin_ready, a = sine(sin, 0.0, ang_done)
        cos_ready, a = sine(cos, PI / 2, a)

        a = layer_norm(x, xn, EPS_LN, *x_ready)
        a = rms_norm(xn, xn, row("gamma1"), square, a[-1], load_rows)
        ring = Ring(banks)
        xnT_ready = to_feature_major(xn, xnT, ring, a, None)

        rope_cos, rope_sin = over_middle(cos, NSEQ), over_middle(sin, NSEQ)

        def by_seq(ap):
            return ap.rearrange("p (b s) -> p b s", b=NSEQ)

        for wa, wb, o1, o2, ba, bb in (("q1", "q2", q1, q2, "q_b1", "q_b2"), ("k1", "k2", k1, k2, "k_b1", "k_b2")):
            for m in range(KT):
                ai, abank, free = ring.take()
                s1 = project_into(abank[:, :], W[wa], m * P, P, lambda k: xnT[:, k, :], free, *xnT_ready)
                bi, bbank, free = ring.take()
                s2 = project_into(bbank[:, :], W[wb], m * P, P, lambda k: xnT[:, k, :], free, *xnT_ready)
                W[wa].release(s1)
                W[wb].release(s2)
                ri, (ta, tb, tc, td), rfree = rope_ring.take()
                e1 = act(lambda e, m=m, abank=abank, ta=ta, ba=ba: e.activation(ta, abank[:, :], ACT.Identity,
                                                                                bias=col(ba, m)), s1, rfree, load_cols)
                e2 = act(lambda e, m=m, bbank=bbank, tb=tb, bb=bb: e.activation(tb, bbank[:, :], ACT.Identity,
                                                                                bias=col(bb, m)), s2)
                ring.free(ai, e1)
                ring.free(bi, e2)
                c1 = dve(lambda e, m=m, o1=o1, ta=ta: e.tensor_tensor(by_seq(o1[:, m, :]), by_seq(ta), rope_cos,
                                                                      ALU.mult), e1, cos_ready)
                c2 = pool(lambda e, tb=tb, tc=tc: e.tensor_tensor(by_seq(tc), by_seq(tb), rope_sin, ALU.mult), e2,
                          sin_ready, rfree)
                c3 = dve(lambda e, m=m, o2=o2, ta=ta: e.tensor_tensor(by_seq(o2[:, m, :]), by_seq(ta), rope_sin,
                                                                      ALU.mult), e1, sin_ready)
                c4 = pool(lambda e, tb=tb, td=td: e.tensor_tensor(by_seq(td), by_seq(tb), rope_cos, ALU.mult), e2,
                          cos_ready)
                c5 = dve(lambda e, m=m, o1=o1, tc=tc: e.tensor_tensor(o1[:, m, :], o1[:, m, :], tc, ALU.subtract), c1,
                         c2)
                qk_ready = dve(lambda e, m=m, o2=o2, td=td: e.tensor_tensor(o2[:, m, :], o2[:, m, :], td, ALU.add), c3,
                               c4)
                rope_ring.free(ri, qk_ready)
        for i in range(NT):
            for n in range(2):
                bi, bank, free = ring.take()
                s = project_tokens(bank[:, :], lambda k, i=i: xnT[:, k, i * P:(i + 1) * P], W_v[n], 0, DIM, free,
                                   *xnT_ready)
                v_ready = act(lambda e, i=i, n=n, bank=bank: e.copy(v_tok[:, i, n * DIM:(n + 1) * DIM], bank[:, :]), s)
                ring.free(bi, v_ready)
                W_v[n].release(s)
        stage_end()
        oT = L(8, TOK)
        mx, sm = small_buf("mx", 4, 4), small_buf("sm", 4, 4)
        ring_s, ring_t, ring_o = Ring(banks[0:3]), Ring(banks[3:5]), Ring(banks[5:8])
        mask_q = over_middle(mask_ij[:, :], KT)

        def scores(n, i, j):
            r, u = 32 * j, n % 4
            si, sbank, sfree = ring_s.take()
            for hm in range(KT):
                for half, (qq, kk) in enumerate(((q1, k1), (q2, k2))):
                    s = pe(lambda e, hm=hm, qq=qq, kk=kk, half=half: e.matmul(
                        sbank[:, hm * P:(hm + 1) * P], qq[r:r + 32, hm, i * P:(i + 1) * P],
                        kk[r:r + 32, hm, i * P:(i + 1) * P], start=(half == 0), stop=(half == 1)),
                           sfree, qk_ready)
            pi, pr, pfree = soft_ring.take()
            s3 = sbank[:, :].rearrange("p (a b) -> p a b", a=KT)
            a = dve(lambda e: e.tensor_tensor(pr, s3, mask_q, ALU.add), s, pfree)
            ring_s.free(si, a)
            a = dve(lambda e: e.tensor_reduce(mx[:, u, :], pr, AX_X, ALU.max), a)
            a = dve(lambda e: e.tensor_scalar(mx[:, u, :], mx[:, u, :], -(64 ** -0.5), None, ALU.mult), a)
            for hm in range(KT):
                ex = act(lambda e, hm=hm: e.activation(pr[:, hm, :], pr[:, hm, :], ACT.Exp, bias=mx[:, u, hm:hm + 1],
                                                       scale=64 ** -0.5, accum_out=sm[:, u, hm:hm + 1]), a)
            return lambda: normalised(i, j, u, pi, pr, ex)

        def normalised(i, j, u, pi, pr, ex):
            a = dve(lambda e: e.reciprocal(sm[:, u, :], sm[:, u, :]), ex)
            a = pool(lambda e: e.tensor_tensor(pr, pr, over_last(sm[:, u, :], P), ALU.mult), a)
            return lambda: transposed(i, j, pi, pr, a)

        def transposed(i, j, pi, pr, a):
            ti, tbank, tfree = ring_t.take()
            for hm in range(KT):
                s = pe(lambda e, hm=hm: e.transpose(tbank[:, hm * P:(hm + 1) * P], pr[:, hm, :], ident[:, :]), a,
                       tfree)
            soft_ring.free(pi, s)
            qi, pt, qfree = probT_ring.take()
            c = act(lambda e: e.copy(pt, tbank[:, :].rearrange("p (a b) -> p a b", a=KT)), s, qfree)
            ring_t.free(ti, c)
            return lambda: attended(i, j, qi, pt, c)

        def attended(i, j, qi, pt, c):
            oi, obank, ofree = ring_o.take()
            r = (j % 2) * 64
            for hm in range(KT):
                h = 4 * hm + j
                s = pe(lambda e, hm=hm, h=h: e.matmul(obank[r:r + 64, hm * P:(hm + 1) * P],
                                                      v_tok[:, i, 64 * h:64 * h + 64], pt[:, hm, :],
                                                      start=True, stop=True), c, ofree, v_ready)
            probT_ring.free(qi, s)
            o3 = oT[r:r + 64, j // 2::2, i * P:(i + 1) * P]
            vb = cols[r:r + 64, COLS["v_b"][0] + j // 2:COLS["v_b"][0] + 8:2]
            o = dve(lambda e: e.tensor_tensor(o3, obank[r:r + 64, :].rearrange("p (a b) -> p a b", a=KT),
                                              over_last(vb, P), ALU.add), s)
            ring_o.free(oi, o)
            return o

        o_ready = pipeline([lambda n=n: scores(n, n // 4, n % 4) for n in range(NT * 4)])

        def finish_attention(i, bank, s):
            a = dve(lambda e: e.tensor_tensor(attn_out[:, i, :], bank[:, :], xn[:, i, :], ALU.add), s)
            return dve(lambda e: e.tensor_tensor(attn_out[:, i, :], attn_out[:, i, :], row("o_b"), ALU.add), a)

        ao_ready = add_product_to_x(oT, 8, W_o, Ring(banks[0:3]), finish_attention, o_ready)
        stage_end()
        return x_ready, ao_ready

    def layer0_experts(x_ready, ao_ready):
        small_reset()
        W_sh = [Weight("L0_ffn_sh_w1", 0), Weight("L0_ffn_sh_w2", 0)]
        router_w = Weight("router_w", 0)
        L = Layout()
        attn_out, an, anT = xn, L(NT, DIM), xnT
        square = L(DIM)
        an_ready = rms_norm(attn_out, an, row("gamma2"), square, *ao_ready)
        ring = Ring(banks)
        anT_ready = to_feature_major(an, anT, ring, an_ready, None)
        for i in range(NT):
            a = pool(lambda e, i=i: e.tensor_tensor(attn_out[:, i, :], attn_out[:, i, :], an[:, i, :], ALU.add),
                     an_ready[i])
            a = pool(lambda e, i=i: e.tensor_tensor(x[:, i, :], attn_out[:, i, :], x[:, i, :], ALU.add), a)
            x_ready = pool(lambda e, i=i: e.tensor_tensor(x[:, i, :], x[:, i, :], row("sh_b2"), ALU.add), a)

        experts = Experts(0, E0, TOP0, HT0, P, L)
        gates_ready = experts.route(router_w, row("router_b"), anT, anT_ready, ring)
        stored_rows = experts.store_rows(an, *an_ready)

        mark = L.at
        hid = L(KT, TOK)
        up_ring, down_ring = Ring(banks[0:4]), Ring(banks[4:8])
        stage_end()
        h_ready = []
        for m in range(KT):
            bi, bank, free = up_ring.take()
            s = project_into(bank[:, :], W_sh[0], m * P, P, lambda k: anT[:, k, :], free)
            h_ready.append(act(lambda e, m=m, bank=bank: e.activation(hid[:, m, :], bank[:, :], ACT.Gelu,
                                                                      bias=col("sh_b1", m)), s))
            up_ring.free(bi, h_ready[-1])
        W_sh[0].release(s)
        experts.place(gates_ready, down_ring)
        for i in range(NT):
            bi, bank, free = down_ring.take()
            s = project_tokens(bank[:, :], lambda k, i=i: hid[:, k, i * P:(i + 1) * P], W_sh[1], 0, DIM, free,
                               *h_ready)
            c = dve(lambda e, i=i, bank=bank: e.tensor_tensor(x[:, i, :], bank[:, :], x[:, i, :], ALU.add), s,
                    x_ready)
            down_ring.free(bi, c)
        W_sh[1].release(s)
        experts.second_bias("L0_ffn_re_b2", down_ring)
        experts.list_tokens(up_ring)

        def weights(ex):
            w1, w2 = Weight("L0_ffn_re_w1", ex), Weight("L0_ffn_re_w2", ex)
            return (w1,), w2

        def activate(h, m, rows_, cols_, views, ready, ex, hfree):
            return act(lambda e: e.activation(h, views[0], ACT.Gelu, bias=col("re_b1", HT0 * ex + m)), *ready, hfree)

        return experts.run(weights, activate, stored_rows, Layout(mark))

    def layer1_cross_attention(x_ready):
        small_reset()
        X = {n: Weight("L1_xattn_" + n, 0) for n in ("Wq", "Wk", "Wv", "Wo")}
        a = layer_norm(x, xn, EPS_LN)
        xnT_ready = to_feature_major(xn, xnT, Ring(banks), a, None)
        oT, o_ready = cross_attention(1, 32, 32 ** -0.5, [X["Wq"]], [X["Wk"]], [X["Wv"]], True, True,
                                      xnT_ready)

        def finish_bias(i, bank, s):
            a = dve(lambda e: e.tensor_tensor(xn[:, i, :], bank[:, :], row("bo"), ALU.add), s)
            return dve(lambda e: e.tensor_tensor(x[:, i, :], xn[:, i, :], x[:, i, :], ALU.add), a)

        x_ready = add_product_to_x(oT, 4, [X["Wo"]], Ring(banks[0:3]), finish_bias, o_ready)
        stage_end()
        return x_ready

    def layer1_lstm(x_ready):
        small_reset()
        W = {n: Weight("L1_attn_" + n, 0) for n in ("Wq", "Wk", "Wv", "Wo", "Wifg", "Wdown")}
        L = Layout()
        qT, kT, v_tok, o_tok, h_tok = L(4, TOK), L(4, TOK), L(NT, DIM), L(NT, DIM), L(NT, DIM)
        a = layer_norm(x, xn, EPS_LN, *x_ready)
        ring = Ring(banks)
        xnT_ready = to_feature_major(xn, xnT, ring, a, None)
        NH, CAP = 4, 15.0
        ifg = small_buf("ifg", NT, 8)
        bi, bank, free = ring.take()
        for i in range(NT):
            s = project_tokens(bank[:, i * 8:(i + 1) * 8], lambda k, i=i: xnT[:, k, i * P:(i + 1) * P], W["Wifg"], 0, 8,
                               free, *xnT_ready)
        W["Wifg"].release(s)
        b3 = bank[:, 0:8 * NT].rearrange("p (i x) -> p i x", i=NT)
        a = dve(lambda e: e.tensor_tensor(ifg, b3, over_middle(row("b_ifg"), NT), ALU.add), s)
        ring.free(bi, a)
        a = act(lambda e: e.activation(ifg, ifg, ACT.Tanh, scale=1.0 / CAP), a)
        ifg_ready = dve(lambda e: e.tensor_scalar(ifg, ifg, CAP, None, ALU.mult), a)
        lsf = small_buf("lsf", NT, NH)
        a = act(lambda e: e.activation(lsf, ifg[:, :, 4:8], ACT.Exp, scale=-1.0), ifg_ready)
        a = dve(lambda e: e.tensor_scalar(lsf, lsf, 1.0, None, ALU.add), a)
        a = act(lambda e: e.activation(lsf, lsf, ACT.Ln), a)
        bi, bank, free = ring.take()
        s = pe(lambda e, bank=bank: e.matmul(bank[:, 0:NT * NH], upto[:, :], lsf.rearrange("p i h -> p (i h)"),
                                             start=True, stop=True), a, free)
        nlf, gj = small_buf("nlf", NT, NH), small_buf("gj", NT, NH)
        nlf_ready = dve(lambda e, bank=bank: e.tensor_copy(nlf.rearrange("p i h -> p (i h)"), bank[:, 0:NT * NH]), s)
        ring.free(bi, nlf_ready)
        gj_ready = dve(lambda e: e.tensor_tensor(gj, ifg[:, :, 0:4], nlf, ALU.add), nlf_ready)
        done = self_attention_inputs(W, {"Wq": qT, "Wk": kT}, {"Wv": v_tok}, ring, xnT_ready)
        for i in range(NT):
            bi, bank, free = ring.take()
            s = project_tokens(bank[:, :], lambda k, i=i: xnT[:, k, i * P:(i + 1) * P], W["Wo"], 0, DIM, free)
            o_done = act(lambda e, i=i, bank=bank: e.activation(o_tok[:, i, :], bank[:, :], ACT.Sigmoid), s)
            ring.free(bi, o_done)
        W["Wo"].release(s)
        stage_end()
        D_ring, C_ring, CT_ring = (Ring([L(NH, P) for _ in range(2)]) for _ in range(3))
        ring_g, ring_s, ring_t, ring_h = Ring(banks[0:2]), Ring(banks[2:4]), Ring(banks[4:6]), Ring(banks[6:8])
        top, gate_top, row_sum, norm = (small_buf(n, NT, NH) for n in ("top", "gate_top", "row_sum", "norm"))
        head_stats = small_buf("head_stats", NT * NH, 6)
        head_mv, head_rstd = small_buf("head_mv", NT * NH, 2), small_buf("head_rstd", NT * NH)
        mask_h = over_middle(mask_ij[:, :], NH)

        def gates_and_scores(i):
            gi, gbank, gfree = ring_g.take()
            for h in range(NH):
                s = broadcast_rows(gbank[:, h * P:(h + 1) * P], gj[:, i, h:h + 1], gj_ready, gfree)
            si, sbank, sfree = ring_s.take()
            for h in range(NH):
                s2 = pe(lambda e, h=h: e.matmul(sbank[:, h * P:(h + 1) * P], qT[:, h, i * P:(i + 1) * P],
                                                kT[:, h, i * P:(i + 1) * P], start=True, stop=True),
                        sfree, done["Wq"], done["Wk"])
            di, D, dfree = D_ring.take()
            g3, s3 = (b[:, :].rearrange("p (a b) -> p a b", a=NH) for b in (gbank, sbank))
            a = dve(lambda e: e.tensor_tensor(D, g3, mask_h, ALU.add), s, dfree)
            ring_g.free(gi, a)
            a = dve(lambda e: e.tensor_reduce(top[:, i, :], D, AX_X, ALU.max), a)
            a = dve(lambda e: e.tensor_scalar(top[:, i, :], top[:, i, :], -1.0, None, ALU.mult), a)
            for h in range(NH):
                d = act(lambda e, h=h: e.activation(D[:, h, :], D[:, h, :], ACT.Exp, bias=top[:, i, h:h + 1]), a)
            a = dve(lambda e: e.tensor_tensor(gate_top[:, i, :], top[:, i, :], nlf[:, i, :], ALU.add), a)
            m = act(lambda e: e.activation(gate_top[:, i, :], gate_top[:, i, :], ACT.Exp), a)
            return lambda: weighted(i, di, D, si, s3, d, m, s2)

        def weighted(i, di, D, si, s3, d, m, s2):
            ci, C, cfree = C_ring.take()
            a = dve(lambda e: e.scalar_tensor_tensor(out=C, in0=s3, scalar=128 ** -0.5, in1=D, op0=ALU.mult,
                                                     op1=ALU.mult), d, s2, cfree)
            c_ready = a
            D_ring.free(di, a)
            ring_s.free(si, a)
            a = dve(lambda e: e.tensor_reduce(row_sum[:, i, :], C, AX_X, ALU.add), a)
            a = dve(lambda e: e.scalar_tensor_tensor(out=norm[:, i, :], in0=row_sum[:, i, :], scalar=-1.0,
                                                     in1=row_sum[:, i, :], op0=ALU.mult, op1=ALU.max), a)
            a = dve(lambda e: e.tensor_tensor(norm[:, i, :], norm[:, i, :], gate_top[:, i, :], ALU.max), a, m)
            a = dve(lambda e: e.tensor_scalar(norm[:, i, :], norm[:, i, :], 1e-6, None, ALU.add), a)
            rn = dve(lambda e: e.reciprocal(norm[:, i, :], norm[:, i, :]), a)
            return lambda: transposed(i, ci, C, c_ready, rn)

        def transposed(i, ci, C, c_ready, rn):
            ti, tbank, tfree = ring_t.take()
            for h in range(NH):
                s = pe(lambda e, h=h: e.transpose(tbank[:, h * P:(h + 1) * P], C[:, h, :], ident[:, :]), c_ready,
                       tfree)
            C_ring.free(ci, s)
            ui, CT, ufree = CT_ring.take()
            c = act(lambda e: e.copy(CT, tbank[:, :].rearrange("p (a b) -> p a b", a=NH)), s, ufree)
            ring_t.free(ti, c)
            return lambda: hidden(i, ui, CT, c, rn)

        def hidden(i, ui, CT, c, rn):
            hi, hbank, hfree = ring_h.take()
            for h in range(NH):
                s = pe(lambda e, h=h: e.matmul(hbank[:, h * P:(h + 1) * P], CT[:, h, :],
                                               v_tok[:, i, h * P:(h + 1) * P], start=True, stop=True), c, hfree,
                       done["Wv"])
            CT_ring.free(ui, s)
            h3 = h_tok[:, i, :].rearrange("p (a b) -> p a b", a=NH)
            a = dve(lambda e: e.tensor_tensor(h3, hbank[:, :].rearrange("p (a b) -> p a b", a=NH),
                                              over_last(norm[:, i, :], P), ALU.mult), s, rn)
            ring_h.free(hi, a)
            for h in range(NH):
                a2 = dve(lambda e, h=h: e.bn_stats(head_stats[:, i * NH + h, :], h3[:, h, :]), a)
            for h in range(NH):
                a3 = dve(lambda e, h=h: e.bn_aggr(head_mv[:, i * NH + h, :], head_stats[:, i * NH + h, :]), a2)
            return a3

        h_stats = pipeline([lambda i=i: gates_and_scores(i) for i in range(NT)])
        r = inverse_root(head_rstd[:, :], head_mv[:, :, 1], 1e-6, h_stats)
        ho_ready = []
        for i in range(NT):
            for h in range(NH):
                hv, n = h_tok[:, i, h * P:(h + 1) * P], i * NH + h
                a = dve(lambda e, hv=hv, n=n: e.tensor_scalar(hv, hv, head_mv[:, n, 0:1], head_rstd[:, n:n + 1],
                                                              ALU.subtract, ALU.mult), r)
            a = pool(lambda e, i=i: e.tensor_tensor(h_tok[:, i, :], h_tok[:, i, :], row("norm_w"), ALU.mult), a)
            a = pool(lambda e, i=i: e.tensor_tensor(h_tok[:, i, :], h_tok[:, i, :], o_tok[:, i, :], ALU.mult), a)
            ho_ready.append(a)
        hT = L(4, TOK)
        hT_ready = to_feature_major(h_tok, hT, Ring(banks[0:2]), ho_ready, None)
        stage_end()
        x_ready = add_product_to_x(hT, 4, [W["Wdown"]], Ring(banks), finish_plain)
        stage_end()
        return x_ready

    def layer1_experts(x_ready):
        small_reset()
        gate_w = Weight("gate_w", 0)
        L = Layout()
        a = layer_norm(x, xn, EPS_LN)
        ring = Ring(banks)
        xnT_ready = to_feature_major(xn, xnT, ring, a, None)
        SLOT1 = HT1 * DIM
        slots1 = [L(SLOT1) for _ in range(3)]
        slots1 += [wmem[:, i * SLOT1:(i + 1) * SLOT1] for i in range(NW * SLOT // SLOT1)]
        experts = Experts(1, E1, TOP1, HT1, LAST1, L)
        gates_ready = experts.route(gate_w, row("gate_b"), xnT, xnT_ready, ring)
        stored_rows = experts.store_rows(xn, *a)
        for i in range(NT):
            c = pool(lambda e, i=i: e.tensor_tensor(x[:, i, :], x[:, i, :], row("sb2"), ALU.add), *a)
        x_ready = c
        stage_end()
        up_ring, down_ring = Ring(banks[0:4]), Ring(banks[4:8])
        NHID = 8
        mark = L.at
        hid_ring = Ring([L(TOK) for _ in range(NHID)])
        shared_silu = [L(TOK) for _ in range(3)]
        silu_ring = Ring(shared_silu)

        def hidden_tile(w1, w3, j, b1, b3):
            ai, abank, afree = up_ring.take()
            s1 = project_into(abank[:, :], w1, j * P, P, lambda k: xnT[:, k, :], afree)
            bi, bbank, bfree = up_ring.take()
            s2 = project_into(bbank[:, :], w3, j * P, P, lambda k: xnT[:, k, :], bfree)
            ti, tmp, tfree = silu_ring.take()
            c1 = act(lambda e: e.activation(tmp, abank[:, :], ACT.Silu, bias=b1), s1, tfree)
            up_ring.free(ai, c1)
            hi, h, hfree = hid_ring.take()
            c2 = dve(lambda e: e.scalar_tensor_tensor(out=h, in0=bbank[:, :], scalar=b3, in1=tmp, op0=ALU.add,
                                                      op1=ALU.mult), s2, c1, hfree)
            up_ring.free(bi, c2)
            silu_ring.free(ti, c2)
            return hi, h, c2, s2

        def down1(parts):
            for i in range(NT):
                bi, bank, free = down_ring.take()
                for n, (hi, h, ready, w2, j) in enumerate(parts):
                    s = pe(lambda e, n=n, h=h, w2=w2, j=j, i=i, bank=bank: e.matmul(
                        bank[:, :], h[:, i * P:(i + 1) * P], w2.view[:, j, :],
                        start=(n == 0), stop=(n == len(parts) - 1)), free, ready, w2.landed)
                    if i == NT - 1:
                        hid_ring.free(hi, s)
                        w2.release(s)
                c = dve(lambda e, i=i, bank=bank: e.tensor_tensor(x[:, i, :], bank[:, :], x[:, i, :], ALU.add), s,
                        x_ready)
                down_ring.free(bi, c)
            return s

        pend = None
        for gidx in range(3):
            w1, w3, w2 = (Weight("L1_ffn_" + n, gidx) for n in ("sw1", "sw3", "sw2"))
            parts = []
            for j in range(4 if gidx < 2 else 3):
                t = 4 * gidx + j
                hi, h, ready, s = hidden_tile(w1, w3, j, col("sb1", t), col("sb3", t))
                parts.append((hi, h, ready, w2, j))
            w1.release(s)
            w3.release(s)
            if gidx == 0:
                experts.place(gates_ready, down_ring)
            else:
                down1(pend)
            pend = parts
        shared_done = down1(pend)
        experts.second_bias("L1_ffn_b2", down_ring)
        experts.list_tokens(up_ring)

        L = Layout(mark)
        expert_silu = Ring([L(3 * P) for _ in range(3)])
        streams1 = [Stream(sem(f"s_expert{i}")) for i in range(len(slots1))]
        ring1 = Ring(slots1)
        for i in range(3, len(slots1)):
            ring1.free(i, shared_done)

        class Expert1Weight:

            def __init__(self, name, ex):
                self.i, buf, read = ring1.take()
                assert read != "held", name
                if name == "w2":
                    self.view = buf.rearrange("p (k n) -> p k n", k=HT1)
                    full = (HT1 - 1) * DIM
                    transfer(sp, streams1[self.i], lambda e: e.dma_start(buf[:, 0:full], A["L1_w2_full"][ex]), read)
                    self.landed = transfer(sp, streams1[self.i], lambda e: e.dma_start(
                        buf[0:LAST1, full:full + DIM], A["L1_w2_last"][ex]), read)
                else:
                    n = KT * INTER1
                    self.view = buf[:, 0:n].rearrange("p (k n) -> p k n", k=KT)
                    self.landed = transfer(sp, streams1[self.i], lambda e: e.dma_start(
                        buf[:, 0:n], A["L1_" + name][ex]), read)
                ring1.free(self.i, "held")

            def release(self, step):
                ring1.free(self.i, step)

        def weights(ex):
            return (Expert1Weight("w1", ex), Expert1Weight("w3", ex)), Expert1Weight("w2", ex)

        def activate(h, m, rows_, cols_, views, ready, ex, hfree):
            ti, tmp, tfree = expert_silu.take()
            b1, b3 = col("b1", HT1 * ex + m, 1, 0, rows_), col("b3", HT1 * ex + m, 1, 0, rows_)
            a = act(lambda e: e.activation(tmp[0:rows_, 0:cols_], views[0], ACT.Silu, bias=b1), *ready, tfree)
            c = dve(lambda e: e.scalar_tensor_tensor(out=h, in0=views[1], scalar=b3, in1=tmp[0:rows_, 0:cols_],
                                                     op0=ALU.add, op1=ALU.mult), *ready, a, hfree)
            expert_silu.free(ti, c)
            return c

        return experts.run(weights, activate, stored_rows, L)

    x_ready = layer0_cross_attention()
    x_ready = layer0_linear_attention(x_ready)
    x_ready, ao_ready = layer0_self_attention(x_ready)
    x_ready = layer0_experts(x_ready, ao_ready)
    x_ready = layer1_cross_attention(x_ready)
    x_ready = layer1_lstm(x_ready)
    x_ready = layer1_experts(x_ready)

    stored = transfer(sp, Stream(sem("s_out")), lambda e: e.dma_start(out_dram, x[:, :, :]), *x_ready)
    sp(lambda e: e.nop(), stored, *cleared.values())

    for q in (pe, dve, act, pool, sp):
        q.number()
    block = ctx.enter_context(nc.Block())

    @block.sync
    def _(e):
        sp.run(e)

    @block.tensor
    def _(e):
        pe.run(e)

    @block.vector
    def _(e):
        dve.run(e)

    @block.scalar
    def _(e):
        act.run(e)

    @block.gpsimd
    def _(e):
        pool.run(e)

    ctx.close()


def lay_out(I):
    def slots(w):
        r, c = w.shape
        return np.ascontiguousarray(w.reshape(4, P, c // 512, 512).transpose(2, 1, 0, 3)).reshape(-1, P, SLOT)

    def row_slots(w):
        return np.ascontiguousarray(w.reshape(-1, 4, P, 512).transpose(0, 2, 1, 3)).reshape(-1, P, SLOT)

    def padded(w, columns):
        return np.concatenate([w, np.zeros((w.shape[0], columns - w.shape[1]), w.dtype)], 1)

    def column(v):
        return v.reshape(-1, P).T

    def rope_half(w, half):
        return w.reshape(w.shape[:-1] + (HEADS, 32, 2))[..., half].reshape(w.shape[:-1] + (512,))

    A = {}
    A["x"] = I["x"].reshape(NT, P, DIM).transpose(1, 0, 2)
    A["ctxT"] = I["ctx_1024"].reshape(NSEQ, CTX, KT, P).transpose(0, 3, 2, 1).reshape(NSEQ, P, KT, CTX)
    A["mask"] = I["mask_BxS2_ik0"]
    for n in ("L0_xattn_w_q", "L0_xattn_w_kv", "L0_ffn_sh_w1", "L0_ffn_sh_w2"):
        A[n] = slots(I[n])
    A["L0_xattn_w_out"] = row_slots(I["L0_xattn_w_out"])
    for n in ("Wq", "Wk", "Wv", "Wo"):
        A["L0_attn_" + n] = slots(I["L0_attn_" + n].T)
        A["L1_xattn_" + n] = slots(I["L1_xattn_" + n].T)
        A["L1_attn_" + n] = slots(I["L1_attn_" + n])
    A["L1_attn_Wdown"] = slots(I["L1_attn_Wdown"])
    A["L1_attn_Wifg"] = slots(padded(np.concatenate([I["L1_attn_Wig"], I["L1_attn_Wfg"]], 1), 512))
    for h in range(2):
        A[f"L0_ffn_q{h + 1}"] = slots(rope_half(I["L0_ffn_q_w"], h))
        A[f"L0_ffn_k{h + 1}"] = slots(rope_half(I["L0_ffn_k_w"], h))
    A["L0_ffn_v"] = slots(I["L0_ffn_v_w"])
    A["L0_ffn_o"] = row_slots(I["L0_ffn_o_w"])
    A["router_w"] = slots(padded(I["L0_ffn_router_w"], 512))
    A["gate_w"] = slots(padded(I["L1_ffn_gate_w"], 512))
    for n in ("L0_ffn_re_w1", "L0_ffn_re_w2"):
        A[n] = row_slots(I[n].reshape(-1, 512))
    for n in ("w1", "w3"):
        w = I["L1_ffn_" + n].reshape(E1, KT, P, INTER1)
        A["L1_" + n] = w.transpose(0, 2, 1, 3).reshape(E1, P, KT * INTER1)
        A["L1_ffn_s" + n] = slots(padded(I["L1_ffn_s" + n], 1536))
    full = (HT1 - 1) * P
    w = I["L1_ffn_w2"]
    A["L1_w2_full"] = w[:, 0:full].reshape(E1, HT1 - 1, P, DIM).transpose(0, 2, 1, 3).reshape(E1, P, -1)
    A["L1_w2_last"] = w[:, full:]
    sw2 = I["L1_ffn_sw2"]
    A["L1_ffn_sw2"] = row_slots(np.concatenate([sw2, np.zeros((1536 - SHARED1, 512), sw2.dtype)], 0))
    A["L0_ffn_re_b2"], A["L1_ffn_b2"] = I["L0_ffn_re_b2"], I["L1_ffn_b2"]
    col_values = {
        "ln_gamma": column(I["L0_xattn_ln_gamma"]), "ln_beta": column(I["L0_xattn_ln_beta"]),
        "q_b1": column(rope_half(I["L0_ffn_q_b"], 0)), "q_b2": column(rope_half(I["L0_ffn_q_b"], 1)),
        "k_b1": column(rope_half(I["L0_ffn_k_b"], 0)), "k_b2": column(rope_half(I["L0_ffn_k_b"], 1)),
        "v_b": column(I["L0_ffn_v_b"]), "theta": np.tile(I["L0_ffn_theta"], 4)[:, None],
        "sh_b1": column(I["L0_ffn_sh_b1"]), "re_b1": column(I["L0_ffn_re_b1"].reshape(-1)),
        "bq": column(I["L1_xattn_bq"]), "bk": column(I["L1_xattn_bk"]), "bv": column(I["L1_xattn_bv"]),
        "b1": column(padded(I["L1_ffn_b1"], HT1 * P).reshape(-1)),
        "b3": column(padded(I["L1_ffn_b3"], HT1 * P).reshape(-1)),
        "sb1": column(I["L1_ffn_sb1"]), "sb3": column(I["L1_ffn_sb3"])}
    A["cols"] = np.concatenate([col_values[n] for n in COLS], 1)
    row_values = {
        "b_out": I["L0_xattn_b_out"], "gate": I["L0_xattn_gate"], "W_gamma": I["L0_attn_W_gamma"],
        "b_gamma": I["L0_attn_b_gamma"], "W_lambda": I["L0_attn_W_lambda"], "b_lambda": I["L0_attn_b_lambda"],
        "gamma1": I["L0_ffn_gamma1"], "gamma2": I["L0_ffn_gamma2"], "o_b": I["L0_ffn_o_b"],
        "sh_b2": I["L0_ffn_sh_b2"], "router_b": I["L0_ffn_router_b"], "bo": I["L1_xattn_bo"],
        "norm_w": I["L1_attn_norm_w"].reshape(-1),
        "b_ifg": np.concatenate([I["L1_attn_big"], I["L1_attn_bfg"]]), "sb2": I["L1_ffn_sb2"],
        "gate_b": I["L1_ffn_gate_b"]}
    A["rows"] = np.concatenate([row_values[n] for n in ROWS])[None, :]
    return {n: np.ascontiguousarray(a) for n, a in A.items()}


def kernel(**inputs):
    import concourse.bacc as bacc
    from concourse.bass_utils import run_bass_kernel_spmd

    arrays = lay_out({n: np.asarray(a) for n, a in inputs.items()})
    nc = bacc.Bacc("TRN2", target_bir_lowering=False, num_devices=1)
    A = {n: nc.dram_tensor("in_" + n, a.shape, mybir.dt.from_np(a.dtype), kind="ExternalInput").ap()
         for n, a in arrays.items()}
    out = nc.dram_tensor("out_x", (P, NT, DIM), F32, kind="ExternalOutput").ap()
    build_program(nc, A, out)
    r = run_bass_kernel_spmd(nc, [{"in_" + n: a for n, a in arrays.items()}], core_ids=[0])
    got = r.results[0]["out_x"]
    return np.ascontiguousarray(got.transpose(1, 0, 2)).reshape(NSEQ, SEQ, DIM)
```

```python
from contextlib import ExitStack

import concourse.bass as bass
from concourse import mybir
import numpy as np

P = 128
F32 = mybir.dt.float32
F32R = mybir.dt.float32r
I32 = mybir.dt.int32
U32 = mybir.dt.uint32
ALU = mybir.AluOpType
ACT = mybir.ActivationFunctionType
AX_X = mybir.AxisListType.X

NSEQ, SEQ, DIM, CTX = 8, 64, 512, 512
TOK = NSEQ * SEQ
NT = TOK // P
KT = DIM // P
HEADS = 16
E0, TOP0 = 31, 3
E1, TOP1 = 16, 2
INTER1 = 704
SHARED1 = 1408
HT0, HT1 = 4, 6
LAST1 = INTER1 - (HT1 - 1) * P
CAP = TOK
CHUNKS = CAP // P
MASKED = -1.0e30
MASK_ENERGY = -1.0e20
EPS_LN = 1e-5
SLOT = KT * DIM

COLS = {}
_n = 0
for _name, _w in [("ln_gamma", 4), ("ln_beta", 4), ("q_b1", 4), ("q_b2", 4), ("k_b1", 4), ("k_b2", 4),
                  ("v_b", 8), ("theta", 1), ("sh_b1", 4), ("re_b1", 4 * E0), ("bq", 4), ("bk", 4), ("bv", 4),
                  ("b1", HT1 * E1), ("b3", HT1 * E1), ("sb1", 11), ("sb3", 11)]:
    COLS[_name] = (_n, _w)
    _n += _w
NCOLS = _n

ROWS = {}
_n = 0
for _name, _w in [("b_out", 512), ("gate", 1), ("W_gamma", 16), ("b_gamma", 16), ("W_lambda", 16),
                  ("b_lambda", 16), ("gamma1", 512), ("gamma2", 512), ("o_b", 512), ("sh_b2", 512),
                  ("router_b", E0), ("bo", 512), ("norm_w", 512), ("b_ifg", 8), ("sb2", 512), ("gate_b", E1)]:
    ROWS[_name] = (_n, _w)
    _n += _w
NROWS = _n


class Step:

    def __init__(self, queue, emit, after):
        self.queue, self.emit, self.after = queue, emit, after
        self.awaited, self.count = False, None


class Queue:

    def __init__(self, sem):
        self.sem, self.steps = sem, []

    def __call__(self, emit, *after):
        step = Step(self, emit, [s for s in after if s is not None])
        for s in step.after:
            s.awaited = True
        self.steps.append(step)
        return step

    def number(self):
        n = 0
        for s in self.steps:
            if s.queue is self and s.awaited:
                n += 1
                s.count = n
            s.reached = n

    def run(self, eng):
        self._run(eng, 0, {})

    def _wait(self, eng, after, seen):
        for a in after:
            if seen.get(id(a.queue), 0) < a.count:
                eng.wait_ge(a.queue.sem, a.count)
                seen[id(a.queue)] = a.count

    def _run(self, eng, at, seen):
        while at < len(self.steps):
            s = self.steps[at]
            if isinstance(s, EndIf):
                return at
            self._wait(eng, s.after, seen)
            if isinstance(s, BeginIf):
                n = eng.value_load(s.emit, min_val=0, max_val=CAP)
                with eng.If(n > 0):
                    end = self._run(eng, at + 1, dict(seen))
                with eng.Else():
                    self._skip(eng, at, end, dict(seen))
                at = end + 1
                continue
            ins = s.emit(eng)
            if isinstance(s, Transfer):
                ins.then_inc(s.stream.sem, 16)
            elif s.awaited:
                ins.then_inc(self.sem, 1)
            at += 1
        return at

    def _skip(self, eng, begin, end, seen):
        before, skipped = self.steps[begin].reached, self.steps[end].reached - self.steps[begin].reached
        if skipped:
            if before:
                eng.wait_ge(self.sem, before)
            eng.sem_inc(self.sem, skipped)
        streams = {}
        for s in self.steps[begin:end]:
            if isinstance(s, Transfer) and s.stand_in is None and not s.local:
                streams.setdefault(id(s.stream), []).append(s)
            elif isinstance(s, Transfer) and s.stand_in and self.steps[begin].inner:
                self._wait(eng, s.after, seen)
                s.stand_in(eng).then_inc(s.stream.sem, 16)
        for ts in streams.values():
            if ts[0].count > 16:
                eng.wait_ge(ts[0].stream.sem, ts[0].count - 16)
            eng.sem_inc(ts[0].stream.sem, 16 * len(ts))


class BeginIf(Step):

    inner = False


class EndIf(Step):
    pass


class Stream:

    def __init__(self, sem):
        self.sem, self.total = sem, 0


class Transfer(Step):

    def __init__(self, issuer, stream, emit, after):
        Step.__init__(self, stream, emit, after)
        stream.total += 16
        self.stream, self.count = stream, stream.total
        self.stand_in = None
        self.local = False


def transfer(issuer, stream, emit, *after):
    t = Transfer(issuer, stream, emit, [s for s in after if s is not None])
    for s in t.after:
        s.awaited = True
    issuer.steps.append(t)
    return t


class Ring:

    def __init__(self, buffers):
        self.buffers, self.read, self.n = buffers, [None] * len(buffers), 0
        self.closed = ()

    def take(self, i=None):
        if i is None:
            while self.n % len(self.buffers) in self.closed:
                self.n += 1
            i = self.n % len(self.buffers)
            self.n += 1
        return i, self.buffers[i], self.read[i]

    def free(self, i, step):
        self.read[i] = step

    def part(self, lo, hi):
        ring = Ring(self.buffers[lo:hi])
        ring.read = self.read[lo:hi]
        return ring


def build_program(nc, A, out_dram):
    ctx = ExitStack()

    def sbuf(name, shape, dt=F32):
        return ctx.enter_context(nc.sbuf_tensor(name, shape, dt))

    x = sbuf("x_tok", [P, NT, DIM])
    xn = sbuf("xn_tok", [P, NT, DIM])
    xnT = sbuf("xnT", [P, KT, TOK])
    cols = sbuf("cols", [P, NCOLS])
    rows = sbuf("rows", [P, NROWS])
    ident = sbuf("ident", [P, P])
    mask_ij = sbuf("mask_ij", [P, P])
    mask_ji = sbuf("mask_ji", [P, P])
    upto = sbuf("upto", [P, P])
    small = sbuf("small", [P, 1024])
    NW = 8
    SPLIT_SLOT = 4
    SPLIT_ARENA = (8 - (NW - SPLIT_SLOT)) * SLOT
    with nc.sbuf_tensor("below_split", [P, SPLIT_SLOT * SLOT], F32):
        with nc.sbuf_tensor("split", [P, 8, KT, DIM], F32R) as split:
            pass
    wmem = sbuf("weights", [P, NW * SLOT])
    wslots = [wmem[:, i * SLOT:(i + 1) * SLOT] for i in range(NW)]
    ARENA = 23424
    EXPERTS_END = ARENA - 4 * DIM - 3 * KT * CTX
    arena = sbuf("arena", [P, ARENA])
    banks = [ctx.enter_context(nc.psum_tensor(f"bank{i}", [P, 512], F32)) for i in range(8)]

    def sem(name):
        return ctx.enter_context(nc.semaphore(name))

    pe, dve, act, pool, sp = (Queue(sem("s_" + n)) for n in ("tensor", "vector", "scalar", "gpsimd", "sync"))
    compute = (pe, dve, act, pool)

    def col(name, j=0, n=1, lo=0, hi=P):
        a = COLS[name][0] + j
        return cols[lo:hi, a:a + n]

    def row(name, j=0, n=None):
        a, w = ROWS[name]
        return rows[:, a + j:a + j + (w if n is None else n)]

    def over_last(ap, n):
        return ap.unsqueeze(2).to_broadcast([ap.shape[0], ap.shape[1], n])

    def over_middle(ap, n):
        return ap.unsqueeze(1).to_broadcast([ap.shape[0], n, ap.shape[1]])

    class Layout:

        def __init__(self, first=0):
            self.at = first

        def __call__(self, *shape):
            n = 1
            for d in shape:
                n *= d
            assert self.at + n <= ARENA, (self.at, n)
            v = arena[:, self.at:self.at + n]
            self.at += n
            if len(shape) == 2:
                v = v.rearrange("p (a b) -> p a b", a=shape[0])
            if len(shape) == 3:
                v = v.rearrange("p (a b c) -> p a b c", a=shape[0], b=shape[1])
            return v

    def stage_end():
        last = [next(s for s in reversed(q.steps) if not isinstance(s, (BeginIf, EndIf))) for q in compute]
        fence.clear()
        fence.extend(last)

        for q in compute:
            q(lambda e: e.nop(), *last)

    fence = []

    class only_if:

        def __init__(self, flag, *after, inner=False):
            self.flag, self.after, self.inner = flag, after, inner

        def __enter__(self):
            for q in compute + (sp,):
                for a in self.after:
                    a.awaited = True
                q.steps.append(BeginIf(q, self.flag, list(self.after)))
                q.steps[-1].inner = self.inner

        def __exit__(self, *exc):
            for q in compute + (sp,):
                q.steps.append(EndIf(q, None, []))

    small_at, used = {}, [0]

    def small_reset():
        small_at.clear()
        used[0] = 0

    def small_buf(name, *shape):
        n = int(np.prod(shape))
        if name not in small_at:
            small_at[name] = used[0]
            used[0] += n
            assert used[0] <= 1024
        v = small[:, small_at[name]:small_at[name] + n]
        if len(shape) == 2:
            v = v.rearrange("p (a b) -> p a b", a=shape[0])
        return v

    wstreams = [Stream(sem(f"s_weights{i}")) for i in range(NW)]
    wring = Ring(wslots)

    class Weight:

        def __init__(self, name, chunk, slot=None):
            self.i, buf, read = wring.take(slot)
            assert read != "held", name
            self.view = buf.rearrange("p (k n) -> p k n", k=KT)
            src = A[name][chunk]
            self.landed = transfer(sp, wstreams[self.i], lambda e: e.dma_start(buf, src), read)
            wring.free(self.i, "held")

        def release(self, step):
            wring.free(self.i, step)

    def project_into(bank, weight, j0, m, rhs, free, *after, nk=KT, start=True, stop=True):
        s = None
        for k in range(nk):
            s = pe(lambda e, k=k: e.matmul(bank, weight.view[:, k, j0:j0 + m], rhs(k),
                                           start=(start and k == 0), stop=(stop and k == nk - 1)),
                   *((free, weight.landed) + after if k == 0 else ()))
        return s

    def project_tokens(bank, lhs, weight, j0, n, free, *after, k0=0, start=True, stop=True):
        s = None
        for k in range(KT):
            s = pe(lambda e, k=k: e.matmul(bank, lhs(k0 + k), weight.view[:, k, j0:j0 + n],
                                           start=(start and k == 0), stop=(stop and k == KT - 1)),
                   *((free, weight.landed) + after if k == 0 else ()))
        return s

    load_cols = transfer(act, Stream(sem("s_cols")), lambda e: e.dma_start(cols[:, :], A["cols"]))

    pool(lambda e: e.memset(ident[:, :], 0.0))
    zeroed = pool(lambda e: e.memset(mask_ij[:, :], 0.0))
    zeroed2 = pool(lambda e: e.memset(mask_ji[:, :], 0.0))
    ident_ready = pool(lambda e: e.affine_select(out=ident[:, :], in_=ident[:, :], compare_op=ALU.not_equal,
                                                 fill=1.0, base=0, pattern=[[-1, P]], channel_multiplier=1),
                       zeroed2)
    a = pool(lambda e: e.affine_select(out=mask_ij[:, :], in_=mask_ij[:, :], compare_op=ALU.is_ge,
                                       fill=MASKED, base=0, pattern=[[-1, P]], channel_multiplier=1), zeroed)
    b = pool(lambda e: e.affine_select(out=mask_ij[:, 0:SEQ], in_=mask_ij[:, 0:SEQ], compare_op=ALU.is_ge,
                                       fill=MASKED, base=SEQ - 1, pattern=[[0, SEQ]], channel_multiplier=-1), a)
    a = pool(lambda e: e.affine_select(out=mask_ji[:, :], in_=mask_ji[:, :], compare_op=ALU.is_ge,
                                       fill=MASKED, base=0, pattern=[[1, P]], channel_multiplier=-1), zeroed2)
    b = pool(lambda e: e.affine_select(out=mask_ji[:, SEQ:P], in_=mask_ji[:, SEQ:P], compare_op=ALU.is_ge,
                                       fill=MASKED, base=-SEQ, pattern=[[0, SEQ]], channel_multiplier=1), a, b)
    masks_ready = b
    upto_ready = dve(lambda e: e.tensor_scalar(upto[:, :], mask_ji[:, :], 0.0, None, ALU.is_equal), masks_ready)

    tri, ones = sbuf("tri", [P, P]), sbuf("ones", [P, P])
    expert_no, token_no = sbuf("expert_no", [P, E0]), sbuf("token_no", [P, NT], I32)
    expert_int = sbuf("expert_int", [P, E0], I32)
    zero_words = sbuf("zero_words", [E0 * CHUNKS, P], I32)
    a = pool(lambda e: e.memset(ones[:, :], 1.0))
    tri_ready = pool(lambda e: e.affine_select(out=tri[:, :], in_=ones[:, :], compare_op=ALU.is_ge, fill=0.0,
                                               base=0, pattern=[[1, P]], channel_multiplier=-1), a)
    a = pool(lambda e: e.iota(expert_int[:, :], pattern=[[1, E0]], base=0, channel_multiplier=0))
    expert_no_ready = dve(lambda e: e.tensor_copy(expert_no[:, :], expert_int[:, :]), a)
    token_no_ready = pool(lambda e: e.iota(token_no[:, :], pattern=[[P, NT]], base=0, channel_multiplier=1))
    zero_words_ready = pool(lambda e: e.memset(zero_words[:, :], 0))
    ids, expert_out, expert_rest, cleared = {}, {}, {}, {}
    token_rows = nc.dram_tensor("token_rows", (TOK, DIM), F32, kind="Internal").ap()
    for layer, n in ((0, E0), (1, E1)):
        ids[layer] = nc.dram_tensor(f"ids{layer}", (n * CAP, 1), I32, kind="Internal").ap()
        expert_out[layer] = nc.dram_tensor(f"expert_out{layer}", (n * P, DIM), F32, kind="Internal").ap()
        expert_rest[layer] = nc.dram_tensor(f"expert_rest{layer}", (n * (CAP - P), DIM), F32, kind="Internal").ap()

    rows_stream, load_rows = Stream(sem("s_rows")), []
    cleared_streams = {layer: Stream(sem(f"s_cleared{layer}")) for layer in (0, 1)}

    def load_late():
        load_rows.append(transfer(sp, rows_stream,
                                  lambda e: e.dma_start(rows[:, :], A["rows"].to_broadcast([P, NROWS]))))
        for layer, n in ((0, E0), (1, E1)):
            cleared[layer] = transfer(sp, cleared_streams[layer], lambda e, n=n, layer=layer: e.dma_start(
                ids[layer].rearrange("(c p) o -> c (p o)", p=P), zero_words[0:n * CHUNKS, :]), zero_words_ready)

    norm_small = sbuf("norm_small", [P, 2, NT, 10])
    square = sbuf("square", [P, DIM])

    def inverse_root(dst, src, eps, *after):
        a = dve(lambda e: e.tensor_scalar(dst, src, eps, None, ALU.add), *after)
        a = act(lambda e: e.activation(dst, dst, ACT.Sqrt), a)
        return dve(lambda e: e.reciprocal(dst, dst), a)

    def layer_norm(i, src, dst, slot, *after):
        return layer_scale(i, src, dst, slot, layer_statistics(i, src, slot, *after))

    def layer_statistics(i, src, slot, *after):
        st = norm_small[:, slot, i, :]
        a = dve(lambda e: e.bn_stats(st[:, 0:6], src[:, i, :]), *after)
        a = dve(lambda e: e.bn_aggr(st[:, 6:8], st[:, 0:6]), a)
        a = dve(lambda e: e.tensor_scalar(st[:, 8:9], st[:, 7:8], EPS_LN, None, ALU.add), a)
        return act(lambda e: e.activation(st[:, 8:9], st[:, 8:9], ACT.Sqrt), a)

    def layer_scale(i, src, dst, slot, a):
        st = norm_small[:, slot, i, :]
        r = dve(lambda e: e.reciprocal(st[:, 8:9], st[:, 8:9]), a)
        return dve(lambda e: e.tensor_scalar(dst[:, i, :], src[:, i, :], st[:, 6:7], st[:, 8:9],
                                             ALU.subtract, ALU.mult), r)

    def rms_norm(i, src, dst, gamma, *after):
        st = norm_small[:, 1, i, :]
        a = dve(lambda e: e.tensor_tensor_reduce(out=square[:, :], in0=src[:, i, :], in1=src[:, i, :],
                                                 scale=1.0 / DIM, scalar=0.0, op0=ALU.mult, op1=ALU.add,
                                                 accum_out=st[:, 0:1]), squared[0], *after)
        squared[0] = a
        r = inverse_root(st[:, 1:2], st[:, 0:1], EPS_LN, a)
        return dve(lambda e: e.scalar_tensor_tensor(out=dst[:, i, :], in0=src[:, i, :], scalar=st[:, 1:2],
                                                    in1=gamma, op0=ALU.mult, op1=ALU.mult), r, load_rows[0])

    squared = [None]

    class FeatureMajor:

        def __init__(self, src, dst, ring, affine=False):
            self.src, self.dst, self.ring, self.affine = src, dst, ring, affine
            self.banks = [ring.take() for _ in range(KT)]

        def tile(self, i, written):
            for k, (_, bank, free) in enumerate(self.banks):
                self.s = pe(lambda e, i=i, k=k, bank=bank: e.transpose(
                    bank[:, i * P:(i + 1) * P], self.src[:, i, k * P:(k + 1) * P], ident[:, :]),
                            written, ident_ready, free)

        def finish(self):
            dst, done = self.dst, []
            for k, (bi, bank, _) in enumerate(self.banks):
                if self.affine:
                    c = dve(lambda e, k=k, bank=bank: e.tensor_scalar(
                        dst[:, k, :], bank[:, :], col("ln_gamma", k), col("ln_beta", k), ALU.mult, ALU.add),
                            self.s, load_cols)
                elif k % 2:
                    c = act(lambda e, k=k, bank=bank: e.copy(dst[:, k, :], bank[:, :]), self.s)
                else:
                    c = dve(lambda e, k=k, bank=bank: e.tensor_copy(dst[:, k, :], bank[:, :]), self.s)
                self.ring.free(bi, c)
                done.append(c)
            return done

    def to_feature_major(src, dst, ring, written, affine=False):
        f = FeatureMajor(src, dst, ring, affine)
        for i in range(NT):
            f.tile(i, written[i])
        return f.finish()

    def multiply(srcT, weights, ring, finish, *after):
        out = []
        for i in range(NT):
            bi, bank, free = ring.take()
            for w, weight in enumerate(weights):
                s = project_tokens(bank[:, :], lambda k, i=i: srcT[:, k, i * P:(i + 1) * P], weight, 0, DIM,
                                   free, *after, k0=w * KT, start=(w == 0), stop=(w == len(weights) - 1))
            f = finish(i, bank, s)
            ring.free(bi, f)
            out.append(f)
            yield i, f
        for weight in weights:
            weight.release(s)

    def multiply_and_normalise(srcT, weights, finish, norm, src, *after):
        written, normed = [], []
        f = FeatureMajor(src, xnT, Ring(banks[4:8]))
        for i, step in multiply(srcT, weights, Ring(banks[0:3]), finish, *after):
            written.append(step)
            normed.append(norm(i, step))
            if i > 0:
                f.tile(i - 1, normed[i - 1])
        f.tile(NT - 1, normed[NT - 1])
        return written, normed, f.finish()

    ctx_stream = Stream(sem("s_ctx"))
    mask_streams = [Stream(sem("s_mask0")), Stream(sem("s_mask1"))]

    def cross_attention(layer, head_dim, scale, load_weights, q_affine, masked, meanwhile=None):
        parts = HEADS * head_dim // DIM
        tiles = HEADS * head_dim // P
        steps, pairs = parts * NSEQ, HEADS // 2 // parts
        L = Layout(SPLIT_ARENA)
        qT = L(tiles, TOK)
        kT1, v1 = L(KT, CTX), L(CTX // P, DIM)
        qblk = [L(P) for _ in range(2)]
        if layer == 1:
            assert L.at <= EXPERTS_END
            L = Layout(EXPERTS_END)
        ctxT = L(KT, CTX)
        kT, v = [L(KT, CTX), kT1], [L(CTX // P, DIM), v1]
        scores = [L(CTX) for _ in range(2)] if masked else []
        prob = [xn[:, i, :] for i in range(2)]
        probT = [xn[:, i, :].rearrange("p (a b) -> p a b", a=CTX // P) for i in range(2, 4)]
        keep = [L(CTX) for _ in range(2)] if masked else None
        banks_p, banks_s = Ring(banks[0:3]), Ring(banks[3:5])
        banks_t, banks_o = Ring(banks[5:6]), Ring(banks[6:8])
        entered = []

        split_k, split_v = (split[:, 0], split[:, 1]), (split[:, 2], split[:, 3])
        split_ctx = [(split[:, 4], split[:, 5]), (split[:, 6], split[:, 7])]

        def split_tile(dst, src, k, *after):
            high, low = dst
            a = act(lambda e: e.copy(high[:, k, :], src[:, k, :]), *after)
            return dve(lambda e: e.tensor_tensor(low[:, k, :], src[:, k, :], high[:, k, :], ALU.subtract), a, *after)

        def multiply_split(bank, stationary, moving, *after):
            order = [(k, a, b) for k in range(KT) for a, b in ((0, 0), (0, 1), (1, 0))]
            for n, (k, a, b) in enumerate(order):
                s = pe(lambda e, n=n, k=k, a=a, b=b: e.matmul(bank[:, :], stationary(a, k), moving(b, k),
                                                              start=(n == 0), stop=(n == len(order) - 1)),
                       *(after if n == 0 else ()))
            return s

        weights_split, kv_read = {}, {}

        def split_weights(part, name, w):
            for k in range(KT):
                a = split_tile(split_k if name == "k" else split_v, w.view, k, w.landed,
                               kv_read.get(part * NSEQ - 1), *entered)
            w.release(a)
            weights_split[name, part] = a

        ctx_split, last_split = {}, [None]

        def load_context(c):
            return transfer(sp, ctx_stream, lambda e: e.dma_start(ctxT, A["ctxT"][c % NSEQ]), last_split[0],
                            *fence_before)

        def split_context(c, k, landed):
            last_split[0] = ctx_split[c] = split_tile(split_ctx[c % 2], ctxT, k, landed, kv_read.get(c - 2), *entered)

        fence_before = list(fence)
        landed = {0: load_context(0)}
        mask_read, mask_made = {}, {}

        def load_mask(b):
            raw = keep[b % 2].bitcast(I32)
            mk = transfer(sp, mask_streams[b % 2],
                          lambda e: e.dma_start(raw, A["mask"][b:b + 1, :].to_broadcast([P, CTX])),
                          mask_read.get(b - 2), *fence)
            mask_made[b] = dve(lambda e: e.tensor_scalar(keep[b % 2], raw, 0, MASK_ENERGY, ALU.is_equal, ALU.mult),
                               mk)

        kv_ready = {}
        last_pv, last_scores = {}, {}

        def kv_groups(c):
            done, part = [], c // NSEQ
            ctx2 = split_ctx[c % 2]

            def key_group(m):
                bi, bank, free = banks_p.take()
                s = multiply_split(bank, lambda a, k: split_k[a][:, k, m * P:(m + 1) * P],
                                   lambda b, k: ctx2[b][:, k, :], free, ctx_split[c], weights_split["k", part])
                if q_affine:
                    o = act(lambda e: e.activation(kT[c % 2][:, m, :], bank[:, :], ACT.Identity,
                                                   bias=col("bk", m)), s, last_scores.get(c - 2), load_cols)
                else:
                    o = act(lambda e: e.copy(kT[c % 2][:, m, :], bank[:, :]), s, last_scores.get(c - 2))
                banks_p.free(bi, o)
                done.append(o)
                kv_read[c] = s

            def value_group(t):
                bi, bank, free = banks_p.take()
                s = multiply_split(bank, lambda a, k: ctx2[a][:, k, t * P:(t + 1) * P],
                                   lambda b, k: split_v[b][:, k, :], free, ctx_split[c], weights_split["v", part])
                dst = v[c % 2][:, t, :]
                if c <= layer:
                    o = act(lambda e: e.copy(dst, bank[:, :]), s)
                else:
                    o = dve(lambda e: e.tensor_copy(dst, bank[:, :]), s, last_pv.get(c - 2))
                banks_p.free(bi, o)
                done.append(o)
                kv_read[c] = s

            kv_ready[c] = done
            return [lambda m=m: key_group(m) for m in range(KT)] + [lambda t=t: value_group(t)
                                                                    for t in range(CTX // P)]

        first_weights = load_weights(0)

        def plain_groups(ring):
            done = kv_ready[0] = []
            w_k, w_v = first_weights

            def key_group(m):
                bi, bank, free = ring.take()
                kv_read[0] = last_split[0] = s = project_into(
                    bank[:, :], w_k, m * P, P, lambda k: ctxT[:, k, :], free, landed[0])
                done.append(act(lambda e: e.activation(kT[0][:, m, :], bank[:, :], ACT.Identity, bias=col("bk", m)),
                                s, load_cols))
                ring.free(bi, done[-1])

            def value_group(t):
                bi, bank, free = ring.take()
                kv_read[0] = last_split[0] = s = project_tokens(
                    bank[:, :], lambda k: ctxT[:, k, t * P:(t + 1) * P], w_v, 0, DIM, free, landed[0])
                done.append(act(lambda e: e.copy(v[0][:, t, :], bank[:, :]), s))
                ring.free(bi, done[-1])

            return ([lambda m=m: key_group(m) for m in range(KT)],
                    [lambda t=t: value_group(t) for t in range(CTX // P)])

        def enter(steps, stores):
            entered.extend(steps)
            wring.closed = range(SPLIT_SLOT, NW)
            if layer == 1:
                landed[1] = load_context(1)
                split_weights(0, "k", first_weights[0])
            entered.extend(stores)
            for k in range(KT):
                split_context(layer, k, landed[layer])
            if layer == 0:
                landed[1] = load_context(1)
                split_weights(0, "k", first_weights[0])
            split_weights(0, "v", first_weights[1])
            return kv_groups(layer)

        if layer == 0:
            groups = enter([], [])
            meanwhile()
            for g in groups:
                g()

        def attend(w_q, xnT_ready):
            zero = [pool(lambda e, z=z: e.memset(z, 0.0)) for z in qblk]

            q_done, s = [], None
            for m in range(tiles):
                bi, bank, free = banks_p.take()
                w = w_q[m // 4]
                s = project_into(bank[:, :], w, (m % 4) * P, P, lambda k: xnT[:, k, :], free, *xnT_ready)
                if q_affine:
                    c = act(lambda e, m=m, bank=bank: e.activation(qT[:, m, :], bank[:, :], ACT.Identity,
                                                                   bias=col("bq", m)), s, load_cols)
                else:
                    c = act(lambda e, m=m, bank=bank: e.copy(qT[:, m, :], bank[:, :]), s)
                banks_p.free(bi, c)
                q_done.append(c)
                w.release(s)
            if layer == 0:
                for k in range(KT):
                    split_context(1, k, landed[1])
            if masked:
                load_mask(0)
            stat = small_buf("xstat", 2, 8)
            per_tile = P // head_dim // 2
            state = {}
            blk_ring, score_ring, prob_ring, probT_ring = Ring(qblk), Ring(scores), Ring(prob), Ring(probT)

            def unit_scores(c, u):
                b, tile = c % NSEQ, c // NSEQ * KT + u // per_tile
                m, r0 = u // per_tile, (u % per_tile) * 2 * head_dim
                ji, blk, free = blk_ring.take()
                r1 = r0 + head_dim
                a = pool(lambda e: e.tensor_copy(blk[r0:r1, 0:SEQ], qT[r0:r1, tile, b * SEQ:(b + 1) * SEQ]),
                         q_done[tile], free, zero[ji])
                a = pool(lambda e: e.tensor_copy(blk[r1:r1 + head_dim, SEQ:P],
                                                 qT[r1:r1 + head_dim, tile, b * SEQ:(b + 1) * SEQ]),
                         q_done[tile], free, zero[ji], a)
                si, bank, sfree = banks_s.take()
                ready = kv_ready[c][0:KT] if u == 0 else ()
                s = pe(lambda e: e.matmul(bank[:, :], blk[r0:r1 + head_dim, :], kT[c % 2][r0:r1 + head_dim, m, :],
                                          start=True, stop=True), a, sfree, *ready)
                blk_ring.free(ji, s)
                last_scores[c] = s
                st = stat[:, u % 2, :]
                if masked:
                    ri, sc, rfree = score_ring.take()
                    g = dve(lambda e: e.tensor_tensor_reduce(out=sc, in0=bank[:, :], in1=keep[b % 2], scale=1.0,
                                                             scalar=-3.0e38, op0=ALU.add, op1=ALU.max,
                                                             accum_out=st[:, 0:1]), s, mask_made[b], rfree)
                    mask_read[b] = g
                    banks_s.free(si, g)
                    source = sc
                else:
                    g = dve(lambda e: e.reduce_max(st[:, 0:1], bank[:, :], AX_X), s)
                    source = bank[:, :]
                n = dve(lambda e: e.tensor_scalar(st[:, 1:2], st[:, 0:1], -scale, None, ALU.mult), g)
                pi, pr, pfree = prob_ring.take()
                ex = act(lambda e: e.activation(pr, source, ACT.Exp, bias=st[:, 1:2], scale=scale,
                                                accum_out=st[:, 2:3]), n, pfree)
                if masked:
                    score_ring.free(ri, ex)
                else:
                    banks_s.free(si, ex)
                rc = dve(lambda e: e.reciprocal(st[:, 3:4], st[:, 2:3]), ex)
                nm = dve(lambda e: e.tensor_scalar(pr, pr, st[:, 3:4], None, ALU.mult), rc)
                state[c, u] = (pi, pr, nm)

            def unit_transpose(c, u):
                pi, pr, nm = state[c, u]
                ti, bank, free = banks_t.take()
                for t in range(CTX // P):
                    s = pe(lambda e, t=t: e.transpose(bank[:, t * P:(t + 1) * P], pr[:, t * P:(t + 1) * P],
                                                      ident[:, :]), nm, free if t == 0 else None)
                prob_ring.free(pi, s)
                qi, pt, tfree = probT_ring.take()
                a = act(lambda e: e.copy(pt, bank[:, :].rearrange("p (a b) -> p a b", a=CTX // P)), s, tfree)
                banks_t.free(ti, a)
                state[c, u] = (qi, pt, a)

            def unit_values(c, u):
                qi, pt, a = state.pop((c, u))
                b, tile = c % NSEQ, c // NSEQ * KT + u // per_tile
                m, r0 = u // per_tile, (u % per_tile) * 2 * head_dim
                ready = kv_ready[c][KT:] if u == 0 else ()
                oi, bank, free = banks_o.take()
                rows2 = 2 * head_dim
                for t in range(CTX // P):
                    s = pe(lambda e, t=t: e.matmul(bank[r0:r0 + rows2, 0:P], v[c % 2][:, t, u * rows2:(u + 1) * rows2],
                                                   pt[:, t, :], start=(t == 0), stop=(t == CTX // P - 1)),
                           a, *((free, *ready) if t == 0 else ()))
                probT_ring.free(qi, s)
                for h in range(2):
                    lo = r0 + h * head_dim
                    hi = lo + head_dim
                    dst = qT[lo:hi, tile, b * SEQ:(b + 1) * SEQ]
                    src = bank[lo:hi, h * SEQ:(h + 1) * SEQ]
                    if q_affine:
                        o = dve(lambda e, dst=dst, src=src, lo=lo, hi=hi: e.tensor_scalar(
                            dst, src, col("bv", m, 1, lo, hi), None, ALU.add), s, load_cols)
                    else:
                        o = dve(lambda e, dst=dst, src=src: e.tensor_copy(dst, src), s)
                banks_o.free(oi, o)
                return s, o

            order = [(c, u) for c in range(steps) for u in range(pairs)]
            todo, last_o = [], None
            for n in range(len(order) + 2):
                c, u = order[n] if n < len(order) else (steps, pairs)
                if u == 0 and c + 1 < steps:
                    if masked:
                        load_mask(c + 1)
                    if (c + 1) % NSEQ == 0:
                        for name, w in zip(("k", "v"), load_weights((c + 1) // NSEQ)):
                            split_weights((c + 1) // NSEQ, name, w)
                    if c + 2 < steps:
                        landed[c + 2] = load_context(c + 2)
                    todo, total, queued = [] if c + 1 in kv_ready else kv_groups(c + 1), 2 * KT, 0
                groups = 0
                if todo:
                    due = -(-total * (u + 1) // pairs)
                    groups, queued = due - queued, due
                if n < len(order):
                    unit_scores(c, u)
                for _ in range(groups // 2):
                    todo.pop(0)()
                if 1 <= n <= len(order):
                    unit_transpose(*order[n - 1])
                for _ in range(groups - groups // 2):
                    todo.pop(0)()
                if 2 <= n:
                    last_pv[order[n - 2][0]], last_o = unit_values(*order[n - 2])
                if c + 2 < steps:
                    for k in range(KT):
                        if min(pairs // 4 + k, pairs - 1) == u:
                            split_context(c + 2, k, landed[c + 2])
            wring.closed = ()
            for i in range(SPLIT_SLOT, NW):
                wring.free(i, kv_read[steps - 1])
            return qT, last_o

        return attend if layer == 0 else (plain_groups, enter, attend)


    def pipeline(items):
        second = fourth = result = None
        for item in items + [None, None]:
            third = second() if second else None
            second = item() if item else None
            after_third = third() if third else None
            if fourth:
                result = fourth()
            fourth = after_third
        return result

    def self_attention_inputs(weights, feature_major, token_major, ring, xnT_ready):
        done = {}
        for n, dst in feature_major.items():
            w = weights[n]
            for m in range(KT):
                bi, bank, free = ring.take()
                s = project_into(bank[:, :], w, m * P, P, lambda k: xnT[:, k, :], free, *xnT_ready)
                c = act(lambda e, m=m, bank=bank, dst=dst: e.copy(dst[:, m, :], bank[:, :]), s)
                ring.free(bi, c)
                done[n] = c
            w.release(s)
        for n, dst in token_major.items():
            w = weights[n]
            for i in range(NT):
                bi, bank, free = ring.take()
                s = project_tokens(bank[:, :], lambda k, i=i: xnT[:, k, i * P:(i + 1) * P], w, 0, DIM, free,
                                   *xnT_ready)
                c = dve(lambda e, i=i, bank=bank, dst=dst: e.tensor_copy(dst[:, i, :], bank[:, :]), s)
                ring.free(bi, c)
                done[n] = c
            w.release(s)
        return done

    def broadcast_rows(bank_view, column, *after):
        return pe(lambda e: e.matmul(bank_view, column.to_broadcast([P, P]), ident[:, :], start=True, stop=True),
                  *after)

    def finish_plain(i, bank, s):
        return dve(lambda e: e.tensor_tensor(x[:, i, :], bank[:, :], x[:, i, :], ALU.add), s)

    b2_stream = Stream(sem("s_b2"))

    class Experts:

        def __init__(self, layer, n, chosen, hidden_tiles, last_rows, L):
            self.layer, self.n, self.chosen = layer, n, chosen
            self.ht = hidden_tiles
            self.rows_of = [P] * (hidden_tiles - 1) + [last_rows]
            self.aff, self.top = small_buf("aff", NT, n), small_buf("top", NT, 8)
            self.pick, self.used, self.work = (small_buf(s, NT, n) for s in ("pick", "used", "work"))
            self.red = small_buf("red", NT)
            self.choice, self.choice_i = small_buf("choice", NT, 8), small_buf("choice_i", NT, 8).bitcast(U32)
            self.slot_f = small_buf("slot_f", NT, chosen)
            self.slot = small_buf("slot", NT, chosen).bitcast(I32)
            self.rank, self.is_first, self.base, self.at_f = (small_buf(s, NT, chosen) for s in
                                                              ("rank", "is_first", "base", "at_f"))
            self.first_at, self.rest_at = (small_buf(s, NT, chosen).bitcast(I32) for s in ("first_at", "rest_at"))
            self.first_gate, self.rest_gate = (small_buf(s, NT, chosen) for s in ("first_gate", "rest_gate"))
            self.over_f, self.over = small_buf("over_f", n + 1), small_buf("over", n + 1).bitcast(I32)
            self.gates = L(NT, n)
            self.gatesT, self.b2 = L(TOK), L(DIM)
            self.ids_row, self.ids = L(P), L(P)
            self.gather = [arena[:, ARENA - (i + 1) * DIM:ARENA - i * DIM] for i in range(4)]
            self.gather_ring = Ring(list(range(4)))
            name = f"s_moe{layer}_"
            self.gather_streams = [Stream(sem(f"{name}gather{i}")) for i in range(4)]
            self.long_streams = [Stream(sem(f"{name}long{i}")) for i in range(3)]
            self.out_streams = [Stream(sem(f"{name}out{i}")) for i in range(3)]
            self.rest_streams = [Stream(sem(f"{name}rest{i}")) for i in range(3)]
            self.scatter_stream, self.ids_stream = Stream(sem(name + "scatter")), Stream(sem(name + "ids"))
            self.zero_stream = Stream(sem(name + "zero"))
            self.rows_stream = Stream(sem(name + "rows"))

        def store_rows(self, src, *after):
            self.stored_rows = transfer(sp, self.rows_stream, lambda e: e.dma_start(
                token_rows.rearrange("(i p) d -> p i d", p=P), src[:, :, :]), *after)

        def route(self, weight, bias, srcT, src_ready, ring):
            n, aff, top, red = self.n, self.aff, self.top, self.red
            bi, bank, free = ring.take()
            for i in range(NT):
                s = project_tokens(bank[:, i * n:(i + 1) * n], lambda k, i=i: srcT[:, k, i * P:(i + 1) * P],
                                   weight, 0, n, free, *src_ready)
            weight.release(s)
            r3 = bank[:, 0:NT * n].rearrange("p (i x) -> p i x", i=NT)
            a = dve(lambda e: e.tensor_tensor(aff, r3, over_middle(bias, NT), ALU.add), s, load_rows[0])
            ring.free(bi, a)
            a = dve(lambda e: e.tensor_reduce(red, aff, AX_X, ALU.max), a)
            a = dve(lambda e: e.tensor_tensor(aff, aff, over_last(red, n), ALU.subtract), a)
            a = act(lambda e: e.activation(aff, aff, ACT.Exp), a)
            a = dve(lambda e: e.tensor_reduce(red, aff, AX_X, ALU.add), a)
            a = dve(lambda e: e.reciprocal(red, red), a)
            a = dve(lambda e: e.tensor_tensor(aff, aff, over_last(red, n), ALU.mult), a)
            t = [dve(lambda e, i=i: e.max(top[:, i, :], aff[:, i, :]), a) for i in range(NT)]
            t = [dve(lambda e, i=i: e.max_index(self.choice_i[:, i, :], top[:, i, :], aff[:, i, :]), t[-1])
                 for i in range(NT)]
            a = dve(lambda e: e.tensor_copy(self.choice, self.choice_i), t[-1])
            numbers = over_middle(expert_no[:, 0:n], NT)
            for k in range(self.chosen):
                a = dve(lambda e, k=k: e.tensor_tensor(self.pick, numbers, over_last(self.choice[:, :, k], n),
                                                       ALU.is_equal), a, expert_no_ready)
                if k == 0:
                    u = dve(lambda e: e.tensor_copy(self.used, self.pick), a)
                    a = dve(lambda e: e.tensor_tensor(self.gates, self.pick, over_last(top[:, :, 0], n), ALU.mult), a)
                else:
                    u = dve(lambda e: e.tensor_tensor(self.used, self.used, self.pick, ALU.add), a, u)
                    a = dve(lambda e, k=k: e.tensor_tensor(self.pick, self.pick, over_last(top[:, :, k], n),
                                                           ALU.mult), a, u)
                    a = dve(lambda e: e.tensor_tensor(self.gates, self.gates, self.pick, ALU.add), a)
            return a, u

        def place(self, routed, ring):
            a, u = routed
            n, used = self.n, self.used
            bi, bank, free = ring.take()
            for i in range(NT):
                for j in range(i + 1):
                    s = pe(lambda e, i=i, j=j, bank=bank: e.matmul(
                        bank[:, i * n:(i + 1) * n], ones[:, :] if j < i else tri[:, :], used[:, j, :],
                        start=(j == 0), stop=(j == i)), u, free, tri_ready)
            count3 = bank[:, 0:NT * n].rearrange("p (i x) -> p i x", i=NT)
            numbers, top3 = over_middle(expert_no[:, 0:n], NT), self.top[:, :, 0:self.chosen]
            for k in range(self.chosen):
                a = dve(lambda e, k=k: e.tensor_tensor(self.pick, numbers, over_last(self.choice[:, :, k], n),
                                                       ALU.is_equal), a)
                a = dve(lambda e: e.tensor_tensor(self.work, count3, self.pick, ALU.mult), a, s)
                a = dve(lambda e: e.tensor_reduce(self.red, self.work, AX_X, ALU.add), a)
                a = dve(lambda e, k=k: e.tensor_scalar(self.rank[:, :, k], self.red, -1.0, None, ALU.add), a)
            ring.free(bi, a)
            chosen = self.choice[:, :, 0:self.chosen]
            a = dve(lambda e: e.scalar_tensor_tensor(out=self.slot_f, in0=chosen, scalar=float(CAP), in1=self.rank,
                                                     op0=ALU.mult, op1=ALU.add), a)
            self.slot_ready = dve(lambda e: e.tensor_copy(self.slot, self.slot_f), a)
            a = dve(lambda e: e.tensor_scalar(self.is_first, self.rank, float(P), None, ALU.is_lt), self.slot_ready)
            a = dve(lambda e: e.tensor_tensor(self.first_gate, self.is_first, top3, ALU.mult), a)
            a = dve(lambda e: e.tensor_tensor(self.rest_gate, top3, self.first_gate, ALU.subtract), a)
            a = dve(lambda e: e.tensor_scalar(self.base, self.rank, float(P - 1), None, ALU.min), a)
            a = dve(lambda e: e.scalar_tensor_tensor(out=self.at_f, in0=chosen, scalar=float(P), in1=self.base,
                                                     op0=ALU.mult, op1=ALU.add), a)
            a = dve(lambda e: e.tensor_copy(self.first_at, self.at_f), a)
            a = dve(lambda e: e.tensor_scalar(self.base, self.rank, -float(P), 0.0, ALU.add, ALU.max), a)
            a = dve(lambda e: e.scalar_tensor_tensor(out=self.at_f, in0=chosen, scalar=float(CAP - P), in1=self.base,
                                                     op0=ALU.mult, op1=ALU.add), a)
            self.at_ready = dve(lambda e: e.tensor_copy(self.rest_at, self.at_f), a)
            for i in range(NT):
                for k in range(self.chosen):
                    self.scattered = transfer(pool, self.scatter_stream, lambda e, i=i, k=k: e.indirect_dma_start(
                        out=ids[self.layer], out_offset=bass.IndirectOffsetOnAxis(ap=self.slot[:, i, k:k + 1], axis=0),
                        in_=token_no[:, i:i + 1], in_offset=None), self.slot_ready, token_no_ready,
                        cleared[self.layer])
            bi, bank, free = ring.take()
            for i in range(NT):
                s = pe(lambda e, i=i, bank=bank: e.matmul(bank[:, 0:n], ones[:, :], used[:, i, :], start=(i == 0),
                                                          stop=(i == NT - 1)), free)
            a = dve(lambda e, bank=bank: e.tensor_scalar(self.over_f[:, 0:n], bank[:, 0:n], -float(P), 0.0, ALU.add,
                                                         ALU.max), s)
            ring.free(bi, a)
            a = dve(lambda e: e.reduce_max(self.over_f[:, n:n + 1], self.over_f[:, 0:n], AX_X), a)
            self.over_ready = dve(lambda e: e.tensor_copy(self.over, self.over_f), a)
            bi, bank, free = ring.take()
            for i in range(NT):
                s = pe(lambda e, i=i, bank=bank: e.transpose(bank[0:n, i * P:(i + 1) * P], self.gates[:, i, :],
                                                             ident[:, :]), routed[0], free)
            self.gatesT_ready = act(lambda e, bank=bank: e.copy(self.gatesT[0:n, :], bank[0:n, :]), s)
            ring.free(bi, self.gatesT_ready)

        def second_bias(self, name, ring):
            landed = transfer(sp, b2_stream, lambda e: e.dma_start(self.b2[0:self.n, :], A[name]), *fence)
            for i in range(NT):
                bi, bank, free = ring.take()
                s = pe(lambda e, i=i, bank=bank: e.matmul(bank[:, :], self.gatesT[0:self.n, i * P:(i + 1) * P],
                                                          self.b2[0:self.n, :], start=True, stop=True),
                       self.gatesT_ready, landed, free)
                c = dve(lambda e, i=i, bank=bank: e.tensor_tensor(x[:, i, :], bank[:, :], x[:, i, :], ALU.add), s)
                ring.free(bi, c)
            self.b2_read = s

        def list_tokens(self, ring):
            n = self.n * CHUNKS
            words = self.ids_row.bitcast(I32)
            landed = transfer(sp, self.ids_stream, lambda e: e.dma_start(
                words[0:n, :], ids[self.layer].rearrange("(c p) o -> c (p o)", p=P)), self.scattered)
            ids_f = self.b2[:, 0:P]
            a = dve(lambda e: e.tensor_copy(ids_f[0:n, :], words[0:n, :]), landed, self.b2_read)
            bi, bank, free = ring.take()
            s = pe(lambda e: e.transpose(bank[:, 0:n], ids_f[0:n, :], ident[0:n, 0:n]), a, free)
            self.ids_ready = dve(lambda e: e.tensor_copy(self.ids.bitcast(I32)[:, 0:n], bank[:, 0:n]), s)
            ring.free(bi, self.ids_ready)
            self.ahead = {ex: self.gather_rows(ex * CHUNKS) for ex in range(3)}

        def gather_rows(self, chunk):
            gi, _, free = self.gather_ring.take()
            dst = self.gather[gi]
            t = transfer(pool, self.gather_streams[gi], lambda e: e.indirect_dma_start(
                out=dst, out_offset=None, in_=token_rows,
                in_offset=bass.IndirectOffsetOnAxis(ap=self.ids.bitcast(I32)[:, chunk:chunk + 1], axis=0)),
                self.ids_ready, self.stored_rows, free)
            return gi, dst, t

        def run(self, weights, activate, L, first_weights, then=None, meanwhile=None):
            ht, layer = self.ht, self.layer
            self.gather_long = [L(DIM) for _ in range(3)]
            self.out = [L(DIM) for _ in range(3)]
            self.tokT = [L(KT, P) for _ in range(2)]
            self.hid = [L(ht, P) for _ in range(2)]
            self.tokT_long, self.hid_long = L(KT, 3 * P), L(ht, 3 * P)
            assert L.at <= (ARENA - 4 * DIM if meanwhile is None else EXPERTS_END)
            ids_i = self.ids.bitcast(I32)
            ring_t, ring_up, ring_down = Ring(banks[0:2]), Ring(banks[2:6]), Ring(banks[6:8])
            gather_ring, out_ring, long_ring = self.gather_ring, Ring(list(range(3))), Ring(list(range(3)))
            tok_ring, hid_ring = Ring(self.tokT), Ring(self.hid)
            stage_end()
            gather = self.gather_rows

            long_landed = [None] * 3

            def gather_long(chunk):
                gi, _, free = long_ring.take()
                dst = self.gather_long[gi]
                t = transfer(pool, self.long_streams[gi], lambda e: e.indirect_dma_start(
                    out=dst, out_offset=None, in_=token_rows,
                    in_offset=bass.IndirectOffsetOnAxis(ap=ids_i[:, chunk:chunk + 1], axis=0)),
                    free, long_landed[gi])
                long_landed[gi] = t
                t.stand_in = lambda e: e.dma_start(dst[0:1, 0:P], token_rows[0:1, 0:P])
                return gi, dst, t

            def transpose_rows(got, dst, free, gather_ring=gather_ring):
                gi, src, landed = got
                bi, bank, bfree = ring_t.take()
                for k in range(KT):
                    s = pe(lambda e, k=k: e.transpose(bank[:, k * P:(k + 1) * P], src[:, k * P:(k + 1) * P],
                                                      ident[:, :]), landed, bfree)
                gather_ring.free(gi, s)
                c = dve(lambda e: e.tensor_copy(dst, bank[:, :].rearrange("p (a b) -> p a b", a=KT)), s, free)
                ring_t.free(bi, c)
                return c

            def up(ex, w_up, tokT, tok_ready, hid, hid_free, width):
                per_bank = 512 // width
                done = []
                for m0 in range(0, ht, per_bank):
                    ms = list(range(m0, min(ht, m0 + per_bank)))
                    got = []
                    for w in w_up:
                        bi, bank, free = ring_up.take()
                        for m in ms:
                            o = (m - m0) * width
                            s = project_into(bank[0:self.rows_of[m], o:o + width], w, m * P, self.rows_of[m],
                                             lambda k: tokT[:, k, :], free, tok_ready)
                        got.append((bi, bank, s))
                    for m in ms:
                        o, r = (m - m0) * width, self.rows_of[m]
                        done.append(activate(hid[0:r, m, :], m, r, width, [b[0:r, o:o + width] for _, b, _ in got],
                                             [s for _, _, s in got], ex, hid_free))
                    for bi, _, _ in got:
                        ring_up.free(bi, done[-1])
                for w in w_up:
                    w.release(s)
                return done, s

            def down(ex, chunk, hid, o, ready, w2, zeroed=None):
                bi, bank, free = ring_down.take()
                for m in range(ht):
                    r = self.rows_of[m]
                    s = pe(lambda e, m=m, r=r: e.matmul(bank[:, :], hid[0:r, m, o:o + P], w2.view[0:r, m, :],
                                                        start=(m == 0), stop=(m == ht - 1)), free, w2.landed, *ready)
                oi, _, ofree = out_ring.take()
                buf = self.out[oi]
                c = act(lambda e: e.copy(buf, bank[:, :]), s, ofree, *(first_stored if chunk else ()))
                ring_down.free(bi, c)
                if chunk == 0:
                    dst = expert_out[layer][ex * P:(ex + 1) * P, :]
                else:
                    row0 = ex * (CAP - P) + (chunk - 1) * P
                    dst = expert_rest[layer][row0:row0 + P, :]
                if chunk == 0:
                    t = transfer(act, self.out_streams[oi], lambda e: e.dma_start(dst, buf), c)
                else:
                    t = transfer(sp, self.rest_streams[oi], lambda e: e.dma_start(dst, buf), c, zeroed)
                out_ring.free(oi, t)
                return s

            got = self.ahead.pop(0)
            ti, tokT, tfree = tok_ring.take()
            tok_ready = transpose_rows(got, tokT, tfree)
            ahead = self.ahead
            pend = None
            for ex in range(self.n):
                w_up, w2 = first_weights[ex] if ex < len(first_weights) else weights(ex)
                hi, hid, hfree = hid_ring.take()
                done, s = up(ex, w_up, tokT, tok_ready, hid, hfree, P)
                tok_ring.free(ti, s)
                if ex + 3 < self.n:
                    ahead[ex + 3] = gather((ex + 3) * CHUNKS)
                if ex + 1 < self.n:
                    ti, tokT, tfree = tok_ring.take()
                    tok_ready = transpose_rows(ahead.pop(ex + 1), tokT, tfree)
                if pend:
                    s = down(*pend[:-1])
                    pend[5].release(s)
                    hid_ring.free(pend[6], s)
                pend = (ex, 0, hid, 0, done, w2, hi)
            s = down(*pend[:-1])
            pend[5].release(s)

            added = [None] * NT

            def combine(table, at, gate, ring, streams, bufs, then, *after):
                for i in range(NT):
                    for k in range(self.chosen):
                        gi, _, free = ring.take()
                        buf = bufs[gi]
                        t = transfer(pool, streams[gi], lambda e, i=i, k=k, buf=buf: e.indirect_dma_start(
                            out=buf, out_offset=None, in_=table,
                            in_offset=bass.IndirectOffsetOnAxis(ap=at[:, i, k:k + 1], axis=0)),
                            free, self.at_ready, long_landed[gi] if ring is long_ring else None, *after)
                        t.local = ring is long_ring
                        if t.local:
                            long_landed[gi] = t
                        c = dve(lambda e, i=i, k=k, buf=buf: e.scalar_tensor_tensor(
                            out=x[:, i, :], in0=buf, scalar=gate[:, i, k:k + 1], in1=x[:, i, :], op0=ALU.mult,
                            op1=ALU.add), t, added[i])
                        added[i] = c
                        ring.free(gi, c)
                    if then:
                        then(i, c)

            def stored():
                return [t for t in out_ring.read if t is not None]

            first_stored = stored()

            with only_if(self.over[0:1, self.n:self.n + 1], self.over_ready):
                zero = self.b2
                a = dve(lambda e: e.memset(zero, 0.0))
                zeroed = transfer(sp, self.zero_stream, lambda e: e.dma_start(
                    expert_rest[layer].rearrange("(c p) d -> p c d", p=P),
                    zero.unsqueeze(1).to_broadcast([P, self.n * (CHUNKS - 1), DIM])), a)
                for ex in range(self.n):
                    with only_if(self.over[0:1, ex:ex + 1], inner=True):
                        w_up, w2 = weights(ex)
                        free = s
                        for c in range(1, CHUNKS):
                            o = (c - 1) * P
                            tok_ready = transpose_rows(gather_long(ex * CHUNKS + c),
                                                       self.tokT_long[:, :, o:o + P], free, long_ring)
                        done, _ = up(ex, w_up, self.tokT_long, tok_ready, self.hid_long, free, 3 * P)
                        for c in range(1, CHUNKS):
                            s = down(ex, c, self.hid_long, (c - 1) * P, done, w2, zeroed)
                        w2.release(s)
                combine(expert_rest[layer], self.rest_at, self.rest_gate, long_ring, self.long_streams,
                        self.gather_long, None, zeroed, *stored())

            if meanwhile:
                meanwhile([next(s for s in reversed(q.steps) if not isinstance(s, (BeginIf, EndIf, Transfer)))
                           for q in (pe, act, dve)], first_stored + stored())
            combine(expert_out[layer], self.first_at, self.first_gate, gather_ring, self.gather_streams,
                        self.gather, then, *first_stored)
            return added


    def layer0_cross_attention():
        small_reset()
        def key_value_weights(part):
            return Weight("L0_xattn_w_kv", part), Weight("L0_xattn_w_kv", 2 + part)

        a = []

        def normalise():
            a.extend(transfer(sp, Stream(sem(f"s_x{i}")), lambda e, i=i: e.dma_start(x[:, i, :], A["x"][:, i, :]))
                     for i in range(NT))
            for slot, src in enumerate((x, xn)):
                scaled = [layer_statistics(i, src, slot, a[i]) for i in range(NT)]
                a[:] = [layer_scale(i, src, xn, slot, scaled[i]) for i in range(NT)]

        attend = cross_attention(0, 64, 64 ** -0.5, key_value_weights, False, False, normalise)
        w_q = [Weight("L0_xattn_w_q", c) for c in range(2)]
        load_late()
        xnT_ready = to_feature_major(xn, xnT, Ring(banks[4:8]), a, affine=True)
        oT, o_ready = attend(w_q, xnT_ready)
        w_out = [Weight("L0_xattn_w_out", c) for c in range(2)]
        tanh_gate = small_buf("tanh_gate", 1)
        tg = act(lambda e: e.activation(tanh_gate[:, :], row("gate"), ACT.Tanh), load_rows[0])

        def finish_gated(i, bank, s):
            a = dve(lambda e: e.tensor_tensor(xn[:, i, :], bank[:, :], row("b_out"), ALU.add), s, load_rows[0])
            return dve(lambda e: e.scalar_tensor_tensor(out=x[:, i, :], in0=xn[:, i, :], scalar=tanh_gate[:, 0:1],
                                                        in1=x[:, i, :], op0=ALU.mult, op1=ALU.add), a, tg)

        ready = multiply_and_normalise(oT, w_out, finish_gated, lambda i, a: layer_norm(i, x, xn, 0, a), xn,
                                       o_ready)
        stage_end()
        return ready

    def layer0_linear_attention(ready):
        _, _, xnT_ready = ready
        small_reset()
        W = {n: Weight("L0_attn_" + n, 0) for n in ("Wk", "Wq", "Wv", "Wo")}
        ring = Ring(banks)
        L = Layout()
        qT, vT, k_tok, yT = L(KT, TOK), L(KT, TOK), L(NT, DIM), L(KT, TOK)
        ksq = L(NT, DIM)
        done = self_attention_inputs(W, {}, {"Wk": k_tok}, ring, xnT_ready)
        G = NT * HEADS
        g = {n: small_buf("g_" + n, G) for n in ("n2", "rn", "sum", "zg", "zl", "log", "one_rho", "L", "minus_L",
                                                 "tmp")}

        def by_head(buf):
            return buf[:, :, :].rearrange("p i (h d) -> p (i h) d", h=HEADS)

        a = pool(lambda e: e.tensor_tensor(ksq[:, :, :], k_tok[:, :, :], k_tok[:, :, :], ALU.mult), done["Wk"])
        a = dve(lambda e: e.tensor_reduce(g["n2"][:, :], by_head(ksq), AX_X, ALU.add), a)
        a = act(lambda e: e.activation(g["rn"][:, :], g["n2"][:, :], ACT.Sqrt), a)
        a = dve(lambda e: e.tensor_scalar(g["rn"][:, :], g["rn"][:, :], 1e-12, None, ALU.max), a)
        a = dve(lambda e: e.reciprocal(g["rn"][:, :], g["rn"][:, :]), a)
        k_ready = dve(lambda e: e.tensor_tensor(by_head(k_tok), by_head(k_tok), over_last(g["rn"], 32), ALU.mult), a)
        a = dve(lambda e: e.tensor_reduce(g["sum"][:, :], by_head(k_tok), AX_X, ALU.add), k_ready)
        done = self_attention_inputs(W, {"Wq": qT}, {}, ring, xnT_ready)

        def gate_logit(dst, w, b, a):
            d3 = dst[:, :].rearrange("p (i h) -> p i h", i=NT)
            s3 = g["sum"][:, :].rearrange("p (i h) -> p i h", i=NT)
            a = dve(lambda e: e.tensor_tensor(d3, s3, over_middle(row(w), NT), ALU.mult), a, load_rows[0])
            return dve(lambda e: e.scalar_tensor_tensor(out=d3, in0=d3, scalar=1.0 / 32, in1=over_middle(row(b), NT),
                                                        op0=ALU.mult, op1=ALU.add), a)

        b = gate_logit(g["zg"], "W_gamma", "b_gamma", a)
        a = gate_logit(g["zl"], "W_lambda", "b_lambda", a)
        a = act(lambda e: e.activation(g["zl"][:, :], g["zl"][:, :], ACT.Exp), a)
        b = act(lambda e: e.activation(g["zg"][:, :], g["zg"][:, :], ACT.Exp, scale=-1.0), b)
        a = dve(lambda e: e.tensor_scalar(g["zl"][:, :], g["zl"][:, :], 1.0, None, ALU.add), a)
        b = dve(lambda e: e.tensor_scalar(g["zg"][:, :], g["zg"][:, :], 1.0, None, ALU.add), b)
        a = dve(lambda e: e.tensor_tensor(g["tmp"][:, :], g["zl"][:, :], g["zg"][:, :], ALU.mult), a, b)
        b = dve(lambda e: e.reciprocal(g["one_rho"][:, :], g["tmp"][:, :]), a)
        b = dve(lambda e: e.tensor_scalar(g["one_rho"][:, :], g["one_rho"][:, :], -1.0, 1.0, ALU.mult, ALU.add), b)
        a = act(lambda e: e.activation(g["log"][:, :], g["tmp"][:, :], ACT.Ln), a)
        done.update(self_attention_inputs(W, {"Wv": vT}, {}, ring, xnT_ready))
        bi, bank, free = ring.take()
        s = pe(lambda e, bank=bank: e.matmul(bank[:, 0:G], upto[:, :], g["log"][:, :], start=True, stop=True), a, free,
               upto_ready)
        minus_ready = dve(lambda e, bank=bank: e.tensor_copy(g["minus_L"][:, :], bank[:, 0:G]), s)
        L_ready = dve(lambda e: e.tensor_scalar(g["L"][:, :], g["minus_L"][:, :], -1.0, None, ALU.mult), minus_ready)
        ring.free(bi, minus_ready)
        k_ready = pool(lambda e: e.tensor_tensor(by_head(k_tok), by_head(k_tok), over_last(g["one_rho"], 32), ALU.mult),
                       b, k_ready)

        ring_a, ring_l, ring_y = ring.part(0, 3), ring.part(3, 6), ring.part(6, 8)
        decay_ring = Ring([L(KT, P) for _ in range(4)])

        def values(i, r, j, di, dec, ready):
            yi, ybank, yfree = ring_y.take()
            for hm in range(KT):
                h = 4 * hm + j
                s = pe(lambda e, hm=hm, h=h: e.matmul(ybank[r:r + 32, hm * P:(hm + 1) * P],
                                                      k_tok[:, i, 32 * h:32 * h + 32], dec[:, hm, :],
                                                      start=True, stop=True), ready, k_ready, yfree)
            decay_ring.free(di, s)
            y_ready = act(lambda e: e.copy(yT[r:r + 32, :, i * P:(i + 1) * P],
                                           ybank[r:r + 32, :].rearrange("p (a b) -> p a b", a=KT)), s)
            ring_y.free(yi, y_ready)
            return y_ready

        def decayed(i, r, j, di, dec, ex, s2, ai, abank):
            a = dve(lambda e: e.tensor_tensor(dec, abank[:, :].rearrange("p (a b) -> p a b", a=KT), dec, ALU.mult),
                    ex, s2)
            ring_a.free(ai, a)
            return lambda: lambda: values(i, r, j, di, dec, a)

        def scores(i, j):
            r = 32 * j
            li, lbank, lfree = ring_l.take()
            for hm in range(KT):
                c = i * HEADS + 4 * hm + j
                s = broadcast_rows(lbank[:, hm * P:(hm + 1) * P], g["L"][:, c:c + 1], L_ready, lfree)
            ai, abank, afree = ring_a.take()
            for hm in range(KT):
                s2 = pe(lambda e, hm=hm: e.matmul(
                    abank[:, hm * P:(hm + 1) * P], vT[r:r + 32, hm, i * P:(i + 1) * P],
                    qT[r:r + 32, hm, i * P:(i + 1) * P], start=True, stop=True),
                        afree, done["Wq"], done["Wv"])
            di, dec, dfree = decay_ring.take()
            for hm in range(KT):
                c = i * HEADS + 4 * hm + j
                a = dve(lambda e, hm=hm, c=c: e.scalar_tensor_tensor(
                    out=dec[:, hm, :], in0=lbank[:, hm * P:(hm + 1) * P], scalar=g["minus_L"][:, c:c + 1],
                    in1=mask_ji[:, :], op0=ALU.add, op1=ALU.add), s, dfree, masks_ready, minus_ready)
            ring_l.free(li, a)
            ex = act(lambda e: e.activation(dec, dec, ACT.Exp), a)
            return lambda: decayed(i, r, j, di, dec, ex, s2, ai, abank)

        y_ready = pipeline([lambda i=i, j=j: scores(i, j) for i in range(NT) for j in range(4)])

        ready = multiply_and_normalise(yT, [W["Wo"]], finish_plain, lambda i, a: rms_norm(
            i, xn, xn, row("gamma1"), layer_norm(i, x, xn, 0, a)), xn, y_ready)
        stage_end()
        return ready

    def layer0_self_attention(ready):
        _, _, xnT_ready = ready
        small_reset()
        W = {n: Weight("L0_ffn_" + n, 0) for n in ("q1", "q2", "k1", "k2")}
        W_v = [Weight("L0_ffn_v", c) for c in range(2)]
        W_o = [Weight("L0_ffn_o", c) for c in range(2)]
        L = Layout()
        attn_out = xn
        q1, q2, k1, k2 = (L(KT, TOK) for _ in range(4))
        v_tok = L(NT, 2 * DIM)
        cos, sin, ang = L(SEQ), L(SEQ), L(SEQ)
        rope_ring = Ring([[L(DIM) for _ in range(4)]])
        soft_ring = Ring([L(KT, P) for _ in range(3)])
        probT_ring = Ring([L(KT, P) for _ in range(2)])
        pos = L(SEQ)
        a = pool(lambda e: e.iota(ang.bitcast(I32), pattern=[[1, SEQ]], base=0, channel_multiplier=0))
        a = dve(lambda e: e.tensor_copy(pos, ang.bitcast(I32)), a)
        ang_done = dve(lambda e: e.tensor_scalar(ang, pos, col("theta"), None, ALU.mult), a, load_cols)
        PI = float(np.pi)
        ROUND = 1.5 * 2.0 ** 23
        C1 = float(np.float32(6.28125))
        C2 = float(np.frombuffer((np.frombuffer(np.float32(2 * np.pi - C1).tobytes(), np.uint32)
                                  & np.uint32(0xFFFFF000)).tobytes(), np.float32)[0])
        C3 = float(np.float32(2 * np.pi - C1 - C2))
        turns = L(SEQ)

        def sine(dst, shift, a):
            a = dve(lambda e: e.tensor_scalar(turns, ang, 1.0 / (2 * PI), shift / (2 * PI), ALU.mult, ALU.add), a)
            a = dve(lambda e: e.tensor_scalar(turns, turns, ROUND, None, ALU.add), a)
            a = dve(lambda e: e.tensor_scalar(turns, turns, -ROUND, None, ALU.add), a)
            src = ang
            for c in (C1, C2, C3):
                a = dve(lambda e, c=c, src=src: e.scalar_tensor_tensor(out=dst, in0=turns, scalar=-c, in1=src,
                                                                       op0=ALU.mult, op1=ALU.add), a)
                src = dst
            if shift:
                a = dve(lambda e: e.tensor_scalar(dst, dst, shift, None, ALU.add), a)
            a = dve(lambda e: e.tensor_scalar(dst, dst, PI, -PI, ALU.min, ALU.max), a)
            return act(lambda e: e.activation(dst, dst, ACT.Sin), a), a

        sin_ready, a = sine(sin, 0.0, ang_done)
        cos_ready, a = sine(cos, PI / 2, a)

        ring = Ring(banks)

        rope_cos, rope_sin = over_middle(cos, NSEQ), over_middle(sin, NSEQ)

        def by_seq(ap):
            return ap.rearrange("p (b s) -> p b s", b=NSEQ)

        for wa, wb, o1, o2, ba, bb in (("q1", "q2", q1, q2, "q_b1", "q_b2"), ("k1", "k2", k1, k2, "k_b1", "k_b2")):
            for m in range(KT):
                ai, abank, free = ring.take()
                s1 = project_into(abank[:, :], W[wa], m * P, P, lambda k: xnT[:, k, :], free, *xnT_ready)
                bi, bbank, free = ring.take()
                s2 = project_into(bbank[:, :], W[wb], m * P, P, lambda k: xnT[:, k, :], free, *xnT_ready)
                W[wa].release(s1)
                W[wb].release(s2)
                ri, (ta, tb, tc, td), rfree = rope_ring.take()
                e1 = act(lambda e, m=m, abank=abank, ta=ta, ba=ba: e.activation(ta, abank[:, :], ACT.Identity,
                                                                                bias=col(ba, m)), s1, rfree, load_cols)
                e2 = act(lambda e, m=m, bbank=bbank, tb=tb, bb=bb: e.activation(tb, bbank[:, :], ACT.Identity,
                                                                                bias=col(bb, m)), s2)
                ring.free(ai, e1)
                ring.free(bi, e2)
                c1 = dve(lambda e, m=m, o1=o1, ta=ta: e.tensor_tensor(by_seq(o1[:, m, :]), by_seq(ta), rope_cos,
                                                                      ALU.mult), e1, cos_ready)
                c2 = pool(lambda e, tb=tb, tc=tc: e.tensor_tensor(by_seq(tc), by_seq(tb), rope_sin, ALU.mult), e2,
                          sin_ready, rfree)
                c3 = dve(lambda e, m=m, o2=o2, ta=ta: e.tensor_tensor(by_seq(o2[:, m, :]), by_seq(ta), rope_sin,
                                                                      ALU.mult), e1, sin_ready)
                c4 = pool(lambda e, tb=tb, td=td: e.tensor_tensor(by_seq(td), by_seq(tb), rope_cos, ALU.mult), e2,
                          cos_ready)
                c5 = dve(lambda e, m=m, o1=o1, tc=tc: e.tensor_tensor(o1[:, m, :], o1[:, m, :], tc, ALU.subtract), c1,
                         c2)
                qk_ready = dve(lambda e, m=m, o2=o2, td=td: e.tensor_tensor(o2[:, m, :], o2[:, m, :], td, ALU.add), c3,
                               c4)
                rope_ring.free(ri, qk_ready)
        for i in range(NT):
            for n in range(2):
                bi, bank, free = ring.take()
                s = project_tokens(bank[:, :], lambda k, i=i: xnT[:, k, i * P:(i + 1) * P], W_v[n], 0, DIM, free,
                                   *xnT_ready)
                v_ready = act(lambda e, i=i, n=n, bank=bank: e.copy(v_tok[:, i, n * DIM:(n + 1) * DIM], bank[:, :]), s)
                ring.free(bi, v_ready)
                W_v[n].release(s)
        oT = L(8, TOK)
        mx, sm = small_buf("mx", 4, 4), small_buf("sm", 4, 4)
        ring_s, ring_t, ring_o = ring.part(0, 3), ring.part(3, 5), ring.part(5, 8)
        mask_q = over_middle(mask_ij[:, :], KT)

        def scores(n, i, j):
            r, u = 32 * j, n % 4
            si, sbank, sfree = ring_s.take()
            for hm in range(KT):
                for half, (qq, kk) in enumerate(((q1, k1), (q2, k2))):
                    s = pe(lambda e, hm=hm, qq=qq, kk=kk, half=half: e.matmul(
                        sbank[:, hm * P:(hm + 1) * P], qq[r:r + 32, hm, i * P:(i + 1) * P],
                        kk[r:r + 32, hm, i * P:(i + 1) * P], start=(half == 0), stop=(half == 1)),
                           sfree, qk_ready)
            pi, pr, pfree = soft_ring.take()
            s3 = sbank[:, :].rearrange("p (a b) -> p a b", a=KT)
            a = dve(lambda e: e.tensor_tensor(pr, s3, mask_q, ALU.add), s, pfree)
            ring_s.free(si, a)
            a = dve(lambda e: e.tensor_reduce(mx[:, u, :], pr, AX_X, ALU.max), a)
            a = dve(lambda e: e.tensor_scalar(mx[:, u, :], mx[:, u, :], -(64 ** -0.5), None, ALU.mult), a)
            for hm in range(KT):
                ex = act(lambda e, hm=hm: e.activation(pr[:, hm, :], pr[:, hm, :], ACT.Exp, bias=mx[:, u, hm:hm + 1],
                                                       scale=64 ** -0.5, accum_out=sm[:, u, hm:hm + 1]), a)
            return lambda: normalised(i, j, u, pi, pr, ex)

        def normalised(i, j, u, pi, pr, ex):
            a = dve(lambda e: e.reciprocal(sm[:, u, :], sm[:, u, :]), ex)
            a = pool(lambda e: e.tensor_tensor(pr, pr, over_last(sm[:, u, :], P), ALU.mult), a)
            return lambda: transposed(i, j, pi, pr, a)

        def transposed(i, j, pi, pr, a):
            ti, tbank, tfree = ring_t.take()
            for hm in range(KT):
                s = pe(lambda e, hm=hm: e.transpose(tbank[:, hm * P:(hm + 1) * P], pr[:, hm, :], ident[:, :]), a,
                       tfree)
            soft_ring.free(pi, s)
            qi, pt, qfree = probT_ring.take()
            c = act(lambda e: e.copy(pt, tbank[:, :].rearrange("p (a b) -> p a b", a=KT)), s, qfree)
            ring_t.free(ti, c)
            return lambda: attended(i, j, qi, pt, c)

        def attended(i, j, qi, pt, c):
            oi, obank, ofree = ring_o.take()
            r = (j % 2) * 64
            for hm in range(KT):
                h = 4 * hm + j
                s = pe(lambda e, hm=hm, h=h: e.matmul(obank[r:r + 64, hm * P:(hm + 1) * P],
                                                      v_tok[:, i, 64 * h:64 * h + 64], pt[:, hm, :],
                                                      start=True, stop=True), c, ofree, v_ready)
            probT_ring.free(qi, s)
            o3 = oT[r:r + 64, j // 2::2, i * P:(i + 1) * P]
            vb = cols[r:r + 64, COLS["v_b"][0] + j // 2:COLS["v_b"][0] + 8:2]
            o = dve(lambda e: e.tensor_tensor(o3, obank[r:r + 64, :].rearrange("p (a b) -> p a b", a=KT),
                                              over_last(vb, P), ALU.add), s)
            ring_o.free(oi, o)
            return o

        o_ready = pipeline([lambda n=n: scores(n, n // 4, n % 4) for n in range(NT * 4)])

        def finish_attention(i, bank, s):
            a = dve(lambda e: e.tensor_tensor(attn_out[:, i, :], bank[:, :], xn[:, i, :], ALU.add), s)
            return dve(lambda e: e.tensor_tensor(attn_out[:, i, :], attn_out[:, i, :], row("o_b"), ALU.add), a)

        an = q1
        ready = multiply_and_normalise(oT, W_o, finish_attention, lambda i, a: rms_norm(
            i, attn_out, an, row("gamma2"), a), an, o_ready)
        stage_end()
        return ready

    def layer0_experts(ready):
        _, an_ready, anT_ready = ready
        small_reset()
        KV_SLOTS = (0, 1)
        wring.closed = KV_SLOTS
        W_sh = [Weight("L0_ffn_sh_w1", 0), Weight("L0_ffn_sh_w2", 0)]
        router_w = Weight("router_w", 0)

        def weights(ex):
            w1, w2 = Weight("L0_ffn_re_w1", ex), Weight("L0_ffn_re_w2", ex)
            return (w1,), w2

        first_weights = [weights(0)]

        def key_value_weights(part):
            return Weight("L1_xattn_Wk", part, KV_SLOTS[0]), Weight("L1_xattn_Wv", part, KV_SLOTS[1])

        plain_groups, enter, attend = cross_attention(1, 32, 32 ** -0.5, key_value_weights, True, True)
        L = Layout()
        attn_out, an, anT = xn, L(NT, DIM), xnT
        for i in range(NT):
            a = pool(lambda e, i=i: e.tensor_tensor(attn_out[:, i, :], attn_out[:, i, :], an[:, i, :], ALU.add),
                     an_ready[i])
            a = pool(lambda e, i=i: e.tensor_tensor(x[:, i, :], attn_out[:, i, :], x[:, i, :], ALU.add), a)
            x_ready = pool(lambda e, i=i: e.tensor_tensor(x[:, i, :], x[:, i, :], row("sh_b2"), ALU.add), a)

        experts = Experts(0, E0, TOP0, HT0, P, L)
        gates_ready = experts.route(router_w, row("router_b"), anT, anT_ready, Ring(banks[7:8]))
        experts.store_rows(an, *an_ready)

        mark = L.at
        hid = L(KT, TOK)
        up_ring, down_ring = Ring(banks[0:4]), Ring(banks[4:8])
        down_ring.free(3, gates_ready[0])
        h_ready = []
        for m in range(KT):
            bi, bank, free = up_ring.take()
            s = project_into(bank[:, :], W_sh[0], m * P, P, lambda k: anT[:, k, :], free)
            h_ready.append(act(lambda e, m=m, bank=bank: e.activation(hid[:, m, :], bank[:, :], ACT.Gelu,
                                                                      bias=col("sh_b1", m)), s))
            up_ring.free(bi, h_ready[-1])
        W_sh[0].release(s)
        keys, values = plain_groups(up_ring)
        for g in keys:
            g()
        experts.place(gates_ready, down_ring)
        for i in range(NT):
            bi, bank, free = down_ring.take()
            s = project_tokens(bank[:, :], lambda k, i=i: hid[:, k, i * P:(i + 1) * P], W_sh[1], 0, DIM, free,
                               *h_ready)
            c = dve(lambda e, i=i, bank=bank: e.tensor_tensor(x[:, i, :], bank[:, :], x[:, i, :], ALU.add), s,
                    x_ready)
            down_ring.free(bi, c)
        W_sh[1].release(s)
        experts.second_bias("L0_ffn_re_b2", down_ring)
        for g in values:
            g()
        first_weights.append(weights(1))
        experts.list_tokens(up_ring)

        def activate(h, m, rows_, cols_, views, ready, ex, hfree):
            return act(lambda e: e.activation(h, views[0], ACT.Gelu, bias=col("re_b1", HT0 * ex + m)), *ready, hfree)

        f = FeatureMajor(xn, xnT, Ring(banks[4:8]))
        X = {}

        groups = []

        def second_context(steps, stores):
            groups.extend(enter(steps, stores))
            X["Wq"] = Weight("L1_xattn_Wq", 0)
            for _ in range(KT):
                groups.pop(0)()

        def normalise(i, a):
            normed.append(layer_norm(i, x, xn, 0, a))
            groups.pop(0)()

        normed = []
        experts.run(weights, activate, Layout(mark), first_weights,
                    normalise, second_context)
        for i in range(NT):
            f.tile(i, normed[i])
        xnT_ready = f.finish()
        stage_end()
        return X, attend, xnT_ready

    def layer1_cross_attention(ready):
        X, attend, xnT_ready = ready
        small_reset()
        oT, o_ready = attend([X["Wq"]], xnT_ready)

        X["Wo"] = Weight("L1_xattn_Wo", 0)

        def finish_bias(i, bank, s):
            a = dve(lambda e: e.tensor_tensor(xn[:, i, :], bank[:, :], row("bo"), ALU.add), s)
            return dve(lambda e: e.tensor_tensor(x[:, i, :], xn[:, i, :], x[:, i, :], ALU.add), a)

        ready = multiply_and_normalise(oT, [X["Wo"]], finish_bias, lambda i, a: layer_norm(i, x, xn, 0, a), xn,
                                       o_ready)
        stage_end()
        return ready

    def layer1_lstm(ready):
        _, _, xnT_ready = ready
        small_reset()
        W = {n: Weight("L1_attn_" + n, 0) for n in ("Wq", "Wk", "Wv", "Wo", "Wifg", "Wdown")}
        L = Layout()
        qT, kT, v_tok, o_tok, h_tok = L(4, TOK), L(4, TOK), L(NT, DIM), L(NT, DIM), L(NT, DIM)
        ring = Ring(banks)
        NH, CAP = 4, 15.0
        ifg = small_buf("ifg", NT, 8)
        bi, bank, free = ring.take()
        for i in range(NT):
            s = project_tokens(bank[:, i * 8:(i + 1) * 8], lambda k, i=i: xnT[:, k, i * P:(i + 1) * P], W["Wifg"], 0, 8,
                               free, *xnT_ready)
        W["Wifg"].release(s)
        b3 = bank[:, 0:8 * NT].rearrange("p (i x) -> p i x", i=NT)
        a = dve(lambda e: e.tensor_tensor(ifg, b3, over_middle(row("b_ifg"), NT), ALU.add), s)
        ring.free(bi, a)
        a = act(lambda e: e.activation(ifg, ifg, ACT.Tanh, scale=1.0 / CAP), a)
        ifg_ready = dve(lambda e: e.tensor_scalar(ifg, ifg, CAP, None, ALU.mult), a)
        lsf = small_buf("lsf", NT, NH)
        a = act(lambda e: e.activation(lsf, ifg[:, :, 4:8], ACT.Exp, scale=-1.0), ifg_ready)
        a = dve(lambda e: e.tensor_scalar(lsf, lsf, 1.0, None, ALU.add), a)
        a = act(lambda e: e.activation(lsf, lsf, ACT.Ln), a)
        bi, bank, free = ring.take()
        s = pe(lambda e, bank=bank: e.matmul(bank[:, 0:NT * NH], upto[:, :], lsf.rearrange("p i h -> p (i h)"),
                                             start=True, stop=True), a, free)
        nlf, gj = small_buf("nlf", NT, NH), small_buf("gj", NT, NH)
        nlf_ready = dve(lambda e, bank=bank: e.tensor_copy(nlf.rearrange("p i h -> p (i h)"), bank[:, 0:NT * NH]), s)
        ring.free(bi, nlf_ready)
        gj_ready = dve(lambda e: e.tensor_tensor(gj, ifg[:, :, 0:4], nlf, ALU.add), nlf_ready)
        done = self_attention_inputs(W, {"Wq": qT, "Wk": kT}, {"Wv": v_tok}, ring, xnT_ready)
        gated = []
        for i in range(NT):
            bi, bank, free = ring.take()
            s = project_tokens(bank[:, :], lambda k, i=i: xnT[:, k, i * P:(i + 1) * P], W["Wo"], 0, DIM, free)
            o_done = act(lambda e, i=i, bank=bank: e.activation(o_tok[:, i, :], bank[:, :], ACT.Sigmoid), s)
            ring.free(bi, o_done)
            gated.append(pool(lambda e, i=i: e.tensor_tensor(o_tok[:, i, :], o_tok[:, i, :], row("norm_w"), ALU.mult),
                              o_done, load_rows[0]))
        W["Wo"].release(s)
        D_ring, C_ring, CT_ring = (Ring([L(NH, P) for _ in range(2)]) for _ in range(3))
        ring_g, ring_s, ring_t, ring_h = (ring.part(2 * i, 2 * i + 2) for i in range(4))
        top, gate_top, row_sum, norm = (small_buf(n, NT, NH) for n in ("top", "gate_top", "row_sum", "norm"))
        head_stats = small_buf("head_stats", NT * NH, 6)
        head_mv, head_rstd = small_buf("head_mv", NT * NH, 2), small_buf("head_rstd", NT * NH)
        mask_h = over_middle(mask_ij[:, :], NH)

        def gates_and_scores(i):
            gi, gbank, gfree = ring_g.take()
            for h in range(NH):
                s = broadcast_rows(gbank[:, h * P:(h + 1) * P], gj[:, i, h:h + 1], gj_ready, gfree)
            si, sbank, sfree = ring_s.take()
            for h in range(NH):
                s2 = pe(lambda e, h=h: e.matmul(sbank[:, h * P:(h + 1) * P], qT[:, h, i * P:(i + 1) * P],
                                                kT[:, h, i * P:(i + 1) * P], start=True, stop=True),
                        sfree, done["Wq"], done["Wk"])
            di, D, dfree = D_ring.take()
            g3, s3 = (b[:, :].rearrange("p (a b) -> p a b", a=NH) for b in (gbank, sbank))
            a = dve(lambda e: e.tensor_tensor(D, g3, mask_h, ALU.add), s, dfree)
            ring_g.free(gi, a)
            a = dve(lambda e: e.tensor_reduce(top[:, i, :], D, AX_X, ALU.max), a)
            a = dve(lambda e: e.tensor_scalar(top[:, i, :], top[:, i, :], -1.0, None, ALU.mult), a)
            for h in range(NH):
                d = act(lambda e, h=h: e.activation(D[:, h, :], D[:, h, :], ACT.Exp, bias=top[:, i, h:h + 1]), a)
            a = dve(lambda e: e.tensor_tensor(gate_top[:, i, :], top[:, i, :], nlf[:, i, :], ALU.add), a)
            m = act(lambda e: e.activation(gate_top[:, i, :], gate_top[:, i, :], ACT.Exp), a)
            return lambda: weighted(i, di, D, si, s3, d, m, s2)

        def weighted(i, di, D, si, s3, d, m, s2):
            ci, C, cfree = C_ring.take()
            a = dve(lambda e: e.scalar_tensor_tensor(out=C, in0=s3, scalar=128 ** -0.5, in1=D, op0=ALU.mult,
                                                     op1=ALU.mult), d, s2, cfree)
            c_ready = a
            D_ring.free(di, a)
            ring_s.free(si, a)
            a = dve(lambda e: e.tensor_reduce(row_sum[:, i, :], C, AX_X, ALU.add), a)
            a = dve(lambda e: e.scalar_tensor_tensor(out=norm[:, i, :], in0=row_sum[:, i, :], scalar=-1.0,
                                                     in1=row_sum[:, i, :], op0=ALU.mult, op1=ALU.max), a)
            a = dve(lambda e: e.tensor_tensor(norm[:, i, :], norm[:, i, :], gate_top[:, i, :], ALU.max), a, m)
            a = dve(lambda e: e.tensor_scalar(norm[:, i, :], norm[:, i, :], 1e-6, None, ALU.add), a)
            rn = dve(lambda e: e.reciprocal(norm[:, i, :], norm[:, i, :]), a)
            return lambda: transposed(i, ci, C, c_ready, rn)

        def transposed(i, ci, C, c_ready, rn):
            ti, tbank, tfree = ring_t.take()
            for h in range(NH):
                s = pe(lambda e, h=h: e.transpose(tbank[:, h * P:(h + 1) * P], C[:, h, :], ident[:, :]), c_ready,
                       tfree)
            C_ring.free(ci, s)
            ui, CT, ufree = CT_ring.take()
            c = act(lambda e: e.copy(CT, tbank[:, :].rearrange("p (a b) -> p a b", a=NH)), s, ufree)
            ring_t.free(ti, c)
            return lambda: hidden(i, ui, CT, c, rn)

        def hidden(i, ui, CT, c, rn):
            hi, hbank, hfree = ring_h.take()
            for h in range(NH):
                s = pe(lambda e, h=h: e.matmul(hbank[:, h * P:(h + 1) * P], CT[:, h, :],
                                               v_tok[:, i, h * P:(h + 1) * P], start=True, stop=True), c, hfree,
                       done["Wv"])
            CT_ring.free(ui, s)
            h3 = h_tok[:, i, :].rearrange("p (a b) -> p a b", a=NH)
            a = dve(lambda e: e.tensor_tensor(h3, hbank[:, :].rearrange("p (a b) -> p a b", a=NH),
                                              over_last(norm[:, i, :], P), ALU.mult), s, rn)
            ring_h.free(hi, a)
            for h in range(NH):
                a2 = dve(lambda e, h=h: e.bn_stats(head_stats[:, i * NH + h, :], h3[:, h, :]), a)
            for h in range(NH):
                a = dve(lambda e, h=h: e.bn_aggr(head_mv[:, i * NH + h, :], head_stats[:, i * NH + h, :]), a2)
            return a

        h_stats = pipeline([lambda i=i: gates_and_scores(i) for i in range(NT)])
        r = inverse_root(head_rstd[:, :], head_mv[:, :, 1], 1e-6, h_stats)
        ho_ready = []
        for i in range(NT):
            for h in range(NH):
                hv, n = h_tok[:, i, h * P:(h + 1) * P], i * NH + h
                a = dve(lambda e, hv=hv, n=n: e.tensor_scalar(hv, hv, head_mv[:, n, 0:1], head_rstd[:, n:n + 1],
                                                              ALU.subtract, ALU.mult), r)
            ho_ready.append(pool(lambda e, i=i: e.tensor_tensor(h_tok[:, i, :], h_tok[:, i, :], o_tok[:, i, :],
                                                                ALU.mult), a, gated[i]))
        hT = L(4, TOK)
        hT_ready = to_feature_major(h_tok, hT, Ring(banks[0:4]), ho_ready)
        ready = multiply_and_normalise(hT, [W["Wdown"]], finish_plain, lambda i, a: layer_norm(i, x, xn, 0, a), xn,
                                       *hT_ready)
        stage_end()
        return ready

    def layer1_experts(ready):
        x_ready, a, xnT_ready = ready
        small_reset()
        gate_w = Weight("gate_w", 0)
        L = Layout()
        SLOT1 = HT1 * DIM
        slots1 = [L(SLOT1) for _ in range(3)]
        slots1 += [wmem[:, i * SLOT1:(i + 1) * SLOT1] for i in range(NW * SLOT // SLOT1)]
        entered = list(fence)
        streams1 = [Stream(sem(f"s_expert{i}")) for i in range(len(slots1))]
        ring1 = Ring(slots1)

        class Expert1Weight:

            def __init__(self, name, ex):
                self.i, buf, read = ring1.take()
                assert read != "held", name
                if name == "w2":
                    self.view = buf.rearrange("p (k n) -> p k n", k=HT1)
                    full = (HT1 - 1) * DIM
                    transfer(sp, streams1[self.i], lambda e: e.dma_start(buf[:, 0:full], A["L1_w2_full"][ex]), read,
                             *entered)
                    self.landed = transfer(sp, streams1[self.i], lambda e: e.dma_start(
                        buf[0:LAST1, full:full + DIM], A["L1_w2_last"][ex]), read, *entered)
                else:
                    n = KT * INTER1
                    self.view = buf[:, 0:n].rearrange("p (k n) -> p k n", k=KT)
                    self.landed = transfer(sp, streams1[self.i], lambda e: e.dma_start(
                        buf[:, 0:n], A["L1_" + name][ex]), read, *entered)
                ring1.free(self.i, "held")

            def release(self, step):
                ring1.free(self.i, step)

        def weights(ex):
            return (Expert1Weight("w1", ex), Expert1Weight("w3", ex)), Expert1Weight("w2", ex)

        shared_weights = [[Weight("L1_ffn_" + n, gidx) for n in ("sw1", "sw3", "sw2")] for gidx in range(2)]
        first_weights = weights(0)
        experts = Experts(1, E1, TOP1, HT1, LAST1, L)
        gates_ready = experts.route(gate_w, row("gate_b"), xnT, xnT_ready, Ring(banks[7:8]))
        experts.store_rows(xn, *a)
        for i in range(NT):
            c = pool(lambda e, i=i: e.tensor_tensor(x[:, i, :], x[:, i, :], row("sb2"), ALU.add), *a)
        x_ready = c
        up_ring, down_ring = Ring(banks[0:4]), Ring(banks[4:8])
        down_ring.free(3, gates_ready[0])
        NHID = 8
        mark = L.at
        hid_ring = Ring([L(TOK) for _ in range(NHID)])
        shared_silu = [L(TOK) for _ in range(3)]
        silu_ring = Ring(shared_silu)

        def hidden_tile(w1, w3, j, b1, b3):
            ai, abank, afree = up_ring.take()
            s1 = project_into(abank[:, :], w1, j * P, P, lambda k: xnT[:, k, :], afree)
            bi, bbank, bfree = up_ring.take()
            s2 = project_into(bbank[:, :], w3, j * P, P, lambda k: xnT[:, k, :], bfree)
            ti, tmp, tfree = silu_ring.take()
            c1 = act(lambda e: e.activation(tmp, abank[:, :], ACT.Silu, bias=b1), s1, tfree)
            up_ring.free(ai, c1)
            hi, h, hfree = hid_ring.take()
            c2 = dve(lambda e: e.scalar_tensor_tensor(out=h, in0=bbank[:, :], scalar=b3, in1=tmp, op0=ALU.add,
                                                      op1=ALU.mult), s2, c1, hfree)
            up_ring.free(bi, c2)
            silu_ring.free(ti, c2)
            return hi, h, c2, s2

        def down1(parts):
            for i in range(NT):
                bi, bank, free = down_ring.take()
                for n, (hi, h, ready, w2, j) in enumerate(parts):
                    s = pe(lambda e, n=n, h=h, w2=w2, j=j, i=i, bank=bank: e.matmul(
                        bank[:, :], h[:, i * P:(i + 1) * P], w2.view[:, j, :],
                        start=(n == 0), stop=(n == len(parts) - 1)), free, ready, w2.landed)
                    if i == NT - 1:
                        hid_ring.free(hi, s)
                        w2.release(s)
                c = dve(lambda e, i=i, bank=bank: e.tensor_tensor(x[:, i, :], bank[:, :], x[:, i, :], ALU.add), s,
                        x_ready)
                down_ring.free(bi, c)
            return s

        pend = None
        for gidx in range(3):
            if gidx < 2:
                w1, w3, w2 = shared_weights[gidx]
            else:
                w1, w3, w2 = (Weight("L1_ffn_" + n, gidx) for n in ("sw1", "sw3", "sw2"))
            parts = []
            for j in range(4 if gidx < 2 else 3):
                t = 4 * gidx + j
                hi, h, ready, s = hidden_tile(w1, w3, j, col("sb1", t), col("sb3", t))
                parts.append((hi, h, ready, w2, j))
            w1.release(s)
            w3.release(s)
            if gidx == 1:
                experts.place(gates_ready, down_ring)
            if gidx > 0:
                down1(pend)
            pend = parts
            if gidx == 2:
                experts.second_bias("L1_ffn_b2", down_ring)
                experts.list_tokens(up_ring)
        shared_done = down1(pend)
        for i in range(3, len(slots1)):
            ring1.free(i, shared_done)

        L = Layout(mark)
        expert_silu = Ring([L(3 * P) for _ in range(3)])
        def activate(h, m, rows_, cols_, views, ready, ex, hfree):
            ti, tmp, tfree = expert_silu.take()
            b1, b3 = col("b1", HT1 * ex + m, 1, 0, rows_), col("b3", HT1 * ex + m, 1, 0, rows_)
            a = act(lambda e: e.activation(tmp[0:rows_, 0:cols_], views[0], ACT.Silu, bias=b1), *ready, tfree)
            c = dve(lambda e: e.scalar_tensor_tensor(out=h, in0=views[1], scalar=b3, in1=tmp[0:rows_, 0:cols_],
                                                     op0=ALU.add, op1=ALU.mult), *ready, a, hfree)
            expert_silu.free(ti, c)
            return c

        return experts.run(weights, activate, L, [first_weights])

    ready = layer0_cross_attention()
    ready = layer0_linear_attention(ready)
    ready = layer0_self_attention(ready)
    ready = layer0_experts(ready)
    ready = layer1_cross_attention(ready)
    ready = layer1_lstm(ready)
    x_ready = layer1_experts(ready)

    stored = [transfer(sp, Stream(sem(f"s_out{i}")), lambda e, i=i: e.dma_start(out_dram[:, i, :], x[:, i, :]),
                       x_ready[i]) for i in range(NT)]
    sp(lambda e: e.nop(), *stored, *cleared.values())

    for q in (pe, dve, act, pool, sp):
        q.number()
    block = ctx.enter_context(nc.Block())

    @block.sync
    def _(e):
        sp.run(e)

    @block.tensor
    def _(e):
        pe.run(e)

    @block.vector
    def _(e):
        dve.run(e)

    @block.scalar
    def _(e):
        act.run(e)

    @block.gpsimd
    def _(e):
        pool.run(e)

    ctx.close()


def lay_out(I):
    def slots(w):
        r, c = w.shape
        return np.ascontiguousarray(w.reshape(4, P, c // 512, 512).transpose(2, 1, 0, 3)).reshape(-1, P, SLOT)

    def row_slots(w):
        return np.ascontiguousarray(w.reshape(-1, 4, P, 512).transpose(0, 2, 1, 3)).reshape(-1, P, SLOT)

    def padded(w, columns):
        return np.concatenate([w, np.zeros((w.shape[0], columns - w.shape[1]), w.dtype)], 1)

    def column(v):
        return v.reshape(-1, P).T

    def rope_half(w, half):
        return w.reshape(w.shape[:-1] + (HEADS, 32, 2))[..., half].reshape(w.shape[:-1] + (512,))

    A = {}
    A["x"] = I["x"].reshape(NT, P, DIM).transpose(1, 0, 2)
    A["ctxT"] = I["ctx_1024"].reshape(NSEQ, CTX, KT, P).transpose(0, 3, 2, 1).reshape(NSEQ, P, KT, CTX)
    A["mask"] = I["mask_BxS2_ik0"]
    for n in ("L0_xattn_w_q", "L0_xattn_w_kv", "L0_ffn_sh_w1", "L0_ffn_sh_w2"):
        A[n] = slots(I[n])
    A["L0_xattn_w_out"] = row_slots(I["L0_xattn_w_out"])
    for n in ("Wq", "Wk", "Wv", "Wo"):
        A["L0_attn_" + n] = slots(I["L0_attn_" + n].T)
        A["L1_xattn_" + n] = slots(I["L1_xattn_" + n].T)
        A["L1_attn_" + n] = slots(I["L1_attn_" + n])
    A["L1_attn_Wdown"] = slots(I["L1_attn_Wdown"])
    A["L1_attn_Wifg"] = slots(padded(np.concatenate([I["L1_attn_Wig"], I["L1_attn_Wfg"]], 1), 512))
    for h in range(2):
        A[f"L0_ffn_q{h + 1}"] = slots(rope_half(I["L0_ffn_q_w"], h))
        A[f"L0_ffn_k{h + 1}"] = slots(rope_half(I["L0_ffn_k_w"], h))
    A["L0_ffn_v"] = slots(I["L0_ffn_v_w"])
    A["L0_ffn_o"] = row_slots(I["L0_ffn_o_w"])
    A["router_w"] = slots(padded(I["L0_ffn_router_w"], 512))
    A["gate_w"] = slots(padded(I["L1_ffn_gate_w"], 512))
    for n in ("L0_ffn_re_w1", "L0_ffn_re_w2"):
        A[n] = row_slots(I[n].reshape(-1, 512))
    for n in ("w1", "w3"):
        w = I["L1_ffn_" + n].reshape(E1, KT, P, INTER1)
        A["L1_" + n] = w.transpose(0, 2, 1, 3).reshape(E1, P, KT * INTER1)
        A["L1_ffn_s" + n] = slots(padded(I["L1_ffn_s" + n], 1536))
    full = (HT1 - 1) * P
    w = I["L1_ffn_w2"]
    A["L1_w2_full"] = w[:, 0:full].reshape(E1, HT1 - 1, P, DIM).transpose(0, 2, 1, 3).reshape(E1, P, -1)
    A["L1_w2_last"] = w[:, full:]
    sw2 = I["L1_ffn_sw2"]
    A["L1_ffn_sw2"] = row_slots(np.concatenate([sw2, np.zeros((1536 - SHARED1, 512), sw2.dtype)], 0))
    A["L0_ffn_re_b2"], A["L1_ffn_b2"] = I["L0_ffn_re_b2"], I["L1_ffn_b2"]
    col_values = {
        "ln_gamma": column(I["L0_xattn_ln_gamma"]), "ln_beta": column(I["L0_xattn_ln_beta"]),
        "q_b1": column(rope_half(I["L0_ffn_q_b"], 0)), "q_b2": column(rope_half(I["L0_ffn_q_b"], 1)),
        "k_b1": column(rope_half(I["L0_ffn_k_b"], 0)), "k_b2": column(rope_half(I["L0_ffn_k_b"], 1)),
        "v_b": column(I["L0_ffn_v_b"]), "theta": np.tile(I["L0_ffn_theta"], 4)[:, None],
        "sh_b1": column(I["L0_ffn_sh_b1"]), "re_b1": column(I["L0_ffn_re_b1"].reshape(-1)),
        "bq": column(I["L1_xattn_bq"]), "bk": column(I["L1_xattn_bk"]), "bv": column(I["L1_xattn_bv"]),
        "b1": column(padded(I["L1_ffn_b1"], HT1 * P).reshape(-1)),
        "b3": column(padded(I["L1_ffn_b3"], HT1 * P).reshape(-1)),
        "sb1": column(I["L1_ffn_sb1"]), "sb3": column(I["L1_ffn_sb3"])}
    A["cols"] = np.concatenate([col_values[n] for n in COLS], 1)
    row_values = {
        "b_out": I["L0_xattn_b_out"], "gate": I["L0_xattn_gate"], "W_gamma": I["L0_attn_W_gamma"],
        "b_gamma": I["L0_attn_b_gamma"], "W_lambda": I["L0_attn_W_lambda"], "b_lambda": I["L0_attn_b_lambda"],
        "gamma1": I["L0_ffn_gamma1"], "gamma2": I["L0_ffn_gamma2"], "o_b": I["L0_ffn_o_b"],
        "sh_b2": I["L0_ffn_sh_b2"], "router_b": I["L0_ffn_router_b"], "bo": I["L1_xattn_bo"],
        "norm_w": I["L1_attn_norm_w"].reshape(-1),
        "b_ifg": np.concatenate([I["L1_attn_big"], I["L1_attn_bfg"]]), "sb2": I["L1_ffn_sb2"],
        "gate_b": I["L1_ffn_gate_b"]}
    A["rows"] = np.concatenate([row_values[n] for n in ROWS])[None, :]
    return {n: np.ascontiguousarray(a) for n, a in A.items()}


def kernel(**inputs):
    import concourse.bacc as bacc
    from concourse.bass_utils import run_bass_kernel_spmd

    arrays = lay_out({n: np.asarray(a) for n, a in inputs.items()})
    nc = bacc.Bacc("TRN2", target_bir_lowering=False, num_devices=1)
    A = {n: nc.dram_tensor("in_" + n, a.shape, mybir.dt.from_np(a.dtype), kind="ExternalInput").ap()
         for n, a in arrays.items()}
    out = nc.dram_tensor("out_x", (P, NT, DIM), F32, kind="ExternalOutput").ap()
    build_program(nc, A, out)
    r = run_bass_kernel_spmd(nc, [{"in_" + n: a for n, a in arrays.items()}], core_ids=[0])
    got = r.results[0]["out_x"]
    return np.ascontiguousarray(got.transpose(1, 0, 2)).reshape(NSEQ, SEQ, DIM)
```
